# Optimizing a Trainium2 kernel written in Bass

```python
import numpy as np
import jax
import jax.numpy as jnp

def _softmax(x, axis=-1):
    return jax.nn.softmax(x, axis=axis)

def _gelu(x):
    return jax.nn.gelu(x, approximate=True)

def _silu(x):
    return jax.nn.silu(x)

def _sigmoid(x):
    return jax.nn.sigmoid(x)

def _layernorm(x, axis=-1, eps=1e-05):
    m = jnp.mean(x, axis=axis, keepdims=True)
    v = jnp.var(x, axis=axis, keepdims=True)
    return (x - m) / jnp.sqrt(v + eps)

def _scatter_add(tgt, idx, src, axis=0):
    return tgt.at[idx].add(src)

def _segment_sum(src, seg, n):
    return jax.ops.segment_sum(src, seg, n)
kernel_name = 'mk_vit_tower_d2_tok_img1024_r4_69effc'

def setup_inputs(seed: int=0):
    np.random.seed(seed)
    _w = jnp.asarray

    def _rec_inputs():
        import jax
        import jax.numpy as jnp
        _rk = jax.random.key(seed)
        x = -0.00016672 + 0.999947 * jax.random.normal(jax.random.fold_in(_rk, 1), (64, 3, 96, 96), jnp.float32)
        return x
    x = _rec_inputs()

    def _L0_tok_setup():
        import jax, jax.numpy as jnp
        import numpy as np
        B, C, H, W = (64, 3, 96, 96)
        P = 16
        HP, WP = (H // P, W // P)
        N = HP * WP
        F = C * P * P
        D = 256
        key = jax.random.key(seed)
        k1, k2, k3, k4, k5 = jax.random.split(key, 5)
        data = jax.random.normal(k1, (B, C, H, W), dtype=jnp.float32)
        lim = 1.0 / np.sqrt(F)
        W_lin = jax.random.uniform(k2, (D, F), minval=-lim, maxval=lim, dtype=jnp.float32)
        b_lin = jax.random.uniform(k3, (D,), minval=-lim, maxval=lim, dtype=jnp.float32)
        class_token = jax.random.normal(k4, (1, 1, D), dtype=jnp.float32)
        position_embeddings = jax.random.normal(k5, (1, N + 1, D), dtype=jnp.float32)
        return {'data': data, 'W_lin': W_lin, 'b_lin': b_lin, 'class_token': class_token, 'position_embeddings': position_embeddings}
    _L0_tok_all = _L0_tok_setup()
    _L0_tok_in = {k: v for k, v in _L0_tok_all.items() if k in ('W_lin', 'b_lin', 'class_token', 'position_embeddings')}
    del _L0_tok_all

    def _L0_attn_setup():
        import jax, jax.numpy as jnp
        import numpy as np
        EMBED_DIM = 256
        NUM_HEADS = 16
        HEAD_DIM = EMBED_DIM // NUM_HEADS
        B, T = (2, 512)
        key = jax.random.key(seed)
        ks = jax.random.split(key, 7)
        s = 0.02
        return {'x': jax.random.normal(ks[0], (B, T, EMBED_DIM), dtype=jnp.float32), 'Wq': jax.random.normal(ks[1], (EMBED_DIM, EMBED_DIM), dtype=jnp.float32) * s, 'bq': jax.random.normal(ks[2], (EMBED_DIM,), dtype=jnp.float32) * s, 'Wkv': jax.random.normal(ks[3], (2 * HEAD_DIM, EMBED_DIM), dtype=jnp.float32) * s, 'bkv': jax.random.normal(ks[4], (2 * HEAD_DIM,), dtype=jnp.float32) * s, 'Wo': jax.random.normal(ks[5], (EMBED_DIM, EMBED_DIM), dtype=jnp.float32) * s, 'bo': jax.random.normal(ks[6], (EMBED_DIM,), dtype=jnp.float32) * s}
    _L0_attn_all = _L0_attn_setup()
    _L0_attn_in = {k: v for k, v in _L0_attn_all.items() if k in ('Wq', 'bq', 'Wkv', 'bkv', 'Wo', 'bo')}
    del _L0_attn_all

    def _L0_ffn_setup():
        import jax, jax.numpy as jnp
        import numpy as np
        LN_EPS = 1e-05

        def entmax15(z):
            z = z / 2.0
            z = z - jnp.max(z, axis=-1, keepdims=True)
            zs = -jnp.sort(-z, axis=-1)
            k = jnp.arange(1, z.shape[-1] + 1, dtype=z.dtype)
            mean = jnp.cumsum(zs, axis=-1) / k
            meansq = jnp.cumsum(zs * zs, axis=-1) / k
            ss = k * (meansq - jnp.square(mean))
            delta = (1.0 - ss) / k
            tau = mean - jnp.sqrt(jnp.clip(delta, 0.0))
            support = jnp.sum((tau <= zs).astype(jnp.int32), axis=-1, keepdims=True)
            tau_star = jnp.take_along_axis(tau, support - 1, axis=-1)
            return jnp.square(jnp.clip(z - tau_star, 0.0))

        def layernorm_noaffine(v):
            m = jnp.mean(v, axis=-1, keepdims=True)
            var = jnp.mean(jnp.square(v - m), axis=-1, keepdims=True)
            return (v - m) / jnp.sqrt(var + LN_EPS)

        def cp_mumoe(x, gate, Win, Wout):
            ones = jnp.ones(x.shape[:-1] + (1,), x.dtype)
            xb = jnp.concatenate([x, ones], axis=-1)
            z = jnp.einsum('btd,dr->btr', xb, Win) * gate
            return jnp.einsum('btr,or->bto', z, Wout)
        key = jax.random.key(seed)
        ks = jax.random.split(key, 8)
        B, T, D, O, D2, E, R = (8, 512, 256, 1024, 256, 16, 128)
        s = lambda k, shape, scale: jax.random.normal(k, shape, jnp.float32) * scale
        return {'x': s(ks[0], (B, T, D), 1.0), 'proj': s(ks[1], (D, E), D ** (-0.5)), 'C1': s(ks[2], (E, R), E ** (-0.5)), 'Win1': s(ks[3], (D + 1, R), D ** (-0.5)), 'Wout1': s(ks[4], (O, R), R ** (-0.5)), 'C2': s(ks[5], (E, R), E ** (-0.5)), 'Win2': s(ks[6], (O + 1, R), O ** (-0.5)), 'Wout2': s(ks[7], (D2, R), R ** (-0.5))}
    _L0_ffn_all = _L0_ffn_setup()
    _L0_ffn_in = {k: v for k, v in _L0_ffn_all.items() if k in ('proj', 'C1', 'Win1', 'Wout1', 'C2', 'Win2', 'Wout2')}
    del _L0_ffn_all

    def _L1_attn_setup():
        import jax, jax.numpy as jnp
        import numpy as np
        from jax.scipy.linalg import solve_triangular
        B, T, D = (2, 2048, 256)
        HEAD_DIM = 128
        H = D // HEAD_DIM
        C = 64
        key = jax.random.key(seed)
        k0, k1, k2, k3 = jax.random.split(key, 4)
        scale = 0.02
        return {'out': jax.random.normal(k0, (B, T, D), jnp.float32), 'W_write': jax.random.normal(k1, (D, D), jnp.float32) * scale, 'W_read': jax.random.normal(k2, (D, D), jnp.float32) * scale, 'W_beta': jax.random.normal(k3, (H, D), jnp.float32) * scale, 'decay': jnp.full((H,), 4.6, jnp.float32)}
    _L1_attn_all = _L1_attn_setup()
    _L1_attn_in = {k: v for k, v in _L1_attn_all.items() if k in ('W_write', 'W_read', 'W_beta', 'decay')}
    del _L1_attn_all

    def _L1_ffn_setup():
        import jax, jax.numpy as jnp
        import numpy as np
        B, S, D, F, E = (4, 512, 256, 1024, 8)
        key = jax.random.key(seed)
        ks = jax.random.split(key, 7)
        s1 = 1.0 / np.sqrt(D)
        s2 = 1.0 / np.sqrt(F)
        x = jax.random.normal(ks[0], (B, S, D), dtype=jnp.float32)
        W1 = jax.random.uniform(ks[1], (E, D, F), jnp.float32, -s1, s1)
        b1 = jax.random.uniform(ks[2], (E, F), jnp.float32, -s1, s1)
        W2 = jax.random.uniform(ks[3], (E, F, D), jnp.float32, -s2, s2)
        b2 = jax.random.uniform(ks[4], (E, D), jnp.float32, -s2, s2)
        Wr = jax.random.uniform(ks[5], (D, E), jnp.float32, -s1, s1)
        br = jax.random.uniform(ks[6], (E,), jnp.float32, -s1, s1)
        return {'x': x, 'W1': W1, 'b1': b1, 'W2': W2, 'b2': b2, 'Wr': Wr, 'br': br}
    _L1_ffn_all = _L1_ffn_setup()
    _L1_ffn_in = {k: v for k, v in _L1_ffn_all.items() if k in ('W1', 'b1', 'W2', 'b2', 'Wr', 'br')}
    del _L1_ffn_all
    return {'x': x, 'L0_tok_W_lin': _L0_tok_in['W_lin'], 'L0_tok_b_lin': _L0_tok_in['b_lin'], 'L0_tok_class_token': _L0_tok_in['class_token'], 'L0_tok_position_embeddings': _L0_tok_in['position_embeddings'], 'L0_attn_Wq': _L0_attn_in['Wq'], 'L0_attn_bq': _L0_attn_in['bq'], 'L0_attn_Wkv': _L0_attn_in['Wkv'], 'L0_attn_bkv': _L0_attn_in['bkv'], 'L0_attn_Wo': _L0_attn_in['Wo'], 'L0_attn_bo': _L0_attn_in['bo'], 'L0_ffn_proj': _L0_ffn_in['proj'], 'L0_ffn_C1': _L0_ffn_in['C1'], 'L0_ffn_Win1': _L0_ffn_in['Win1'], 'L0_ffn_Wout1': _L0_ffn_in['Wout1'], 'L0_ffn_C2': _L0_ffn_in['C2'], 'L0_ffn_Win2': _L0_ffn_in['Win2'], 'L0_ffn_Wout2': _L0_ffn_in['Wout2'], 'L1_attn_W_write': _L1_attn_in['W_write'], 'L1_attn_W_read': _L1_attn_in['W_read'], 'L1_attn_W_beta': _L1_attn_in['W_beta'], 'L1_attn_decay': _L1_attn_in['decay'], 'L1_ffn_W1': _L1_ffn_in['W1'], 'L1_ffn_b1': _L1_ffn_in['b1'], 'L1_ffn_W2': _L1_ffn_in['W2'], 'L1_ffn_b2': _L1_ffn_in['b2'], 'L1_ffn_Wr': _L1_ffn_in['Wr'], 'L1_ffn_br': _L1_ffn_in['br']}

def reference(x, L0_tok_W_lin, L0_tok_b_lin, L0_tok_class_token, L0_tok_position_embeddings, L0_attn_Wq, L0_attn_bq, L0_attn_Wkv, L0_attn_bkv, L0_attn_Wo, L0_attn_bo, L0_ffn_proj, L0_ffn_C1, L0_ffn_Win1, L0_ffn_Wout1, L0_ffn_C2, L0_ffn_Win2, L0_ffn_Wout2, L1_attn_W_write, L1_attn_W_read, L1_attn_W_beta, L1_attn_decay, L1_ffn_W1, L1_ffn_b1, L1_ffn_W2, L1_ffn_b2, L1_ffn_Wr, L1_ffn_br):
    import jax
    import jax.numpy as jnp

    def _L0_tok_ref(data, W_lin, b_lin, class_token, position_embeddings):
        import jax, jax.numpy as jnp
        import numpy as np
        B, C, H, W = (64, 3, 96, 96)
        P = 16
        HP, WP = (H // P, W // P)
        N = HP * WP
        F = C * P * P
        D = 256
        b = data.shape[0]
        x = data.reshape(b, C, HP, P, WP, P)
        x = x.transpose(0, 2, 4, 1, 3, 5).reshape(b, N, F)
        x = jnp.einsum('bnf,df->bnd', x, W_lin) + b_lin
        cls = jnp.broadcast_to(class_token, (b, 1, D))
        out = jnp.concatenate([cls, x], axis=1) + position_embeddings
        return out

    def _L0_attn_ref(x, Wq, bq, Wkv, bkv, Wo, bo):
        import jax, jax.numpy as jnp
        import numpy as np
        EMBED_DIM = 256
        NUM_HEADS = 16
        HEAD_DIM = EMBED_DIM // NUM_HEADS
        B, T = (2, 512)
        bsz, tgt_len, _ = x.shape
        scaling = HEAD_DIM ** (-0.5)
        q = (jnp.einsum('bte,oe->bto', x, Wq) + bq) * scaling
        kv = jnp.einsum('bte,oe->bto', x, Wkv) + bkv
        k, v = (kv[..., :HEAD_DIM], kv[..., HEAD_DIM:])
        qr = q.reshape(bsz, NUM_HEADS * tgt_len, HEAD_DIM)
        attn_weights = jnp.einsum('brd,bsd->brs', qr, k)
        attn_probs = jax.nn.softmax(attn_weights, axis=-1)
        attn_output = jnp.einsum('brs,bsd->brd', attn_probs, v)
        attn_output = attn_output.reshape(bsz, NUM_HEADS, tgt_len, HEAD_DIM)
        attn_output = attn_output.transpose(0, 2, 1, 3).reshape(bsz, tgt_len, EMBED_DIM)
        out = jnp.einsum('bte,oe->bto', attn_output, Wo) + bo
        return out

    def _L0_ffn_ref(x, proj, C1, Win1, Wout1, C2, Win2, Wout2):
        import jax, jax.numpy as jnp
        import numpy as np
        LN_EPS = 1e-05

        def entmax15(z):
            z = z / 2.0
            z = z - jnp.max(z, axis=-1, keepdims=True)
            zs = -jnp.sort(-z, axis=-1)
            k = jnp.arange(1, z.shape[-1] + 1, dtype=z.dtype)
            mean = jnp.cumsum(zs, axis=-1) / k
            meansq = jnp.cumsum(zs * zs, axis=-1) / k
            ss = k * (meansq - jnp.square(mean))
            delta = (1.0 - ss) / k
            tau = mean - jnp.sqrt(jnp.clip(delta, 0.0))
            support = jnp.sum((tau <= zs).astype(jnp.int32), axis=-1, keepdims=True)
            tau_star = jnp.take_along_axis(tau, support - 1, axis=-1)
            return jnp.square(jnp.clip(z - tau_star, 0.0))

        def layernorm_noaffine(v):
            m = jnp.mean(v, axis=-1, keepdims=True)
            var = jnp.mean(jnp.square(v - m), axis=-1, keepdims=True)
            return (v - m) / jnp.sqrt(var + LN_EPS)

        def cp_mumoe(x, gate, Win, Wout):
            ones = jnp.ones(x.shape[:-1] + (1,), x.dtype)
            xb = jnp.concatenate([x, ones], axis=-1)
            z = jnp.einsum('btd,dr->btr', xb, Win) * gate
            return jnp.einsum('btr,or->bto', z, Wout)
        a = entmax15(layernorm_noaffine(jnp.einsum('btd,de->bte', x, proj)))
        g1 = jnp.einsum('bte,er->btr', a, C1)
        h = cp_mumoe(x, g1, Win1, Wout1)
        h = jax.nn.gelu(h, approximate=False)
        g2 = jnp.einsum('bte,er->btr', a, C2)
        return cp_mumoe(h, g2, Win2, Wout2)

    def _L1_attn_ref(out, W_write, W_read, W_beta, decay):
        import jax, jax.numpy as jnp
        import numpy as np
        from jax.scipy.linalg import solve_triangular
        B, T, D = (2, 2048, 256)
        HEAD_DIM = 128
        H = D // HEAD_DIM
        C = 64
        Bs, Ts, Ds = out.shape
        d = HEAD_DIM
        Hn = Ds // d
        x = out.astype(jnp.float32)
        k = x.reshape(Bs, Ts, Hn, d)
        k = k / jnp.maximum(jnp.linalg.norm(k, axis=-1, keepdims=True), 1e-12)
        k = k.transpose(0, 2, 1, 3)
        v = (x @ W_write.T).reshape(Bs, Ts, Hn, d).transpose(0, 2, 1, 3)
        beta = jax.nn.sigmoid(x @ W_beta.T).transpose(0, 2, 1)[..., None]
        v = v * beta
        k_beta = k * beta
        pad = -Ts % C
        if pad:
            pw = ((0, 0), (0, 0), (0, pad), (0, 0))
            k, v, k_beta = (jnp.pad(a, pw) for a in (k, v, k_beta))
        Tp = k.shape[2]
        N = Tp // C
        log_gamma = jnp.log(jax.nn.sigmoid(decay))
        pos = jnp.arange(C, dtype=jnp.float32)
        cum_decay = (pos + 1.0)[None, :] * log_gamma[:, None]
        Ldiff = cum_decay[:, :, None] - cum_decay[:, None, :]
        L = jnp.tril(jnp.exp(jnp.tril(Ldiff)))
        decay_exp = jnp.exp(cum_decay)[None, :, None, :, None]
        chunk_total_decay = jnp.exp(cum_decay[:, -1])[None, :, None, None]
        dw = jnp.exp(cum_decay[:, -1:] - cum_decay)[None, :, :, None]
        de = jnp.exp(cum_decay)[None, :, :, None]
        k = k.reshape(Bs, Hn, N, C, d)
        v = v.reshape(Bs, Hn, N, C, d)
        k_beta = k_beta.reshape(Bs, Hn, N, C, d)
        A0 = jnp.tril(-(jnp.einsum('bhnid,bhnjd->bhnij', k_beta, k) * L[None, :, None]), -1)
        eye = jnp.eye(C, dtype=jnp.float32)
        M = eye - A0
        A = solve_triangular(M, jnp.broadcast_to(eye, M.shape), lower=True, unit_diagonal=True)
        v = A @ v
        k_cumdecay = A @ (k_beta * decay_exp)
        kc = k.transpose(2, 0, 1, 3, 4)
        vc = v.transpose(2, 0, 1, 3, 4)
        kcd = k_cumdecay.transpose(2, 0, 1, 3, 4)

        def step(S, inp):
            k_i, v_i, kcd_i = inp
            attn = jnp.tril(jnp.einsum('bhid,bhjd->bhij', k_i, k_i) * L[None])
            v_new = v_i - kcd_i @ S
            o_i = k_i * de @ S + attn @ v_new
            S_new = chunk_total_decay * S + jnp.einsum('bhcd,bhce->bhde', k_i * dw, v_new)
            return (S_new, o_i)
        S0 = jnp.zeros((Bs, Hn, d, d), jnp.float32)
        _, o = jax.lax.scan(step, S0, (kc, vc, kcd))
        o = o.transpose(1, 2, 0, 3, 4).reshape(Bs, Hn, Tp, d)
        o = o.transpose(0, 2, 1, 3).reshape(Bs, Tp, Ds)[:, :Ts]
        return out + (o @ W_read.T).astype(out.dtype)

    def _L1_ffn_ref(x, W1, b1, W2, b2, Wr, br):
        import jax, jax.numpy as jnp
        import numpy as np
        B, S, D, F, E = (4, 512, 256, 1024, 8)
        b, s, d = x.shape
        e = Wr.shape[1]
        logits = x @ Wr + br
        idx = jnp.argmax(logits, axis=-1)
        probs = jax.nn.softmax(logits, axis=-1)
        gates = jnp.take_along_axis(probs, idx[..., None], axis=-1)[..., 0]
        xf = x.reshape(-1, d)
        idxf = idx.reshape(-1)
        gf = gates.reshape(-1)
        out = jnp.zeros_like(xf)
        for ei in range(e):
            h = jax.nn.gelu(xf @ W1[ei] + b1[ei], approximate=False)
            y = h @ W2[ei] + b2[ei]
            mask = (idxf == ei).astype(xf.dtype)
            out = out + y * (gf * mask)[:, None]
        return out.reshape(b, s, d)
    h = _L0_tok_ref(x, L0_tok_W_lin, L0_tok_b_lin, L0_tok_class_token, L0_tok_position_embeddings)
    h = h + _L0_attn_ref(_layernorm(h, axis=-1), L0_attn_Wq, L0_attn_bq, L0_attn_Wkv, L0_attn_bkv, L0_attn_Wo, L0_attn_bo)
    h = h + _L0_ffn_ref(_layernorm(h, axis=-1), L0_ffn_proj, L0_ffn_C1, L0_ffn_Win1, L0_ffn_Wout1, L0_ffn_C2, L0_ffn_Win2, L0_ffn_Wout2)
    h = h + _L1_attn_ref(_layernorm(h, axis=-1), L1_attn_W_write, L1_attn_W_read, L1_attn_W_beta, L1_attn_decay)
    h = h + _L1_ffn_ref(_layernorm(h, axis=-1), L1_ffn_W1, L1_ffn_b1, L1_ffn_W2, L1_ffn_b2, L1_ffn_Wr, L1_ffn_br)
    return h

_drawn_inputs = setup_inputs


def setup_inputs(seed=0):
    import zlib

    import numpy as np

    out = dict(_drawn_inputs(seed))
    spreads = {'L1_attn_decay': (4.599999904632568, 0.6)}
    factors = {'L0_tok_b_lin': 2.992,
     'L0_attn_Wq': 8.0,
     'L0_attn_bq': 8.0,
     'L0_attn_Wkv': 4.265,
     'L0_attn_bkv': 8.0,
     'L0_attn_Wo': 3.848,
     'L0_attn_bo': 3.138,
     'L0_ffn_proj': 4.149,
     'L0_ffn_C1': 4.413,
     'L0_ffn_Win1': 4.394,
     'L0_ffn_Wout1': 4.326,
     'L0_ffn_C2': 4.119,
     'L0_ffn_Win2': 4.145,
     'L0_ffn_Wout2': 4.164,
     'L1_attn_W_beta': 64.0,
     'L1_ffn_b1': 64.0,
     'L1_ffn_b2': 200.0,
     'L1_ffn_br': 64.0,
     'L1_attn_W_write': 8.0,
     'L1_attn_W_read': 8.0,
     'L1_ffn_W1': 8.0,
     'L1_ffn_W2': 8.0,
     'L1_ffn_Wr': 8.0}
    for name, (base, spread) in spreads.items():
        noise = np.random.default_rng([zlib.crc32(name.encode()), seed]).standard_normal(out[name].shape)
        drawn = base * np.exp(spread * noise) if base else spread * noise
        out[name] = jnp.asarray(drawn.astype(out[name].dtype))
    for name, factor in factors.items():
        out[name] = (out[name] * factor).astype(out[name].dtype)
    return out
```

```python
from contextlib import ExitStack, contextmanager

import concourse.bass as bass
from concourse import mybir

ALU = mybir.AluOpType
ACT = mybir.ActivationFunctionType
F32 = mybir.dt.float32
I32 = mybir.dt.int32
AX_X = mybir.AxisListType.X

B, TOK, D = 64, 37, 256
IPT = 3
R = IPT * TOK
NT = -(-B // IPT)
PAIRS = NT // 2
FP = 768
PC = FP // 128
NH, HD = 16, 16
HH = NH // 2
E0, RK, O0 = 16, 128, 1024
OC = O0 // 128
H1 = 2
NE, FF = 8, 1024
FC = FF // 128
ST = (B * TOK + NE * 127) // 128
EPS = 1e-5
KW = HH * TOK
SPAN = R + TOK
VW = 96 + 128
CHUNKS = [(0, 3), (3, 3), (6, 2)]
MT = 19

PACK1 = [("w_lin", PC * D), ("pos", D), ("pos_add", D), ("w_q", 2 * D), ("b_q", D), ("w_k", 2 * 128),
         ("b_k", 1), ("w_v", 2 * HD), ("b_v", HD)]
PACK2 = [("w_o", 2 * D), ("b_o", D), ("proj", 2 * E0), ("w_in1", 2 * RK), ("b_in1", 1), ("c1", RK), ("c2", RK),
         ("w_out1", O0), ("w_in2", OC * RK), ("b_in2", 1), ("w_out2", D), ("w_vb", 2 * (D + H1)),
         ("mask_head", HH), ("lag_t", R), ("keep_t", R), ("lag", R), ("keep", R), ("decay", H1),
         ("inv_k", NT * E0), ("rank_k", NT * E0), ("seg_e0", NT * E0)]
PACKC = [("ident", 128), ("mask_img", IPT), ("w_read", 2 * D), ("w_r", 2 * NE), ("b_r", NE), ("before", R),
         ("ones", R), ("valid", NT), ("b1", NE * FC), ("b2", NE * D), ("seg_e", NT * NE), ("seg_t", NE * NT),
         ("starts", MT), ("tile_no", ST)]


def offsets(pack):
    at, out = 0, {}
    for name, width in pack:
        out[name] = (at, width)
        at += width
    return out, at


def build(nc, x_h, pack1_h, pack2_h, packc_h, w1_h, w2_h, out_h):
    at1, n1w = offsets(PACK1)
    at2, n2w = offsets(PACK2)
    atc, ncw = offsets(PACKC)

    q_rows = nc.dram_tensor("q_rows", (NT * R, D), F32).ap()
    q_mixed = nc.dram_tensor("q_mixed", (NT * R, D), F32).ap()
    n_rows = nc.dram_tensor("n_rows", (NT * R, H1 * TOK), F32).ap()
    a_rows = nc.dram_tensor("a_rows", (NT * R, H1 * TOK), F32).ap()
    x_slots = nc.dram_tensor("x_slots", (ST * 128, D), F32).ap()
    y_slots = nc.dram_tensor("y_slots", (ST * 128, D), F32).ap()

    with ExitStack() as top:
        def sb(name, width, dt=F32, rows=128):
            return top.enter_context(nc.sbuf_tensor(name, [rows, width], dt))

        def sem(name):
            return top.enter_context(nc.semaphore(name))

        W1S = NE * 2 * FF
        W2S = NE * FC * D
        arena_w1 = sb("arena_w1", W1S)
        arena_w2 = sb("arena_w2", W2S)
        resid = sb("resid", NT * D)
        keepx = sb("keepx", NT * D)
        cst = sb("cst", ncw)
        work = sb("work", 5632)
        slot_i = sb("slot_i", NT, I32)
        expert_i = sb("expert_i", ST, I32, rows=1)
        gate = sb("gate", NT)
        bank = [top.enter_context(nc.psum_tensor(f"bank{k}", [128, 512], F32)) for k in range(8)]

        def carver(arena, start=0):
            pos = [start]

            def carve(width, rows=128):
                a = pos[0]
                pos[0] += width
                assert pos[0] <= arena.shape[1], (pos[0], arena.shape)
                return arena[0:rows, a:a + width]
            return carve

        def c(name, rows=128):
            a, w = atc[name]
            return cst[0:rows, a:a + w]

        ident = c("ident")
        carve_a = carver(arena_w1)
        pack1 = carve_a(n1w)
        pack2 = carve_a(n2w)

        def p1(name, rows=128):
            a, w = at1[name]
            return pack1[0:rows, a:a + w]

        def p2(name, rows=128):
            a, w = at2[name]
            return pack2[0:rows, a:a + w]

        carve_0 = carver(arena_w2)
        x_t = carve_0(2 * NT * R)
        k_rep = carve_0(NT * R)
        carve_1 = carver(arena_w2, W2S // 2)
        attn_t = carve_1(NT * H1 * R, R)
        sys_n = carve_1(TOK * TOK)
        sys_x = carve_1(TOK * TOK)
        carve_1b = carver(arena_w2, W2S // 2)
        v_rep = carve_1b(NT * IPT * HD, R)
        gate_t = carve_1b(NT * R, E0)
        lg0 = carve_1b(NT * E0, R)

        in_params = sem("in_params")
        in_params2 = sem("in_params2")
        in_cst = sem("in_cst")
        zeros_out = sem("zeros_out")
        w2a_in = sem("w2a_in")
        w2b_in = sem("w2b_in")
        w1_in = sem("w1_in")

        phase_sems = []

        def psem(name):
            phase_sems.append(nc.alloc_semaphore(name=f"p{len(blocks)}_{name}"))
            return phase_sems[-1]

        def pair(name):
            return [psem(f"{name}{j}") for j in range(2)]

        @contextmanager
        def phase():
            with ExitStack() as inner:
                blocks.append(inner)
                yield
            nc.clear_and_free_semaphores(phase_sems)
            nc.all_engine_barrier()
            phase_sems.clear()

        blocks = []

        def enter(block):
            return blocks[-1].enter_context(block)

        def stand_alone(eng):
            eng.wait_ge(in_cst, 16)

        ph2_carve = carver(arena_w1, n1w + n2w)
        posb = ph2_carve(D, R)
        qm = [ph2_carve(2 * IPT * SPAN) for _ in range(2)]
        kb = [ph2_carve(IPT * KW) for _ in range(2)]
        vb2 = [ph2_carve(IPT * VW, R) for _ in range(2)]
        xp = [x[:, 0:IPT * PC * TOK] for x in kb]
        ph1 = carver(arena_w1, n1w + n2w + D + 4 * IPT * (SPAN + 0) + 2 * IPT * KW + 2 * IPT * VW)
        xt3 = [ph1(2 * IPT * R) for _ in range(2)]
        wc = carver(work)
        xn = [wc(D, R) for _ in range(2)]
        xt = [wc(2 * R) for _ in range(2)]
        st = [wc(8, R) for _ in range(2)]
        ve = [wc(4, R) for _ in range(2)]
        qn = [wc(D, R) for _ in range(2)]
        small = [wc(3 * NH, R) for _ in range(2)]
        prob = [wc(NH * TOK, R) for _ in range(2)]

        def norm_stats(dve, x, j, sems, n1, after=None):
            s_st, s_ag, s_ve = sems
            if after is not None:
                stand_alone(dve)
                dve.wait_ge(after[j], n1)
            nc.vector.bn_stats(st[j][:, 0:6], x).then_inc(s_st[j], 1)
            stand_alone(dve)
            dve.wait_ge(s_st[j], n1)
            nc.vector.bn_aggr(st[j][:, 6:8], st[j][:, 0:6]).then_inc(s_ag[j], 1)
            dve.wait_ge(s_ag[j], n1)
            nc.vector.tensor_scalar(ve[j][:, 0:1], st[j][:, 7:8], EPS, None, ALU.add).then_inc(s_ve[j], 1)

        def norm_power(pool, j, s_ve, s_rs, n1):
            pool.wait_ge(s_ve[j], n1)
            nc.gpsimd.tensor_tensor(ve[j][:, 1:2], ve[j][:, 0:1], ve[j][:, 2:3], ALU.pow).then_inc(s_rs[j], 1)

        def norm_apply(out, x, j):
            return nc.vector.tensor_scalar(out, x, st[j][:, 6:7], ve[j][:, 1:2], ALU.subtract, ALU.mult)

        with phase():
            x_in = pair("x_in")
            embedded = pair("embedded")
            summed = pair("summed")
            stats = [pair("st"), pair("ag"), pair("ve")]
            powered = pair("powered")
            normed = pair("normed")
            turned = pair("turned")
            xt_ready = pair("xt_ready")
            q_done = pair("q_done")
            kv_done = pair("kv_done")
            q_out = pair("q_out")
            k_out = pair("k_out")
            v_out = pair("v_out")
            q_stored = pair("q_stored")
            thrice = pair("thrice")
            setup = psem("setup")
            pos_ready = psem("pos_ready")
            zero_ready = psem("zero_ready")
            block = enter(nc.Block())

            @block.sync
            def _(sp):
                sp.dma_start(pack1, pack1_h).then_inc(in_params, 16)
                with sp.Fori(0, PAIRS) as i:
                    for j in range(2):
                        sp.wait_ge(embedded[j], i)
                        sp.dma_start(xp[j], x_h[bass.ds(2 * i + j, 1)].rearrange("o p n -> (o p) n")).then_inc(x_in[j], 16)

            @block.tensor
            def _(pe):
                pe.wait_ge(in_params, 16)
                pe.wait_ge(in_cst, 16)
                w_lin = p1("w_lin").rearrange("p (c n) -> p c n", c=PC)
                w_q = p1("w_q").rearrange("p (c n) -> p c n", c=2)
                w_k = p1("w_k").rearrange("p (c n) -> p c n", c=2)
                w_v = p1("w_v").rearrange("p (c n) -> p c n", c=2)
                with pe.Fori(0, PAIRS) as i:
                    n1, n16 = pe.snap(i + 1), pe.snap(16 * i + 16)
                    for j in range(2):
                        pe.wait_ge(x_in[j], n16)
                        pe.wait_ge(summed[j], i)
                        for k in range(PC):
                            mm = nc.tensor.matmul(bank[j][0:R, 0:D], xp[j][:, k * R:(k + 1) * R], w_lin[:, k, :],
                                                  start=(k == 0), stop=(k == PC - 1))
                        mm.then_inc(embedded[j], 1)
                    for j in range(2):
                        pe.wait_ge(normed[j], n1)
                        pe.wait_ge(xt_ready[j], i)
                        for k in range(2):
                            mm = nc.tensor.transpose(bank[2 + j][:, k * R:(k + 1) * R], xn[j][:, k * 128:(k + 1) * 128],
                                                     ident[0:R, 0:R])
                        mm.then_inc(turned[j], 1)
                    for j in range(2):
                        pe.wait_ge(xt_ready[j], n1)
                        pe.wait_ge(q_out[j], i)
                        for k in range(2):
                            mm = nc.tensor.matmul(bank[4 + j][0:R, 0:D], xt[j][:, k * R:(k + 1) * R], w_q[:, k, :],
                                                  start=(k == 0), stop=(k == 1))
                        mm.then_inc(q_done[j], 1)
                    for j in range(2):
                        pe.wait_ge(k_out[j], i)
                        pe.wait_ge(v_out[j], i)
                        for k in range(2):
                            nc.tensor.matmul(bank[6 + j][:, 0:R], w_k[:, k, :], xt[j][:, k * R:(k + 1) * R],
                                             start=(k == 0), stop=(k == 1))
                        pe.wait_ge(thrice[j], n1)
                        for m in range(IPT):
                            for k in range(2):
                                a = (k * IPT + m) * R
                                mm = nc.tensor.matmul(bank[6 + j][0:R, R + m * HD:R + (m + 1) * HD],
                                                      xt3[j][:, a:a + R], w_v[:, k, :],
                                                      start=(k == 0), stop=(k == 1))
                        mm.then_inc(kv_done[j], 1)

            @block.vector
            def _(dve):
                dve.wait_ge(in_params, 16)
                nc.vector.tensor_tensor(posb, p1("pos", R), p1("pos_add", R), ALU.add).then_inc(pos_ready, 1)
                for j in range(2):
                    nc.vector.memset(ve[j][:, 2:3], -0.5).then_inc(setup, 1)
                dve.wait_ge(pos_ready, 1)
                with dve.Fori(0, PAIRS) as i:
                    n1 = dve.snap(i + 1)
                    for j in range(2):
                        h = resid[0:R, bass.ds((2 * i + j) * D, D)]
                        dve.wait_ge(embedded[j], n1)
                        nc.vector.tensor_tensor(h, bank[j][0:R, 0:D], posb, ALU.add).then_inc(summed[j], 1)
                        norm_stats(dve, h, j, stats, n1, summed)
                        dve.wait_ge(powered[j], n1)
                        dve.wait_ge(turned[j], i)
                        norm_apply(xn[j], h, j).then_inc(normed[j], 1)
                    for j in range(2):
                        dve.wait_ge(q_done[j], n1)
                        dve.wait_ge(q_stored[j], 16 * i)
                        nc.vector.tensor_tensor(qn[j], bank[4 + j][0:R, 0:D], p1("b_q", R), ALU.add).then_inc(q_out[j], 1)
                    for j in range(2):
                        dve.wait_ge(kv_done[j], n1)
                        nc.vector.tensor_scalar(k_rep[:, bass.ds((2 * i + j) * R, R)], bank[6 + j][:, 0:R],
                                                p1("b_k"), None, ALU.add).then_inc(k_out[j], 1)
                        nc.vector.tensor_tensor(
                            v_rep[:, bass.ds((2 * i + j) * IPT * HD, IPT * HD)].rearrange("p (m d) -> p m d", m=IPT),
                            bank[6 + j][0:R, R:R + IPT * HD].rearrange("p (m d) -> p m d", m=IPT),
                            p1("b_v", R).unsqueeze(1).broadcast_to([R, IPT, HD]), ALU.add).then_inc(v_out[j], 1)

            @block.scalar
            def _(act):
                act.dma_start(cst[:], packc_h).then_inc(in_cst, 16)
                act.dma_start(pack2, pack2_h).then_inc(in_params2, 16)
                act.wait_ge(zero_ready, 3)
                act.dma_start(x_slots.rearrange("(s p) d -> p s d", p=128),
                              arena_w2[:, W2S - D:W2S].unsqueeze(1).broadcast_to([128, ST, D])).then_inc(zeros_out, 16)
                act.dma_start(a_rows[B * TOK:, :], arena_w2[0:NT * R - B * TOK, W2S - D:W2S - D + H1 * TOK]).then_inc(zeros_out, 16)
                with act.Fori(0, PAIRS) as i:
                    n1 = act.snap(i + 1)
                    for j in range(2):
                        act.wait_ge(turned[j], n1)
                        act.wait_ge(kv_done[j], i)
                        act.wait_ge(thrice[j], i)
                        nc.scalar.copy(xt[j], bank[2 + j][:, 0:2 * R]).then_inc(xt_ready[j], 1)

                act.wait_ge(zeros_out, 32)

            @block.gpsimd
            def _(pool):
                for j in range(2):
                    nc.gpsimd.memset(vb2[j], 0.0).then_inc(zero_ready, 1)
                nc.gpsimd.memset(arena_w2[:, W2S - D:W2S], 0.0).then_inc(zero_ready, 1)
                for j in range(2):
                    nc.gpsimd.memset(qm[j], 0.0).then_inc(zero_ready, 1)
                pool.wait_ge(setup, 2)
                with pool.Fori(0, PAIRS) as i:
                    n1 = pool.snap(i + 1)
                    for j in range(2):
                        norm_power(pool, j, stats[2], powered, n1)
                    for j in range(2):
                        stand_alone(pool)
                        pool.wait_ge(xt_ready[j], n1)
                        pool.wait_ge(kv_done[j], i)
                        nc.gpsimd.tensor_copy(xt3[j].rearrange("p (a r t) -> p a r t", a=2 * IPT, r=IPT),
                                              xt[j].rearrange("p (a t) -> p a t", a=2 * IPT).unsqueeze(2)
                                              .broadcast_to([128, 2 * IPT, IPT, TOK])).then_inc(thrice[j], 1)
                    for j in range(2):
                        pool.wait_ge(q_out[j], n1)
                        pool.dma_start(q_rows[bass.ds((2 * i + j) * R, R), :], qn[j]).then_inc(q_stored[j], 16)
                for j in range(2):
                    pool.wait_ge(q_stored[j], 16 * PAIRS)
                pool.wait_ge(zero_ready, 5)

        if PHASES < 2:
            return
        with phase():
            pt = [wc(2 * IPT * R, R) for _ in range(2)]
            q_rows_in = pair("q_rows_in")
            mixed = pair("mixed")
            q_turned = pair("q_turned")
            q_masked = pair("q_masked")
            k_block = pair("k_block")
            v_block = pair("v_block")
            with_bo = pair("with_bo")
            scored = pair("scored")
            maxed = pair("maxed")
            shifted = pair("shifted")
            exped = pair("exped")
            row_sum = pair("row_sum")
            row_inv = pair("row_inv")
            scaled = pair("scaled")
            p_turned = pair("p_turned")
            p_copied = pair("p_copied")
            mixed_v = pair("mixed_v")
            o_copied = pair("o_copied")
            projected = pair("projected")
            added = pair("added")
            stats = [pair("st"), pair("ag"), pair("ve")]
            powered = pair("powered")
            normed = pair("normed")
            turned = pair("turned")
            xt_ready = pair("xt_ready")
            x_saved = pair("x_saved")
            logits = pair("logits")
            logits_out = pair("logits_out")
            ot = [q[:, 0:2 * R] for q in (ph2_carve(2 * R), ph2_carve(2 * R))]
            hbo = [ph2_carve(D, R) for _ in range(2)]
            block = enter(nc.Block())

            def head_cols(ap, half):
                return ap[0:R, half * KW:(half + 1) * KW]

            @block.sync
            def _(sp):
                with sp.Fori(0, PAIRS) as i:
                    n48 = sp.snap(16 * IPT * i + 16 * IPT)
                    for j in range(2):
                        for m in range(IPT):
                            rows = bass.ds((2 * i + j) * R + m * TOK, TOK)
                            src = q_rows[rows, :].rearrange("t (g d) -> (t g) d", d=HD).rearrange("(h t) d -> h t d", h=NH)
                            dst = q_mixed[rows, :].rearrange("t (h d) -> h t d", d=HD)
                            sp.dma_start(dst, src).then_inc(mixed[j], 16)
                    for j in range(2):
                        sp.wait_ge(mixed[j], n48)
                        sp.wait_ge(q_turned[j], i)
                        sp.dma_start(qn[j], q_mixed[bass.ds((2 * i + j) * R, R), :]).then_inc(q_rows_in[j], 16)

            @block.tensor
            def _(pe):
                pe.wait_ge(in_params2, 16)
                w_o = p2("w_o").rearrange("p (c n) -> p c n", c=2)
                proj = p2("proj").rearrange("p (c n) -> p c n", c=2)
                with pe.Fori(0, PAIRS) as i:
                    n1, n16 = pe.snap(i + 1), pe.snap(16 * i + 16)
                    for j in range(2):
                        pe.wait_ge(q_rows_in[j], n16)
                        pe.wait_ge(o_copied[j], i)
                        for k in range(2):
                            mm = nc.tensor.transpose(bank[4 + j][:, k * R:(k + 1) * R], qn[j][:, k * 128:(k + 1) * 128],
                                                     ident[0:R, 0:R])
                        mm.then_inc(q_turned[j], 1)
                    for j in range(2):
                        pe.wait_ge(q_masked[j], n1)
                        pe.wait_ge(k_block[j], n1)
                        pe.wait_ge(p_copied[j], i)
                        for half in range(2):
                            for m in range(IPT):
                                a = half * IPT * SPAN + m * R
                                mm = nc.tensor.matmul(bank[2 * j + half][0:R, 0:KW], qm[j][:, a:a + R],
                                                      kb[j][:, m * KW:(m + 1) * KW], start=(m == 0), stop=(m == IPT - 1))
                        mm.then_inc(scored[j], 1)
                    for j in range(2):
                        pe.wait_ge(scaled[j], n1)
                        for half in range(2):
                            for k, (h0, hn) in enumerate(CHUNKS):
                                mm = nc.tensor.transpose(bank[2 * j + half][0:hn * TOK, k * R:(k + 1) * R],
                                                         head_cols(prob[j], half)[:, h0 * TOK:(h0 + hn) * TOK],
                                                         ident[0:R, 0:R])
                        mm.then_inc(p_turned[j], 1)
                        pe.wait_ge(p_copied[j], n1)
                        pe.wait_ge(v_block[j], n1)
                        for half in range(2):
                            for m in range(IPT):
                                for k, (h0, hn) in enumerate(CHUNKS):
                                    K = hn * TOK
                                    lo = m * VW + 96 - h0 * HD
                                    a = half * IPT * R + k * R + m * TOK
                                    mm = nc.tensor.matmul(bank[4 + j][:, half * R + m * TOK:half * R + (m + 1) * TOK],
                                                          vb2[j][0:K, lo:lo + 128], pt[j][0:K, a:a + TOK],
                                                          start=(k == 0), stop=(k == 2))
                        mm.then_inc(mixed_v[j], 1)
                    for j in range(2):
                        pe.wait_ge(o_copied[j], n1)
                        pe.wait_ge(added[j], i)
                        for k in range(2):
                            mm = nc.tensor.matmul(bank[4 + j][0:R, 2 * R:2 * R + D], ot[j][:, k * R:(k + 1) * R],
                                                  w_o[:, k, :], start=(k == 0), stop=(k == 1))
                        mm.then_inc(projected[j], 1)
                    for j in range(2):
                        pe.wait_ge(normed[j], n1)
                        pe.wait_ge(logits_out[j], i)
                        for k in range(2):
                            mm = nc.tensor.transpose(bank[6 + j][:, k * R:(k + 1) * R], xn[j][:, k * 128:(k + 1) * 128],
                                                     ident[0:R, 0:R])
                        mm.then_inc(turned[j], 1)
                    for j in range(2):
                        pe.wait_ge(xt_ready[j], n1)
                        for k in range(2):
                            mm = nc.tensor.matmul(bank[6 + j][0:R, 2 * R:2 * R + E0], xt[j][:, k * R:(k + 1) * R],
                                                  proj[:, k, :], start=(k == 0), stop=(k == 1))
                        mm.then_inc(logits[j], 1)

            @block.vector
            def _(dve):
                with dve.Fori(0, PAIRS) as i:
                    n1 = dve.snap(i + 1)
                    for j in range(2):
                        dve.wait_ge(scored[j], n1)
                        for half in range(2):
                            mx = nc.vector.tensor_reduce(
                                small[j][:, half * HH:(half + 1) * HH],
                                bank[2 * j + half][0:R, 0:KW].rearrange("p (h s) -> p h s", h=HH), AX_X, ALU.max)
                        mx.then_inc(maxed[j], 1)
                        dve.wait_ge(maxed[j], n1)
                        dve.wait_ge(p_turned[j], i)
                        for half in range(2):
                            sub = nc.vector.tensor_tensor(
                                head_cols(prob[j], half).rearrange("p (h s) -> p h s", h=HH),
                                bank[2 * j + half][0:R, 0:KW].rearrange("p (h s) -> p h s", h=HH),
                                small[j][:, half * HH:(half + 1) * HH].unsqueeze(2).broadcast_to([R, HH, TOK]),
                                ALU.subtract)
                        sub.then_inc(shifted[j], 1)
                    for j in range(2):
                        dve.wait_ge(exped[j], n1)
                        nc.vector.tensor_reduce(small[j][:, NH:2 * NH], prob[j].rearrange("p (h s) -> p h s", h=NH),
                                                AX_X, ALU.add).then_inc(row_sum[j], 1)
                        dve.wait_ge(row_sum[j], n1)
                        dve.wait_ge(scaled[j], i)
                        nc.vector.reciprocal(small[j][:, 2 * NH:3 * NH], small[j][:, NH:2 * NH]).then_inc(row_inv[j], 1)
                    for j in range(2):
                        h = resid[0:R, bass.ds((2 * i + j) * D, D)]
                        dve.wait_ge(projected[j], n1)
                        dve.wait_ge(with_bo[j], n1)
                        nc.vector.tensor_tensor(h, bank[4 + j][0:R, 2 * R:2 * R + D], hbo[j], ALU.add).then_inc(added[j], 1)
                        norm_stats(dve, h, j, stats, n1, added)
                        dve.wait_ge(powered[j], n1)
                        dve.wait_ge(turned[j], i)
                        norm_apply(xn[j], h, j).then_inc(normed[j], 1)
                    for j in range(2):
                        dve.wait_ge(logits[j], n1)
                        nc.vector.tensor_copy(lg0[:, bass.ds((2 * i + j) * E0, E0)],
                                              bank[6 + j][0:R, 2 * R:2 * R + E0]).then_inc(logits_out[j], 1)

            @block.scalar
            def _(act):
                with act.Fori(0, PAIRS) as i:
                    n1 = act.snap(i + 1)
                    for j in range(2):
                        act.wait_ge(q_turned[j], n1)
                        act.wait_ge(scored[j], i)
                        nc.scalar.mul(qm[j].rearrange("p (c m w) -> p c m w", c=2, m=IPT)[:, :, :, 0:TOK],
                                      bank[4 + j][:, 0:2 * R].rearrange("p (c m t) -> p c m t", c=2, m=IPT),
                                      HD ** -0.5).then_inc(q_masked[j], 1)
                    for j in range(2):
                        act.wait_ge(shifted[j], n1)
                        nc.scalar.activation(prob[j], prob[j], ACT.Exp).then_inc(exped[j], 1)
                    for j in range(2):
                        act.wait_ge(p_turned[j], n1)
                        act.wait_ge(mixed_v[j], i)
                        for half in range(2):
                            for k, rows in ((0, R), (2, 2 * TOK)):
                                w = 2 * R if k == 0 else R
                                a = half * IPT * R + k * R
                                cp = nc.scalar.copy(pt[j][0:rows, a:a + w], bank[2 * j + half][0:rows, k * R:k * R + w])
                        cp.then_inc(p_copied[j], 1)
                        act.wait_ge(mixed_v[j], n1)
                        act.wait_ge(projected[j], i)
                        nc.scalar.copy(ot[j], bank[4 + j][:, 0:2 * R]).then_inc(o_copied[j], 1)
                    for j in range(2):
                        act.wait_ge(turned[j], n1)
                        act.wait_ge(logits[j], i)
                        act.wait_ge(x_saved[j], i)
                        nc.scalar.copy(xt[j], bank[6 + j][:, 0:2 * R]).then_inc(xt_ready[j], 1)

            @block.gpsimd
            def _(pool):
                pool.wait_ge(in_params2, 16)
                with pool.Fori(0, PAIRS) as i:
                    n1 = pool.snap(i + 1)
                    for j in range(2):
                        pool.wait_ge(scored[j], i)
                        for m in range(IPT):
                            tt = nc.gpsimd.tensor_tensor(
                                kb[j][:, m * KW:(m + 1) * KW].rearrange("p (h s) -> p h s", h=HH),
                                k_rep[:, bass.ds((2 * i + j) * R + m * TOK, TOK)].unsqueeze(1).broadcast_to([128, HH, TOK]),
                                p2("mask_head").unsqueeze(2).broadcast_to([128, HH, TOK]), ALU.mult)
                        tt.then_inc(k_block[j], 1)
                        pool.wait_ge(mixed_v[j], i)
                        for m in range(IPT):
                            tt = nc.gpsimd.tensor_tensor(
                                vb2[j][:, m * VW + 96:m * VW + 144].rearrange("p (h d) -> p h d", h=IPT),
                                v_rep[:, bass.ds((2 * i + j) * IPT * HD + m * HD, HD)].unsqueeze(1).broadcast_to([R, IPT, HD]),
                                c("mask_img", R).unsqueeze(2).broadcast_to([R, IPT, HD]), ALU.mult)
                        tt.then_inc(v_block[j], 1)
                        pool.wait_ge(added[j], i)
                        nc.gpsimd.tensor_tensor(hbo[j], resid[0:R, bass.ds((2 * i + j) * D, D)], p2("b_o", R),
                                                ALU.add).then_inc(with_bo[j], 1)
                    for j in range(2):
                        pool.wait_ge(row_inv[j], n1)
                        nc.gpsimd.tensor_tensor(
                            prob[j].rearrange("p (h s) -> p h s", h=NH), prob[j].rearrange("p (h s) -> p h s", h=NH),
                            small[j][:, 2 * NH:3 * NH].unsqueeze(2).broadcast_to([R, NH, TOK]), ALU.mult).then_inc(scaled[j], 1)
                    for j in range(2):
                        norm_power(pool, j, stats[2], powered, n1)
                    for j in range(2):
                        stand_alone(pool)
                        pool.wait_ge(xt_ready[j], n1)
                        for k in range(2):
                            cp = nc.gpsimd.tensor_copy(x_t[:, bass.ds(k * NT * R + (2 * i + j) * R, R)],
                                                       xt[j][:, k * R:(k + 1) * R])
                        cp.then_inc(x_saved[j], 1)

        if PHASES < 3:
            return
        with phase():
            chain = psem("chain")
            var_ready = psem("var_ready")
            std_ready = psem("std_ready")
            delta_ready = psem("delta_ready")
            root_ready = psem("root_ready")
            gates_ready = psem("gates_ready")
            gates_turned = psem("gates_turned")
            gates_stored = psem("gates_stored")
            NG = NT * E0
            ec = carver(arena_w1, n1w + n2w)
            z, zs, zr, s1, s2, t1 = (ec(NG, R) for _ in range(6))
            m1, m2 = ec(NT, R), ec(NT, R)
            block = enter(nc.Block())

            def grp(ap):
                return ap.rearrange("p (t e) -> p t e", t=NT)

            def wide(ap):
                return ap.unsqueeze(2).broadcast_to([R, NT, E0])

            @block.vector
            def _(dve):
                count = [0]

                def link(ins):
                    count[0] += 1
                    ins.then_inc(chain, 1)
                    dve.wait_ge(chain, count[0])

                tt, ts, red = nc.vector.tensor_tensor, nc.vector.tensor_scalar, nc.vector.tensor_reduce
                link(red(m1, grp(lg0), AX_X, ALU.add))
                link(ts(m2, m1, 1.0 / E0, None, ALU.mult))
                link(tt(grp(z), grp(lg0), wide(m2), ALU.subtract))
                link(tt(t1, z, z, ALU.mult))
                link(red(m1, grp(t1), AX_X, ALU.add))
                ts(m2, m1, 1.0 / E0, EPS, ALU.mult, ALU.add).then_inc(var_ready, 1)
                dve.wait_ge(std_ready, 1)
                link(nc.vector.reciprocal(m2, m1))
                link(tt(grp(z), grp(z), wide(m2), ALU.mult))
                link(red(m1, grp(z), AX_X, ALU.max))
                link(tt(grp(t1), grp(z), wide(m1), ALU.subtract))
                link(ts(z, t1, 0.5, None, ALU.mult))
                for t in range(NT):
                    last = nc.vector.max(zs[:, t * E0:t * E0 + 8], z[:, t * E0:(t + 1) * E0])
                link(last)
                for t in range(NT):
                    last = nc.vector.match_replace(zr[:, t * E0:(t + 1) * E0], zs[:, t * E0:t * E0 + 8],
                                                   z[:, t * E0:(t + 1) * E0], -1e30)
                link(last)
                for t in range(NT):
                    last = nc.vector.max(zs[:, t * E0 + 8:(t + 1) * E0], zr[:, t * E0:(t + 1) * E0])
                link(last)
                link(tt(t1, zs, zs, ALU.mult))
                link(nc.vector.tensor_tensor_scan(s1, p2("seg_e0", R), zs, 0.0, ALU.mult, ALU.add))
                link(nc.vector.tensor_tensor_scan(s2, p2("seg_e0", R), t1, 0.0, ALU.mult, ALU.add))
                link(tt(s1, s1, p2("inv_k", R), ALU.mult))
                link(tt(s2, s2, p2("inv_k", R), ALU.mult))
                link(tt(t1, s1, s1, ALU.mult))
                link(tt(s2, s2, t1, ALU.subtract))
                link(tt(t1, p2("inv_k", R), s2, ALU.subtract))
                ts(s2, t1, 0.0, None, ALU.max).then_inc(delta_ready, 1)
                dve.wait_ge(root_ready, 1)
                link(tt(s1, s1, t1, ALU.subtract))
                link(tt(t1, s1, zs, ALU.is_le))
                link(red(m1, grp(t1), AX_X, ALU.add))
                link(tt(grp(t1), grp(p2("rank_k", R)), wide(m1), ALU.is_equal))
                link(tt(t1, t1, s1, ALU.mult))
                link(red(m1, grp(t1), AX_X, ALU.add))
                link(tt(grp(t1), grp(z), wide(m1), ALU.subtract))
                nc.vector.scalar_tensor_tensor(z, t1, 0.0, t1, ALU.max, ALU.mult).then_inc(gates_ready, 1)
                for b in range(-(-NT // 4)):
                    n = min(4, NT - 4 * b)
                    dve.wait_ge(gates_turned, b + 1)
                    nc.vector.tensor_copy(gate_t[:, 4 * b * R:(4 * b + n) * R], bank[b][0:E0, 0:n * R]).then_inc(gates_stored, 1)

            @block.scalar
            def _(act):
                act.wait_ge(var_ready, 1)
                nc.scalar.activation(m1, m2, ACT.Sqrt).then_inc(std_ready, 1)
                act.wait_ge(delta_ready, 1)
                nc.scalar.activation(t1, s2, ACT.Sqrt).then_inc(root_ready, 1)

            @block.tensor
            def _(pe):
                pe.wait_ge(gates_ready, 1)
                for b in range(-(-NT // 4)):
                    n = min(4, NT - 4 * b)
                    for k in range(n):
                        t = 4 * b + k
                        mm = nc.tensor.transpose(bank[b][0:E0, k * R:(k + 1) * R], z[:, t * E0:(t + 1) * E0], ident[0:R, 0:R])
                    mm.then_inc(gates_turned, 1)

        if PHASES < 4:
            return
        with phase():
            z1_done, z1_gated, hid_done, hid_act, z2_done, z2_gated, y_done, y_added = (
                psem(n) for n in ("z1_done", "z1_gated", "hid_done", "hid_act", "z2_done", "z2_gated", "y_done", "y_added"))
            g_out = psem("g_out")
            W = 2 * R
            bc = carver(arena_w1, n1w + n2w)
            z1 = bc(W)
            z2 = bc(W)
            gsb = bc(2 * W)
            hid = bc(OC * W)
            block = enter(nc.Block())

            @block.tensor
            def _(pe):
                w_in1 = p2("w_in1").rearrange("p (c n) -> p c n", c=2)
                w_out1 = p2("w_out1").rearrange("p (c n) -> p c n", c=OC)
                w_in2 = p2("w_in2").rearrange("p (c n) -> p c n", c=OC)
                with pe.Fori(0, PAIRS) as i:
                    n1 = pe.snap(i + 1)
                    tok = pe.snap(i * W)
                    pe.wait_ge(z1_gated, i)
                    pe.wait_ge(g_out, i)
                    for g, name in enumerate(("c1", "c2")):
                        nc.tensor.matmul(bank[6][:, g * W:(g + 1) * W], p2(name, E0), gate_t[:, bass.ds(tok, W)],
                                         start=True, stop=True)
                    for k in range(2):
                        mm = nc.tensor.matmul(bank[0][:, 0:W], w_in1[:, k, :], x_t[:, bass.ds(tok + k * NT * R, W)],
                                              start=(k == 0), stop=(k == 1))
                    mm.then_inc(z1_done, 1)
                    pe.wait_ge(z1_gated, n1)
                    for f in range(OC):
                        if f % 2 == 0:
                            pe.wait_ge(hid_act, i * (OC // 2))
                        mm = nc.tensor.matmul(bank[2 + f // 2][:, (f % 2) * W:(f % 2 + 1) * W], w_out1[:, f, :], z1,
                                              start=True, stop=True)
                        if f % 2:
                            mm.then_inc(hid_done, 1)
                    pe.wait_ge(z2_gated, i)
                    for f in range(OC):
                        if f % 2 == 0:
                            pe.wait_ge(hid_act, i * (OC // 2) + f // 2 + 1)
                        mm = nc.tensor.matmul(bank[1][:, 0:W], w_in2[:, f, :], hid[:, f * W:(f + 1) * W],
                                              start=(f == 0), stop=(f == OC - 1))
                    mm.then_inc(z2_done, 1)
                    pe.wait_ge(z2_gated, n1)
                    pe.wait_ge(y_added, i)
                    for j in range(2):
                        mm = nc.tensor.matmul(bank[7][0:R, j * D:(j + 1) * D], z2[:, j * R:(j + 1) * R], p2("w_out2"),
                                              start=True, stop=True)
                    mm.then_inc(y_done, 1)

            @block.vector
            def _(dve):
                with dve.Fori(0, PAIRS) as i:
                    n1 = dve.snap(i + 1)
                    dve.wait_ge(z1_done, n1)
                    dve.wait_ge(hid_done, i * (OC // 2))
                    nc.vector.tensor_copy(gsb, bank[6][:, 0:2 * W]).then_inc(g_out, 1)
                    dve.wait_ge(g_out, n1)
                    nc.vector.scalar_tensor_tensor(z1, bank[0][:, 0:W], p2("b_in1"), gsb[:, 0:W],
                                                   ALU.add, ALU.mult).then_inc(z1_gated, 1)
                    dve.wait_ge(z2_done, n1)
                    dve.wait_ge(y_done, i)
                    nc.vector.scalar_tensor_tensor(z2, bank[1][:, 0:W], p2("b_in2"), gsb[:, W:2 * W],
                                                   ALU.add, ALU.mult).then_inc(z2_gated, 1)
                    dve.wait_ge(y_done, n1)
                    h = resid[0:R, bass.ds(i * 2 * D, 2 * D)]
                    nc.vector.tensor_tensor(h, h, bank[7][0:R, 0:2 * D], ALU.add).then_inc(y_added, 1)

            @block.scalar
            def _(act):
                with act.Fori(0, PAIRS) as i:
                    act.wait_ge(z2_done, i)
                    for f in range(OC // 2):
                        act.wait_ge(hid_done, i * (OC // 2) + f + 1)
                        nc.scalar.activation(hid[:, 2 * f * W:2 * (f + 1) * W], bank[2 + f][:, 0:2 * W], ACT.Gelu).then_inc(hid_act, 1)

        if PHASES < 5:
            return
        with phase():
            stats = [pair("st"), pair("ag"), pair("ve")]
            (powered, normed, sq_done, roots, rooted, floored, inverted, k_ready, turned, t_ready, v_done, g_done, beta_out,
             v_out, at_out, n_masked, n_reduced, n_scaled, n_stored, x_added, g_free) = (
                pair(n) for n in ("powered", "normed", "sq_done", "roots", "rooted", "floored", "inverted", "k_ready",
                                      "turned", "t_ready", "v_done", "g_done", "beta_out", "v_out", "at_out", "n_masked",
                                      "n_reduced", "n_scaled", "n_stored", "x_added", "g_free"))
            tables = psem("tables")
            chain = psem("chain")
            cc = carver(arena_w1, n1w + n2w)
            lt, ln = cc(H1 * R, R), cc(H1 * R, R)
            dec = cc(8, R)
            kn = [cc(D, R) for _ in range(2)]
            xk = [cc(4 * R) for _ in range(2)]
            sq = [cc(D, R) for _ in range(2)]
            nf = [cc(H1 * R, R) for _ in range(2)]
            nk = [cc(H1 * TOK, R) for _ in range(2)]
            nb = [cc(H1 * TOK, R) for _ in range(2)]
            sc = [cc(12, R) for _ in range(2)]
            block = enter(nc.Block())

            @block.sync
            def _(sp):
                sp.dma_start(arena_w2[:, 0:W2S // 2], w2_h[:, 0:W2S // 2]).then_inc(w2a_in, 16)
                with sp.Fori(0, PAIRS) as i:
                    for j in range(2):
                        sp.wait_ge(n_scaled[j], i + 1)
                        sp.dma_start(n_rows[bass.ds((2 * i + j) * R, R), :], nb[j]).then_inc(n_stored[j], 16)
                for j in range(2):
                    sp.wait_ge(n_stored[j], 16 * PAIRS)

            @block.tensor
            def _(pe):
                w_vb = p2("w_vb").rearrange("p (c n) -> p c n", c=2)
                with pe.Fori(0, PAIRS) as i:
                    n1 = pe.snap(i + 1)
                    for j in range(2):
                        pe.wait_ge(normed[j], n1)
                        pe.wait_ge(k_ready[j], n1)
                        pe.wait_ge(t_ready[j], i)
                        for k in range(4):
                            src = (xn, kn)[k // 2][j][:, (k % 2) * 128:(k % 2 + 1) * 128]
                            mm = nc.tensor.transpose(bank[j][:, k * R:(k + 1) * R], src, ident[0:R, 0:R])
                        mm.then_inc(turned[j], 1)
                    for j in range(2):
                        pe.wait_ge(t_ready[j], n1)
                        pe.wait_ge(v_out[j], i)
                        pe.wait_ge(beta_out[j], i)
                        for k in range(2):
                            mm = nc.tensor.matmul(bank[2 + j][0:R, 0:D + H1], xk[j][:, k * R:(k + 1) * R], w_vb[:, k, :],
                                                  start=(k == 0), stop=(k == 1))
                        mm.then_inc(v_done[j], 1)
                        pe.wait_ge(n_masked[j], i)
                        pe.wait_ge(at_out[j], i)
                        for h in range(H1):
                            kt = xk[j][:, (2 + h) * R:(3 + h) * R]
                            mm = nc.tensor.matmul(bank[4 + j][0:R, h * R:(h + 1) * R], kt, kt, start=True, stop=True)
                        mm.then_inc(g_done[j], 1)

            @block.scalar
            def _(act):
                act.wait_ge(tables, 1)
                nc.scalar.activation(dec[:, 0:H1], p2("decay", R), ACT.Sigmoid).then_inc(chain, 1)
                act.wait_ge(chain, 1)
                nc.scalar.activation(dec[:, H1:2 * H1], dec[:, 0:H1], ACT.Ln).then_inc(chain, 1)
                act.wait_ge(chain, 2)
                for h in range(H1):
                    g = dec[:, H1 + h:H1 + h + 1]
                    nc.scalar.activation(lt[:, h * R:(h + 1) * R], p2("lag_t", R), ACT.Exp, scale=g)
                    nc.scalar.activation(ln[:, h * R:(h + 1) * R], p2("lag", R), ACT.Exp, scale=g).then_inc(chain, 1)
                with act.Fori(0, PAIRS) as i:
                    n1 = act.snap(i + 1)
                    for j in range(2):
                        act.wait_ge(turned[j], n1)
                        act.wait_ge(g_done[j], i)
                        nc.scalar.copy(xk[j], bank[j][:, 0:4 * R]).then_inc(t_ready[j], 1)
                    for j in range(2):
                        act.wait_ge(v_done[j], n1)
                        act.wait_ge(n_scaled[j], i)
                        nc.scalar.activation(sc[j][:, 6:8], bank[2 + j][0:R, D:D + H1], ACT.Sigmoid).then_inc(beta_out[j], 1)
                        act.wait_ge(beta_out[j], n1)
                        for h in range(H1):
                            cp = nc.scalar.activation(keepx[0:R, bass.ds((2 * i + j) * D + h * 128, 128)],
                                                      bank[2 + j][0:R, h * 128:(h + 1) * 128], ACT.Copy,
                                                      scale=sc[j][:, 6 + h:7 + h])
                        cp.then_inc(v_out[j], 1)

            @block.vector
            def _(dve):
                for j in range(2):
                    nc.vector.memset(sc[j][:, 8:10], 0.5)
                nc.vector.memset(sc[0][:, 10:11], 0.5).then_inc(tables, 1)
                dve.wait_ge(chain, 2 + H1)
                for h in range(H1):
                    nc.vector.tensor_tensor(lt[:, h * R:(h + 1) * R], lt[:, h * R:(h + 1) * R], p2("keep_t", R), ALU.mult)
                    last = nc.vector.tensor_tensor(ln[:, h * R:(h + 1) * R], ln[:, h * R:(h + 1) * R], p2("keep", R), ALU.mult)
                last.then_inc(tables, 1)
                dve.wait_ge(tables, 2)
                with dve.Fori(1, PAIRS + 1) as n1:
                    i = dve.snap(n1 - 1)
                    for j in range(2):
                        h = resid[0:R, bass.ds((2 * i + j) * D, D)]
                        stand_alone(dve)
                        dve.wait_ge(k_ready[j], i)
                        norm_stats(dve, h, j, stats, n1)
                        dve.wait_ge(powered[j], n1)
                        dve.wait_ge(turned[j], i)
                        norm_apply(xn[j], h, j).then_inc(normed[j], 1)
                        dve.wait_ge(normed[j], n1)
                        nc.vector.tensor_tensor(h, h, xn[j], ALU.add).then_inc(x_added[j], 1)
                        nc.vector.tensor_tensor(sq[j], xn[j], xn[j], ALU.mult).then_inc(sq_done[j], 1)
                        dve.wait_ge(sq_done[j], n1)
                        nc.vector.tensor_reduce(sc[j][:, 0:2], sq[j].rearrange("p (h d) -> p h d", h=H1), AX_X,
                                                ALU.add).then_inc(roots[j], 1)
                        dve.wait_ge(rooted[j], n1)
                        nc.vector.tensor_scalar(sc[j][:, 2:4], sc[j][:, 4:6], 1e-12, None, ALU.max).then_inc(floored[j], 1)
                        dve.wait_ge(floored[j], n1)
                        nc.vector.reciprocal(sc[j][:, 4:6], sc[j][:, 2:4]).then_inc(inverted[j], 1)
                        dve.wait_ge(inverted[j], n1)
                        for g in range(H1):
                            kk = nc.vector.tensor_scalar(kn[j][:, g * 128:(g + 1) * 128], xn[j][:, g * 128:(g + 1) * 128],
                                                         sc[j][:, 4 + g:5 + g], None, ALU.mult)
                        kk.then_inc(k_ready[j], 1)
                    for j in range(2):
                        dve.wait_ge(g_done[j], n1)
                        nc.vector.tensor_tensor(attn_t[:, bass.ds((2 * i + j) * H1 * R, H1 * R)], bank[4 + j][0:R, 0:H1 * R],
                                                lt, ALU.mult).then_inc(at_out[j], 1)
                        nc.vector.tensor_tensor(nf[j], bank[4 + j][0:R, 0:H1 * R], ln, ALU.mult).then_inc(n_masked[j], 1)
                        dve.wait_ge(n_masked[j], n1)
                        nc.vector.tensor_reduce(nk[j].rearrange("p (h t) -> p h t", h=H1),
                                                nf[j].rearrange("p (h m t) -> p h t m", h=H1, m=IPT), AX_X,
                                                ALU.add).then_inc(n_reduced[j], 1)
                        dve.wait_ge(n_reduced[j], n1)
                        dve.wait_ge(beta_out[j], n1)
                        dve.wait_ge(n_stored[j], 16 * i)
                        nc.vector.tensor_tensor(nb[j].rearrange("p (h t) -> p h t", h=H1), nk[j].rearrange("p (h t) -> p h t", h=H1),
                                                sc[j][:, 6:8].unsqueeze(2).broadcast_to([R, H1, TOK]),
                                                ALU.mult).then_inc(n_scaled[j], 1)

            @block.gpsimd
            def _(pool):
                pool.wait_ge(tables, 1)
                with pool.Fori(0, PAIRS) as i:
                    n1 = pool.snap(i + 1)
                    for j in range(2):
                        norm_power(pool, j, stats[2], powered, n1)
                        pool.wait_ge(roots[j], n1)
                        nc.gpsimd.tensor_tensor(sc[j][:, 4:6], sc[j][:, 0:2], sc[j][:, 8:10], ALU.pow).then_inc(rooted[j], 1)

        if PHASES < 6:
            return
        with phase():
            n_in = psem("n_in")
            chain = psem("chain")
            zeroed = psem("zeroed")
            solved = psem("solved")
            a_stored = psem("a_stored")
            prod = work[:, 0:(TOK - 1) ** 2]
            block = enter(nc.Block())

            def systems(rows, h):
                return rows[0:B * TOK, h * TOK:(h + 1) * TOK].rearrange("(b i) j -> b i j", b=B)

            @block.sync
            def _(sp):
                for h in range(H1):
                    sp.dma_start(sys_n[h * B:(h + 1) * B, :].rearrange("p (i j) -> p i j", i=TOK),
                                 systems(n_rows, h)).then_inc(n_in, 16)
                sp.dma_start(arena_w1[:, :], w1_h).then_inc(w1_in, 16)
                sp.wait_ge(solved, 1)
                for h in range(H1):
                    sp.dma_start(systems(a_rows, h),
                                 sys_x[h * B:(h + 1) * B, :].rearrange("p (j i) -> p j i", j=TOK)).then_inc(a_stored, 16)
                sp.wait_ge(a_stored, 16 * H1)

            @block.vector
            def _(dve):
                x = sys_x.rearrange("p (c i) -> p c i", c=TOK)
                n = sys_n.rearrange("p (i j) -> p i j", i=TOK)
                nc.vector.memset(sys_x, 0.0).then_inc(zeroed, 1)
                dve.wait_ge(zeroed, 1)
                nc.vector.memset(sys_x[:, 0:TOK * TOK:TOK + 1], 1.0).then_inc(zeroed, 1)
                dve.wait_ge(zeroed, 2)
                dve.wait_ge(n_in, 16 * H1)
                for i in range(1, TOK):
                    w = prod[:, 0:i * i].rearrange("p (c j) -> p c j", c=i)
                    nc.vector.tensor_tensor(w, x[:, 0:i, 0:i], n[:, i, 0:i].unsqueeze(1).broadcast_to([128, i, i]),
                                            ALU.mult).then_inc(chain, 1)
                    dve.wait_ge(chain, 2 * i - 1)
                    nc.vector.tensor_reduce(x[:, 0:i, i], w, AX_X, ALU.add).then_inc(chain, 1)
                    dve.wait_ge(chain, 2 * i)
                nc.vector.engine_nop().then_inc(solved, 1)

        if PHASES < 7:
            return
        with phase():
            stats = [pair("st"), pair("ag"), pair("ve")]
            (a_in, a_block, vn_done, vn_out, o_done, o_out, r_done, added, powered, normed, turned, xt_ready, logits,
             logits_out, x_kept) = (
                pair(n) for n in ("a_in", "a_block", "vn_done", "vn_out", "o_done", "o_out", "r_done", "added",
                                      "powered", "normed", "turned", "xt_ready", "logits", "logits_out", "x_kept"))
            setup = psem("setup")
            wc = carver(work)
            lgr = wc(NT * NE, R)
            xn = [wc(D, R) for _ in range(2)]
            xt = [wc(2 * R) for _ in range(2)]
            st = [wc(8, R) for _ in range(2)]
            ve = [wc(4, R) for _ in range(2)]
            ac = [wc(H1 * TOK, R) for _ in range(2)]
            ab = [wc(H1 * R, R) for _ in range(2)]
            vn = [wc(D, R) for _ in range(2)]
            ot = [wc(H1 * R) for _ in range(2)]
            block = enter(nc.Block())

            @block.sync
            def _(sp):
                with sp.Fori(0, PAIRS) as i:
                    for j in range(2):
                        sp.wait_ge(a_block[j], i)
                        sp.dma_start(ac[j], a_rows[bass.ds((2 * i + j) * R, R), :]).then_inc(a_in[j], 16)

            @block.gpsimd
            def _(pool):
                pool.wait_ge(setup, 2)
                with pool.Fori(0, PAIRS) as i:
                    n1, n16 = pool.snap(i + 1), pool.snap(16 * i + 16)
                    for j in range(2):
                        pool.wait_ge(a_in[j], n16)
                        pool.wait_ge(vn_done[j], i)
                        for h in range(H1):
                            tt = nc.gpsimd.tensor_tensor(
                                ab[j][:, h * R:(h + 1) * R].rearrange("p (m t) -> p m t", m=IPT),
                                ac[j][:, h * TOK:(h + 1) * TOK].unsqueeze(1).broadcast_to([R, IPT, TOK]),
                                c("mask_img", R).unsqueeze(2).broadcast_to([R, IPT, TOK]), ALU.mult)
                        tt.then_inc(a_block[j], 1)
                    for j in range(2):
                        norm_power(pool, j, stats[2], powered, n1)
                    for j in range(2):
                        stand_alone(pool)
                        pool.wait_ge(normed[j], n1)
                        nc.gpsimd.tensor_copy(keepx[0:R, bass.ds((2 * i + j) * D, D)], xn[j]).then_inc(x_kept[j], 1)

            @block.tensor
            def _(pe):
                w_read = c("w_read").rearrange("p (c n) -> p c n", c=2)
                w_r = c("w_r").rearrange("p (c n) -> p c n", c=2)
                with pe.Fori(0, PAIRS) as i:
                    n1 = pe.snap(i + 1)
                    for j in range(2):
                        pe.wait_ge(a_block[j], n1)
                        pe.wait_ge(vn_out[j], i)
                        for h in range(H1):
                            mm = nc.tensor.matmul(bank[j][0:R, h * 128:(h + 1) * 128], ab[j][:, h * R:(h + 1) * R],
                                                  keepx[0:R, bass.ds((2 * i + j) * D + h * 128, 128)], start=True, stop=True)
                        mm.then_inc(vn_done[j], 1)
                    for j in range(2):
                        pe.wait_ge(vn_out[j], n1)
                        pe.wait_ge(o_out[j], i)
                        for h in range(H1):
                            mm = nc.tensor.matmul(bank[2 + j][:, h * R:(h + 1) * R], vn[j][:, h * 128:(h + 1) * 128],
                                                  attn_t[:, bass.ds(((2 * i + j) * H1 + h) * R, R)], start=True, stop=True)
                        mm.then_inc(o_done[j], 1)
                    for j in range(2):
                        pe.wait_ge(o_out[j], n1)
                        pe.wait_ge(added[j], i)
                        for k in range(2):
                            mm = nc.tensor.matmul(bank[4 + j][0:R, 0:D], ot[j][:, k * R:(k + 1) * R], w_read[:, k, :],
                                                  start=(k == 0), stop=(k == 1))
                        mm.then_inc(r_done[j], 1)
                    for j in range(2):
                        pe.wait_ge(normed[j], n1)
                        pe.wait_ge(logits_out[j], i)
                        for k in range(2):
                            mm = nc.tensor.transpose(bank[6 + j][:, k * R:(k + 1) * R], xn[j][:, k * 128:(k + 1) * 128],
                                                     ident[0:R, 0:R])
                        mm.then_inc(turned[j], 1)
                    for j in range(2):
                        pe.wait_ge(xt_ready[j], n1)
                        for k in range(2):
                            mm = nc.tensor.matmul(bank[6 + j][0:R, 2 * R:2 * R + NE], xt[j][:, k * R:(k + 1) * R],
                                                  w_r[:, k, :], start=(k == 0), stop=(k == 1))
                        mm.then_inc(logits[j], 1)

            @block.scalar
            def _(act):
                with act.Fori(0, PAIRS) as i:
                    n1 = act.snap(i + 1)
                    for j in range(2):
                        act.wait_ge(vn_done[j], n1)
                        act.wait_ge(o_done[j], i)
                        nc.scalar.copy(vn[j], bank[j][0:R, 0:D]).then_inc(vn_out[j], 1)
                    for j in range(2):
                        act.wait_ge(o_done[j], n1)
                        act.wait_ge(r_done[j], i)
                        nc.scalar.copy(ot[j], bank[2 + j][:, 0:H1 * R]).then_inc(o_out[j], 1)
                    for j in range(2):
                        act.wait_ge(turned[j], n1)
                        act.wait_ge(logits[j], i)
                        nc.scalar.copy(xt[j], bank[6 + j][:, 0:2 * R]).then_inc(xt_ready[j], 1)

            @block.vector
            def _(dve):
                for j in range(2):
                    nc.vector.memset(ve[j][:, 2:3], -0.5).then_inc(setup, 1)
                with dve.Fori(0, PAIRS) as i:
                    n1 = dve.snap(i + 1)
                    for j in range(2):
                        h = resid[0:R, bass.ds((2 * i + j) * D, D)]
                        dve.wait_ge(r_done[j], n1)
                        nc.vector.tensor_tensor(h, h, bank[4 + j][0:R, 0:D], ALU.add).then_inc(added[j], 1)
                        norm_stats(dve, h, j, stats, n1, added)
                        dve.wait_ge(powered[j], n1)
                        dve.wait_ge(turned[j], i)
                        dve.wait_ge(x_kept[j], i)
                        norm_apply(xn[j], h, j).then_inc(normed[j], 1)
                    for j in range(2):
                        dve.wait_ge(logits[j], n1)
                        nc.vector.tensor_tensor(lgr[:, bass.ds((2 * i + j) * NE, NE)], bank[6 + j][0:R, 2 * R:2 * R + NE],
                                                c("b_r", R), ALU.add).then_inc(logits_out[j], 1)

        if PHASES < 8:
            return
        x_sent = psem("x_sent")
        with phase():
            chain = psem("chain")
            shifted_s = psem("shifted")
            exp_done = psem("exp_done")
            hot_ready = psem("hot_ready")
            counted = psem("counted")
            slots_ready = psem("slots_ready")
            NG = NT * NE
            rc = carver(work, NG)
            dl, ex, eq, cu, one_hot, cte, inc, tmp = (rc(NG, R) for _ in range(8))
            m1, m2 = rc(NT, R), rc(NT, R)
            cmp_t = rc(NE * MT, R)
            tiles_e, upto_e, off_e = rc(NE, R), rc(NE, R), rc(NE, R)
            past = rc(ST * NE, R)
            eno = rc(ST, R)
            block = enter(nc.Block())

            def by_tile(ap):
                return ap.rearrange("p (t e) -> p t e", t=NT)

            @block.sync
            def _(sp):
                sp.dma_start(arena_w2[:, W2S // 2:W2S], w2_h[:, W2S // 2:W2S]).then_inc(w2b_in, 16)

            @block.scalar
            def _(act):
                act.wait_ge(shifted_s, 1)
                nc.scalar.activation(ex, dl, ACT.Exp).then_inc(exp_done, 1)

            @block.tensor
            def _(pe):
                pe.wait_ge(hot_ready, 1)
                nc.tensor.matmul(bank[0][0:R, 0:NG], c("before", R), one_hot, start=True, stop=True)
                nc.tensor.matmul(bank[1][0:R, 0:NG], c("ones", R), one_hot, start=True, stop=True).then_inc(counted, 1)

            @block.vector
            def _(dve):
                count = [0]

                def link(ins):
                    count[0] += 1
                    ins.then_inc(chain, 1)
                    dve.wait_ge(chain, count[0])

                tt, ts, red = nc.vector.tensor_tensor, nc.vector.tensor_scalar, nc.vector.tensor_reduce
                link(red(m1, by_tile(lgr), AX_X, ALU.max))
                tt(by_tile(dl), by_tile(lgr), m1.unsqueeze(2).broadcast_to([R, NT, NE]), ALU.subtract).then_inc(shifted_s, 1)
                dve.wait_ge(shifted_s, 1)
                link(ts(eq, dl, 0.0, None, ALU.is_equal))
                link(nc.vector.tensor_tensor_scan(cu, c("seg_e", R), eq, 0.0, ALU.mult, ALU.add))
                link(nc.vector.scalar_tensor_tensor(tmp, cu, 1.0, eq, ALU.is_equal, ALU.mult))
                tt(by_tile(one_hot), by_tile(tmp), c("valid", R).unsqueeze(2).broadcast_to([R, NT, NE]), ALU.mult).then_inc(hot_ready, 1)
                dve.wait_ge(exp_done, 1)
                link(red(m2, by_tile(ex), AX_X, ALU.add))
                link(nc.vector.reciprocal(gate[0:R, :], m2))
                dve.wait_ge(counted, 1)
                link(nc.vector.tensor_copy(cte.rearrange("p (e t) -> p e t", e=NE),
                                           bank[1][0:R, 0:NG].rearrange("p (t e) -> p e t", e=NE)))
                link(nc.vector.tensor_tensor_scan(inc, c("seg_t", R), cte, 0.0, ALU.mult, ALU.add))
                link(tt(cte, inc, cte, ALU.subtract))
                total = inc.rearrange("p (e t) -> p e t", e=NE)[:, :, NT - 1:NT]
                link(tt(cmp_t.rearrange("p (e k) -> p e k", e=NE), total.broadcast_to([R, NE, MT]),
                        c("starts", R).unsqueeze(1).broadcast_to([R, NE, MT]), ALU.is_gt))
                link(red(tiles_e, cmp_t.rearrange("p (e k) -> p e k", e=NE), AX_X, ALU.add))
                link(nc.vector.tensor_tensor_scan(upto_e, c("ones", R)[:, 0:NE], tiles_e, 0.0, ALU.mult, ALU.add))
                link(tt(off_e, upto_e, tiles_e, ALU.subtract))
                link(ts(off_e, off_e, 128.0, None, ALU.mult))
                link(tt(cte.rearrange("p (e t) -> p e t", e=NE), cte.rearrange("p (e t) -> p e t", e=NE),
                        off_e.unsqueeze(2).broadcast_to([R, NE, NT]), ALU.add))
                link(tt(by_tile(tmp), by_tile(bank[0][0:R, 0:NG]), cte.rearrange("p (e t) -> p t e", e=NE), ALU.add))
                link(tt(tmp, tmp, one_hot, ALU.mult))
                link(red(m1, by_tile(tmp), AX_X, ALU.add))
                nc.vector.tensor_copy(slot_i[0:R, :], m1).then_inc(slots_ready, 1)
                link(tt(past.rearrange("p (s e) -> p s e", s=ST), upto_e.unsqueeze(1).broadcast_to([R, ST, NE]),
                        c("tile_no", R).unsqueeze(2).broadcast_to([R, ST, NE]), ALU.is_le))
                link(red(eno, past.rearrange("p (s e) -> p s e", s=ST), AX_X, ALU.add))
                link(ts(eno, eno, float(NE - 1), None, ALU.min))
                link(nc.vector.tensor_copy(expert_i[0:1, :], eno[0:1, :]))

            @block.gpsimd
            def _(pool):
                pool.wait_ge(slots_ready, 1)
                for t in range(NT):
                    rows = min(R, (B - t * IPT) * TOK)
                    pool.indirect_dma_start(x_slots, bass.IndirectOffsetOnAxis(ap=slot_i[0:rows, t:t + 1], axis=0),
                                            keepx[0:rows, t * D:(t + 1) * D], None).then_inc(x_sent, 16)
                pool.wait_ge(x_sent, 16 * NT)

        if PHASES < 9:
            return
        with phase():
            x_turned = psem("x_turned")
            xt_ready = psem("xt_ready")
            (x_in, h_done, h_out, h_turned, y_done, y_out, y_stored) = (
                pair(n) for n in ("x_in", "h_done", "h_out", "h_turned", "y_done", "y_out",
                                      "y_stored"))
            h_act = [pair(f"h_act{f}_") for f in range(2)]
            wc = carver(work)
            xg = [wc(D) for _ in range(2)]
            xgt = wc(2 * D)
            hp = [wc(FF) for _ in range(2)]
            ht = [wc(FF) for _ in range(2)]
            yo = [wc(D) for _ in range(2)]
            block = enter(nc.Block())

            @block.sync
            def _(sp):
                with sp.Fori(0, ST // 2) as i:
                    n1 = sp.snap(i + 1)
                    for j in range(2):
                        sp.wait_ge(x_turned, i)
                        sp.dma_start(xg[j], x_slots[bass.ds((2 * i + j) * 128, 128), :]).then_inc(x_in[j], 16)

            @block.tensor
            def _(pe):
                pe.wait_ge(w1_in, 16)
                pe.wait_ge(w2a_in, 16)
                pe.wait_ge(w2b_in, 16)
                with pe.Fori(0, ST // 2) as i:
                    n1, n16 = pe.snap(i + 1), pe.snap(16 * i + 16)
                    expert = [pe.value_load(expert_i[0:1, bass.ds(2 * i + j, 1)], min_val=0, max_val=NE - 1) for j in range(2)]
                    pe.wait_ge(xt_ready, i)
                    for j in range(2):
                        pe.wait_ge(x_in[j], n16)
                        for k in range(2):
                            mm = nc.tensor.transpose(bank[6][:, (2 * j + k) * 128:(2 * j + k + 1) * 128],
                                                     xg[j][:, k * 128:(k + 1) * 128], ident)
                    mm.then_inc(x_turned, 1)
                    pe.wait_ge(xt_ready, n1)
                    for j in range(2):
                        pe.wait_ge(h_out[j], i * 2)
                        for f in range(2):
                            for k in range(2):
                                mm = nc.tensor.matmul(bank[2 * j + f][:, :], xgt[:, (2 * j + k) * 128:(2 * j + k + 1) * 128],
                                                      arena_w1[:, bass.ds(expert[j] * (2 * FF) + (k * FF + f * 512), 512)],
                                                      start=(k == 0), stop=(k == 1))
                            mm.then_inc(h_done[j], 1)
                    for j in range(2):
                        for f in range(2):
                            pe.wait_ge(h_out[j], i * 2 + f + 1)
                            if j == 0:
                                pe.wait_ge(h_act[f][1], i)
                            else:
                                pe.wait_ge(h_act[f][0], n1)
                            for k in range(4):
                                mm = nc.tensor.transpose(bank[4 + f][:, k * 128:(k + 1) * 128],
                                                         hp[j][:, (4 * f + k) * 128:(4 * f + k + 1) * 128], ident)
                            mm.then_inc(h_turned[j], 1)
                        if j == 0:
                            pe.wait_ge(y_out[1], i)
                        else:
                            pe.wait_ge(y_out[0], n1)
                        for f in range(2):
                            pe.wait_ge(h_act[f][j], n1)
                            for k in range(4):
                                g = 4 * f + k
                                mm = nc.tensor.matmul(bank[7][:, j * D:(j + 1) * D], ht[j][:, g * 128:(g + 1) * 128],
                                                      arena_w2[:, bass.ds(expert[j] * (FC * D) + g * D, D)],
                                                      start=(g == 0), stop=(g == FC - 1))
                        mm.then_inc(y_done[j], 1)

            @block.vector
            def _(dve):
                with dve.Fori(0, ST // 2) as i:
                    n1 = dve.snap(i + 1)
                    expert = [dve.value_load(expert_i[0:1, bass.ds(2 * i + j, 1)], min_val=0, max_val=NE - 1) for j in range(2)]
                    dve.wait_ge(x_turned, n1)
                    dve.wait_ge(h_done[1], i * 2)
                    nc.vector.tensor_copy(xgt, bank[6][:, :]).then_inc(xt_ready, 1)
                    for j in range(2):
                        for f in range(2):
                            dve.wait_ge(h_done[j], i * 2 + f + 1)
                            dve.wait_ge(h_turned[j], i * 2)
                            nc.vector.tensor_copy(hp[j][:, f * 512:(f + 1) * 512], bank[2 * j + f][:, :]).then_inc(h_out[j], 1)
                    for j in range(2):
                        dve.wait_ge(y_done[j], n1)
                        dve.wait_ge(y_stored[j], 16 * i)
                        nc.vector.tensor_tensor(yo[j], bank[7][:, j * D:(j + 1) * D],
                                                cst[:, bass.ds(expert[j] * D + atc["b2"][0], D)], ALU.add).then_inc(y_out[j], 1)

            @block.scalar
            def _(act):
                with act.Fori(0, ST // 2) as i:
                    n1 = act.snap(i + 1)
                    expert = [act.value_load(expert_i[0:1, bass.ds(2 * i + j, 1)], min_val=0, max_val=NE - 1) for j in range(2)]
                    for j in range(2):
                        for f in range(2):
                            act.wait_ge(h_turned[j], i * 2 + f + 1)
                            act.wait_ge(y_done[j], i)
                            for k in range(4):
                                g = 4 * f + k
                                cp = nc.scalar.activation(ht[j][:, g * 128:(g + 1) * 128], bank[4 + f][:, k * 128:(k + 1) * 128],
                                                          ACT.Gelu, bias=cst[:, bass.ds(expert[j] * FC + (atc["b1"][0] + g), 1)])
                            cp.then_inc(h_act[f][j], 1)

            @block.gpsimd
            def _(pool):
                with pool.Fori(0, ST // 2) as i:
                    n1 = pool.snap(i + 1)
                    for j in range(2):
                        pool.wait_ge(y_out[j], n1)
                        pool.dma_start(y_slots[bass.ds((2 * i + j) * 128, 128), :], yo[j]).then_inc(y_stored[j], 16)
                for j in range(2):
                    pool.wait_ge(y_stored[j], 16 * (ST // 2))

        with phase():
            NB = 4
            y_in = [psem(f"y_in{k}") for k in range(NB)]
            gated = psem("gated")
            out_sent = psem("out_sent")
            yg = [work[:, k * D:(k + 1) * D] for k in range(NB)]
            block = enter(nc.Block())

            def rows_of(t):
                return min(R, (B - t * IPT) * TOK)

            @block.gpsimd
            def _(pool):
                for t in range(NT):
                    if t >= NB:
                        pool.wait_ge(gated, t - NB + 1)
                    n = rows_of(t)
                    pool.indirect_dma_start(yg[t % NB][0:n, :], None, y_slots,
                                            bass.IndirectOffsetOnAxis(ap=slot_i[0:n, t:t + 1], axis=0)).then_inc(y_in[t % NB], 16)

            @block.vector
            def _(dve):
                for t in range(NT):
                    n = rows_of(t)
                    h = resid[0:n, t * D:(t + 1) * D]
                    dve.wait_ge(y_in[t % NB], 16 * (t // NB + 1))
                    nc.vector.scalar_tensor_tensor(h, yg[t % NB][0:n, :], gate[0:n, t:t + 1], h, ALU.mult,
                                                   ALU.add).then_inc(gated, 1)

            @block.sync
            def _(sp):
                for t in range(NT):
                    n = rows_of(t)
                    sp.wait_ge(gated, t + 1)
                    sp.dma_start(out_h[t * R:t * R + n, :], resid[0:n, t * D:(t + 1) * D]).then_inc(out_sent, 16)
                sp.wait_ge(out_sent, 16 * NT)


PHASES = 99


def lay_out(inp):
    import numpy as np

    f = {k: np.asarray(v) for k, v in inp.items()}

    def chunks(w, c):
        return w.reshape(c, 128, -1).transpose(1, 0, 2).reshape(128, -1)

    def rows(v, n=R):
        return np.broadcast_to(np.asarray(v).reshape(1, -1), (n, v.size))

    patches = f["x"].reshape(B, 3, 6, 16, 6, 16).transpose(0, 2, 4, 1, 3, 5).reshape(B, TOK - 1, FP)
    padded = np.zeros((NT * IPT, TOK, FP), np.float32)
    padded[:B, 1:] = patches
    x_h = np.ascontiguousarray(padded.reshape(NT, IPT, TOK, PC, 128).transpose(0, 4, 3, 1, 2).reshape(NT, 128, -1))

    p = {}
    p["w_lin"] = chunks(f["L0_tok_W_lin"].T, PC)
    p["pos"] = np.tile(f["L0_tok_position_embeddings"][0], (IPT, 1))
    add = np.concatenate([f["L0_tok_class_token"][0], rows(f["L0_tok_b_lin"], TOK - 1)], 0)
    p["pos_add"] = np.tile(add, (IPT, 1))
    p["w_q"] = chunks(f["L0_attn_Wq"].T, 2)
    p["b_q"] = rows(f["L0_attn_bq"])
    kv, bkv = f["L0_attn_Wkv"], f["L0_attn_bkv"]
    p["w_k"] = chunks(np.tile(kv[:HD].T, (1, HH)), 2)
    p["b_k"] = np.tile(bkv[:HD], HH)[:, None]
    p["w_v"] = chunks(kv[HD:].T, 2)
    p["b_v"] = rows(bkv[HD:])
    p["w_o"] = chunks(f["L0_attn_Wo"].T, 2)
    p["b_o"] = rows(f["L0_attn_bo"])
    p["proj"] = chunks(f["L0_ffn_proj"], 2)
    p["w_in1"] = chunks(f["L0_ffn_Win1"][:D], 2)
    p["b_in1"] = f["L0_ffn_Win1"][D][:, None]
    p["c1"], p["c2"] = f["L0_ffn_C1"], f["L0_ffn_C2"]
    p["w_out1"] = f["L0_ffn_Wout1"].T
    p["w_in2"] = chunks(f["L0_ffn_Win2"][:O0], OC)
    p["b_in2"] = f["L0_ffn_Win2"][O0][:, None]
    p["w_out2"] = f["L0_ffn_Wout2"].T
    p["w_vb"] = chunks(np.concatenate([f["L1_attn_W_write"].T, f["L1_attn_W_beta"].T], 1), 2)
    p["decay"] = rows(f["L1_attn_decay"])
    p["w_read"] = chunks(f["L1_attn_W_read"].T, 2)
    p["w_r"] = chunks(f["L1_ffn_Wr"], 2)
    p["b_r"] = rows(f["L1_ffn_br"])
    p["b1"] = f["L1_ffn_b1"].reshape(NE, FC, 128).transpose(2, 0, 1).reshape(128, -1)
    p["b2"] = rows(f["L1_ffn_b2"], 128)

    r = np.arange(R)
    img, pos = r // TOK, r % TOK
    same = img[:, None] == img[None, :]
    lag = (pos[:, None] - pos[None, :]).astype(np.float32)
    p["mask_head"] = np.arange(128)[:, None] // HD == np.arange(HH)
    p["lag"] = np.where(same & (lag > 0), lag, 0)
    p["keep"] = -1.0 * (same & (lag > 0))
    p["lag_t"] = np.where(same.T & (lag.T >= 0), lag.T, 0)
    p["keep_t"] = same.T & (lag.T >= 0)
    k = np.tile(np.arange(1, E0 + 1, dtype=np.float32), NT)
    p["inv_k"], p["rank_k"], p["seg_e0"] = rows(1 / k), rows(k), rows(np.float32(k > 1))
    p["ident"] = np.eye(128)
    p["mask_img"] = img[:, None] == np.arange(IPT)
    p["before"] = r[:, None] < r[None, :]
    p["ones"] = np.ones((R, R))
    p["valid"] = np.arange(NT)[None, :] * R + r[:, None] < B * TOK
    p["seg_e"] = rows(np.float32(np.arange(NT * NE) % NE > 0))
    p["seg_t"] = rows(np.float32(np.arange(NT * NE) % NT > 0))
    p["starts"] = rows(128.0 * np.arange(MT))
    p["tile_no"] = rows(1.0 * np.arange(ST))

    def packed(pack):
        at, n = offsets(pack)
        out = np.zeros((128, n), np.float32)
        for name, (a, w) in at.items():
            out[:p[name].shape[0], a:a + w] = p[name]
        return out

    w1 = f["L1_ffn_W1"].reshape(NE, 2, 128, FF).transpose(2, 0, 1, 3).reshape(128, -1)
    w2 = f["L1_ffn_W2"].reshape(NE, FC, 128, D).transpose(2, 0, 1, 3).reshape(128, -1)
    return {"in_x": x_h, "in_pack1": packed(PACK1), "in_pack2": packed(PACK2), "in_packc": packed(PACKC),
            "in_w1": np.ascontiguousarray(w1), "in_w2": np.ascontiguousarray(w2)}


def kernel(**inputs):
    import concourse.bacc as _bacc
    from concourse import mybir as _mybir
    from concourse.bass_utils import run_bass_kernel_spmd as _run

    nc = _bacc.Bacc("TRN2", target_bir_lowering=False, num_devices=1)
    arrays = lay_out(inputs)
    args = [nc.dram_tensor(n, a.shape, _mybir.dt.from_np(a.dtype), kind="ExternalInput").ap() for n, a in arrays.items()]
    args.append(nc.dram_tensor("out_0", (B * TOK, D), F32, kind="ExternalOutput").ap())
    build(nc, *args)
    r = _run(nc, [arrays], core_ids=[0])
    return r.results[0]["out_0"].reshape(B, TOK, D)
```

```python
from contextlib import ExitStack, contextmanager

import concourse.bass as bass
from concourse import mybir

ALU = mybir.AluOpType
ACT = mybir.ActivationFunctionType
F32 = mybir.dt.float32
I32 = mybir.dt.int32
AX_X = mybir.AxisListType.X

B, TOK, D = 64, 37, 256
IPT = 3
R = IPT * TOK
NT = -(-B // IPT)
PAIRS = NT // 2
FP = 768
PC = FP // 128
NH, HD = 16, 16
HH = NH // 2
E0, RK, O0 = 16, 128, 1024
OC = O0 // 128
H1 = 2
NE, FF = 8, 1024
FC = FF // 128
ST = (B * TOK + NE * 127) // 128
EPS = 1e-5
KW = HH * TOK
SPAN = R + TOK
HP = 64
PR = HP + TOK
MT = 19

PACK1 = [("w_lin", PC * D), ("pos", D), ("pos_add", D), ("w_q", 2 * D), ("b_q", D), ("w_k", 2 * 128),
         ("b_k", 1), ("w_v", 2 * HD), ("b_v", HD)]
PACK2 = [("w_o", 2 * D), ("b_o", D), ("proj", 2 * E0), ("w_in1", 2 * RK), ("b_in1", 1), ("c1", RK), ("c2", RK),
         ("w_out1", O0), ("w_in2", OC * RK), ("b_in2", 1), ("w_out2", D), ("w_vb", 2 * (D + H1)),
         ("mask_head", HH), ("mask_pair", 2), ("lag_t", R), ("keep_t", R), ("lag", R), ("keep", R), ("decay", H1),
         ("inv_k", NT * E0), ("rank_k", NT * E0), ("seg_e0", NT * E0)]
PACKC = [("ident", 128), ("mask_img", IPT), ("w_read", 2 * D), ("w_r", 2 * NE), ("b_r", NE), ("before", R),
         ("ones", R), ("valid", NT), ("b1", NE * FC), ("b2", NE * D), ("seg_e", NT * NE), ("seg_t", NE * NT),
         ("starts", MT), ("tile_no", ST)]


def offsets(pack, start=0):
    at, out = 0, {}
    for name, width in pack:
        out[name] = (at, width)
        at += width
    return out, start + -(-(at - start) // PAIRS) * PAIRS


def build(nc, x_h, pack1_h, pack2_h, packc_h, w1_h, w2_h, out_h):
    at1, n1w = offsets(PACK1)
    at2, n2w = offsets(PACK2)
    atc, ncw = offsets(PACKC, 128)

    q_rows = nc.dram_tensor("q_rows", (NT * R, D), F32).ap()
    n_rows = nc.dram_tensor("n_rows", (NT * R, H1 * TOK), F32).ap()
    a_rows = nc.dram_tensor("a_rows", (NT * R, H1 * TOK), F32).ap()
    x_slots = nc.dram_tensor("x_slots", (ST * 128, D), F32).ap()
    y_slots = nc.dram_tensor("y_slots", (ST * 128, D), F32).ap()

    with ExitStack() as top:
        def sb(name, width, dt=F32, rows=128):
            return top.enter_context(nc.sbuf_tensor(name, [rows, width], dt))

        def sem(name):
            return top.enter_context(nc.semaphore(name))

        W1S = NE * 2 * FF
        W2S = NE * FC * D
        arena_w1 = sb("arena_w1", W1S)
        arena_w2 = sb("arena_w2", W2S)
        resid = sb("resid", NT * D)
        keepx = sb("keepx", NT * D)
        cst = sb("cst", ncw)
        work = sb("work", 5632)
        slot_i = sb("slot_i", NT, I32)
        expert_i = sb("expert_i", ST, I32, rows=1)
        gate = sb("gate", NT)
        bank = [top.enter_context(nc.psum_tensor(f"bank{k}", [128, 512], F32)) for k in range(8)]

        def carver(arena, start=0):
            pos = [start]

            def carve(width, rows=128):
                a = pos[0]
                pos[0] += width
                assert pos[0] <= arena.shape[1], (pos[0], arena.shape)
                return arena[0:rows, a:a + width]
            return carve

        def c(name, rows=128):
            a, w = atc[name]
            return cst[0:rows, a:a + w]

        ident = c("ident")
        carve_a = carver(arena_w1)
        pack1 = carve_a(n1w)
        pack2 = carve_a(n2w)

        def p1(name, rows=128):
            a, w = at1[name]
            return pack1[0:rows, a:a + w]

        def p2(name, rows=128):
            a, w = at2[name]
            return pack2[0:rows, a:a + w]

        carve_0 = carver(arena_w2)
        x_t = carve_0(2 * NT * R)
        k_rep = carve_0(NT * R)
        carve_1 = carver(arena_w2, W2S // 2)
        attn_t = carve_1(NT * H1 * R, R)
        sys_n = carve_1(TOK * TOK)
        sys_x = carve_1(TOK * TOK)
        carve_1b = carver(arena_w2, W2S // 2)
        v_rep = carve_1b(NT * IPT * HD, PR)
        gate_t = carve_1b(NT * R, E0)
        lg0 = carve_1b(NT * E0, R)

        zeros = arena_w2[:, W2S - D:W2S]

        in_params = sem("in_params")
        in_qkv = sem("in_qkv")
        in_ident = sem("in_ident")
        in_params2 = sem("in_params2")
        in_cst = sem("in_cst")
        zeros_out = sem("zeros_out")
        w2a_in = sem("w2a_in")
        w2b_in = sem("w2b_in")
        w1_in = sem("w1_in")

        phase_sems = []

        def psem(name):
            phase_sems.append(nc.alloc_semaphore(name=f"p{len(blocks)}_{name}"))
            return phase_sems[-1]

        def pair(name):
            return [psem(f"{name}{j}") for j in range(2)]

        @contextmanager
        def phase():
            with ExitStack() as inner:
                blocks.append(inner)
                yield
            nc.clear_and_free_semaphores(phase_sems)
            nc.all_engine_barrier()
            phase_sems.clear()

        blocks = []

        def enter(block):
            return blocks[-1].enter_context(block)

        def stand_alone(eng):
            eng.wait_ge(in_ident, 16)

        def at(eng, i, shift=0, total=PAIRS):
            if isinstance(i, int):
                return (i + shift, i + shift + 1) if 0 <= i + shift < total else None
            return (eng.snap(i + shift), eng.snap(i + shift + 1))

        def run_turns(eng, turn, ahead=0, behind=0, total=PAIRS):
            for i in range(-ahead, behind + 1):
                turn(i)
            with eng.Fori(behind + 1, total - ahead) as i:
                turn(i)
            for i in range(total - ahead, total + behind):
                turn(i)

        def wait_free(eng, semaphore, n):
            if not (isinstance(n, int) and n == 0):
                eng.wait_ge(semaphore, n)

        ph2_carve = carver(arena_w1, n1w + n2w)
        posb = ph2_carve(D, R)
        qm = [ph2_carve(2 * IPT * SPAN) for _ in range(2)]
        kb = [ph2_carve(IPT * KW) for _ in range(2)]
        vb = [ph2_carve(IPT * 2 * HD, PR) for _ in range(2)]
        xp = [x[:, 0:IPT * PC * TOK] for x in kb]
        wc = carver(work)
        xn = [wc(D, R) for _ in range(2)]
        xt = [wc(2 * R) for _ in range(2)]
        st = [wc(8, R) for _ in range(2)]
        ve = [wc(4, R) for _ in range(2)]
        qn = [wc(D, R) for _ in range(2)]
        small = [wc(3 * NH, R) for _ in range(2)]
        prob = [wc(NH * HP, R) for _ in range(2)]

        def norm_stats(dve, x, j, sems, n1, after):
            s_st, s_ag, s_ve = sems
            stand_alone(dve)
            dve.wait_ge(after[j], n1)
            nc.vector.bn_stats(st[j][:, 0:6], x).then_inc(s_st[j], 1)
            stand_alone(dve)
            dve.wait_ge(s_st[j], n1)
            nc.vector.bn_aggr(st[j][:, 6:8], st[j][:, 0:6]).then_inc(s_ag[j], 1)
            dve.wait_ge(s_ag[j], n1)
            nc.vector.tensor_scalar(ve[j][:, 0:1], st[j][:, 7:8], EPS, None, ALU.add).then_inc(s_ve[j], 1)

        def norm_power(pool, j, s_ve, s_rs, n1):
            pool.wait_ge(s_ve[j], n1)
            nc.gpsimd.tensor_tensor(ve[j][:, 1:2], ve[j][:, 0:1], ve[j][:, 2:3], ALU.pow).then_inc(s_rs[j], 1)

        def norm_apply(out, x, j):
            return nc.vector.tensor_scalar(out, x, st[j][:, 6:7], ve[j][:, 1:2], ALU.subtract, ALU.mult)

        with phase():
            x_in = pair("x_in")
            embedded = pair("embedded")
            summed = pair("summed")
            stats = [pair("st"), pair("ag"), pair("ve")]
            powered = pair("powered")
            normed = pair("normed")
            turned = pair("turned")
            xt_ready = pair("xt_ready")
            q_done = pair("q_done")
            kv_done = pair("kv_done")
            q_out = pair("q_out")
            k_out = pair("k_out")
            v_out = pair("v_out")
            q_stored = pair("q_stored")
            setup = psem("setup")
            pos_ready = psem("pos_ready")
            zero_ready = psem("zero_ready")
            block = enter(nc.Block())

            @block.sync
            def _(sp):
                embed_w = at1["w_q"][0]
                sp.dma_start(pack1[:, 0:embed_w], pack1_h[:, 0:embed_w]).then_inc(in_params, 16)

                def turn(i):
                    for j in range(2):
                        wait_free(sp, embedded[j], i)
                        sp.dma_start(xp[j], x_h[bass.ds(2 * i + j, 1)].rearrange("o p n -> (o p) n")).then_inc(x_in[j], 16)

                run_turns(sp, turn)

            @block.tensor
            def _(pe):
                pe.wait_ge(in_params, 16)
                pe.wait_ge(in_ident, 16)
                pe.wait_ge(in_qkv, 16)
                w_lin = p1("w_lin").rearrange("p (c n) -> p c n", c=PC)
                w_q = p1("w_q").rearrange("p (c n) -> p c n", c=2)
                w_k = p1("w_k").rearrange("p (c n) -> p c n", c=2)
                w_v = p1("w_v").rearrange("p (c n) -> p c n", c=2)

                def embed(pair_at, j):
                    if pair_at is None:
                        return
                    i, n1 = pair_at
                    pe.wait_ge(x_in[j], 16 * n1)
                    wait_free(pe, summed[j], i)
                    for k in range(PC):
                        mm = nc.tensor.matmul(bank[j][0:R, 0:D], xp[j][:, k * R:(k + 1) * R], w_lin[:, k, :],
                                              start=(k == 0), stop=(k == PC - 1))
                    mm.then_inc(embedded[j], 1)

                def turn_rows(pair_at, j):
                    if pair_at is None:
                        return
                    i, n1 = pair_at
                    pe.wait_ge(normed[j], n1)
                    wait_free(pe, xt_ready[j], i)
                    for k in range(2):
                        mm = nc.tensor.transpose(bank[2 + j][:, k * R:(k + 1) * R], xn[j][:, k * 128:(k + 1) * 128],
                                                 ident[0:R, 0:R])
                    mm.then_inc(turned[j], 1)

                def queries_keys_values(pair_at, j):
                    if pair_at is None:
                        return
                    i, n1 = pair_at
                    pe.wait_ge(xt_ready[j], n1)
                    wait_free(pe, q_out[j], i)
                    for k in range(2):
                        mm = nc.tensor.matmul(bank[4 + j][0:R, 0:D], xt[j][:, k * R:(k + 1) * R], w_q[:, k, :],
                                              start=(k == 0), stop=(k == 1))
                    mm.then_inc(q_done[j], 1)
                    wait_free(pe, k_out[j], i)
                    wait_free(pe, v_out[j], 2 * i)
                    for k in range(2):
                        nc.tensor.matmul(bank[6 + j][:, 0:R], w_k[:, k, :], xt[j][:, k * R:(k + 1) * R],
                                         start=(k == 0), stop=(k == 1))
                    for lo in (0, HP):
                        for m in range(IPT):
                            for k in range(2):
                                a = k * R + m * TOK
                                mm = nc.tensor.matmul(bank[6 + j][lo:lo + TOK, R + m * HD:R + (m + 1) * HD],
                                                      xt[j][:, a:a + TOK], w_v[:, k, :], start=(k == 0), stop=(k == 1))
                    mm.then_inc(kv_done[j], 1)

                def turn(i):
                    last, this = at(pe, i, -1), at(pe, i)
                    embed(this, 0)
                    turn_rows(last, 1)
                    queries_keys_values(last, 0)
                    embed(this, 1)
                    turn_rows(this, 0)
                    queries_keys_values(last, 1)

                run_turns(pe, turn, behind=1)

            @block.vector
            def _(dve):
                dve.wait_ge(in_params, 16)
                dve.wait_ge(in_qkv, 16)
                nc.vector.tensor_tensor(posb, p1("pos", R), p1("pos_add", R), ALU.add).then_inc(pos_ready, 1)
                for j in range(2):
                    nc.vector.memset(ve[j][:, 2:3], -0.5).then_inc(setup, 1)
                dve.wait_ge(pos_ready, 1)

                def add_and_norm(pair_at, j):
                    if pair_at is None:
                        return
                    i, n1 = pair_at
                    h = resid[0:R, bass.ds((2 * i + j) * D, D)]
                    dve.wait_ge(embedded[j], n1)
                    nc.vector.tensor_tensor(h, bank[j][0:R, 0:D], posb, ALU.add).then_inc(summed[j], 1)
                    norm_stats(dve, h, j, stats, n1, summed)
                    dve.wait_ge(powered[j], n1)
                    wait_free(dve, turned[j], i)
                    norm_apply(xn[j], h, j).then_inc(normed[j], 1)

                def queries_keys_values(pair_at, j):
                    if pair_at is None:
                        return
                    i, n1 = pair_at
                    dve.wait_ge(q_done[j], n1)
                    wait_free(dve, q_stored[j], 16 * i)
                    nc.vector.tensor_tensor(qn[j], bank[4 + j][0:R, 0:D], p1("b_q", R), ALU.add).then_inc(q_out[j], 1)
                    dve.wait_ge(kv_done[j], n1)
                    nc.vector.tensor_scalar(k_rep[:, bass.ds((2 * i + j) * R, R)], bank[6 + j][:, 0:R],
                                            p1("b_k"), None, ALU.add).then_inc(k_out[j], 1)
                    for lo in (0, HP):
                        rows = slice(lo, lo + TOK)
                        nc.vector.tensor_tensor(
                            v_rep[rows, bass.ds((2 * i + j) * IPT * HD, IPT * HD)].rearrange("p (m d) -> p m d", m=IPT),
                            bank[6 + j][rows, R:R + IPT * HD].rearrange("p (m d) -> p m d", m=IPT),
                            p1("b_v")[rows, :].unsqueeze(1).broadcast_to([TOK, IPT, HD]), ALU.add).then_inc(v_out[j], 1)

                def turn(i):
                    last, this = at(dve, i, -1), at(dve, i)
                    add_and_norm(this, 0)
                    queries_keys_values(last, 0)
                    add_and_norm(this, 1)
                    queries_keys_values(last, 1)

                dve.wait_ge(zero_ready, 6)
                run_turns(dve, turn, behind=1)

            @block.scalar
            def _(act):
                embed_w = at1["w_q"][0]
                act.dma_start(ident, packc_h[:, 0:128]).then_inc(in_ident, 16)
                act.dma_start(pack1[:, embed_w:], pack1_h[:, embed_w:]).then_inc(in_qkv, 16)

                def copy_rows(pair_at, j):
                    if pair_at is None:
                        return
                    i, n1 = pair_at
                    act.wait_ge(turned[j], n1)
                    wait_free(act, kv_done[j], i)
                    nc.scalar.copy(xt[j], bank[2 + j][:, 0:2 * R]).then_inc(xt_ready[j], 1)

                def turn(i):
                    for part, source, arrived in ((pack2, pack2_h, in_params2), (cst[:, 128:], packc_h[:, 128:], in_cst)):
                        w = part.shape[1] // PAIRS
                        act.dma_start(part[:, bass.ds(i * w, w)], source[:, bass.ds(i * w, w)]).then_inc(arrived, 16)
                    for j in range(2):
                        copy_rows(at(act, i), j)

                run_turns(act, turn)

            @block.gpsimd
            def _(pool):
                nc.gpsimd.memset(v_rep[:, :], 0.0).then_inc(zero_ready, 1)
                nc.gpsimd.memset(zeros, 0.0).then_inc(zero_ready, 1)
                for j in range(2):
                    nc.gpsimd.memset(qm[j], 0.0).then_inc(zero_ready, 1)
                for j in range(2):
                    nc.gpsimd.memset(prob[j], 0.0).then_inc(zero_ready, 1)
                pool.wait_ge(setup, 2)

                def turn(i):
                    last, this = at(pool, i, -1), at(pool, i)
                    for j in range(2):
                        if this is not None:
                            norm_power(pool, j, stats[2], powered, this[1])
                        if last is not None:
                            pool.wait_ge(q_out[j], last[1])
                            pool.dma_start(q_rows[bass.ds((2 * last[0] + j) * R, R), :], qn[j]).then_inc(q_stored[j], 16)

                run_turns(pool, turn, behind=1)
                for j in range(2):
                    pool.wait_ge(q_stored[j], 16 * PAIRS)
                pool.wait_ge(zero_ready, 6)

        with phase():
            pt = [wc(HH * R, PR) for _ in range(2)]
            q_in = pair("q_in")
            q_turned = pair("q_turned")
            q_masked = pair("q_masked")
            k_block = pair("k_block")
            v_block = pair("v_block")
            with_bo = pair("with_bo")
            scored = pair("scored")
            maxed = pair("maxed")
            shifted = pair("shifted")
            exped = pair("exped")
            row_sum = pair("row_sum")
            row_inv = pair("row_inv")
            scaled = pair("scaled")
            p_turned = [pair(f"p_turned{half}_") for half in range(2)]
            p_copied = [pair(f"p_copied{half}_") for half in range(2)]
            mixed_v = pair("mixed_v")
            o_copied = pair("o_copied")
            projected = pair("projected")
            added = pair("added")
            stats = [pair("st"), pair("ag"), pair("ve")]
            powered = pair("powered")
            normed = pair("normed")
            turned = pair("turned")
            xt_ready = pair("xt_ready")
            x_saved = pair("x_saved")
            logits = pair("logits")
            logits_out = pair("logits_out")
            ot = [q[:, 0:2 * R] for q in (ph2_carve(2 * R), ph2_carve(2 * R))]
            hbo = [ph2_carve(D, R) for _ in range(2)]
            block = enter(nc.Block())

            def by_head(ap, heads=HH):
                return ap.rearrange("p (h s) -> p h s", h=heads)[:, :, 0:TOK]

            @block.sync
            def _(sp):
                def turn(i):
                    for j in range(2):
                        wait_free(sp, q_turned[j], i)
                        for m in range(IPT):
                            src = q_rows[bass.ds((2 * i + j) * R + m * TOK, TOK), :].rearrange("t (g d) -> (t g) d", d=HD)
                            sp.dma_start(qn[j][m * TOK:(m + 1) * TOK, :].rearrange("t (h d) -> t h d", d=HD),
                                         src.rearrange("(h t) d -> t h d", h=NH)).then_inc(q_in[j], 16)

                run_turns(sp, turn)

            @block.tensor
            def _(pe):
                pe.wait_ge(in_params2, 16 * PAIRS)
                w_o = p2("w_o").rearrange("p (c n) -> p c n", c=2)
                proj = p2("proj").rearrange("p (c n) -> p c n", c=2)

                def turn_queries(pair_at, j):
                    if pair_at is None:
                        return
                    i, n1 = pair_at
                    pe.wait_ge(q_in[j], 16 * IPT * n1)
                    if j:
                        pe.wait_ge(q_masked[0], n1)
                    else:
                        wait_free(pe, q_masked[1], i)
                    for k in range(2):
                        mm = nc.tensor.transpose(bank[6][:, k * R:(k + 1) * R], qn[j][:, k * 128:(k + 1) * 128],
                                                 ident[0:R, 0:R])
                    mm.then_inc(q_turned[j], 1)

                def scores(pair_at, j):
                    if pair_at is None:
                        return
                    i, n1 = pair_at
                    pe.wait_ge(q_masked[j], n1)
                    pe.wait_ge(k_block[j], n1)
                    wait_free(pe, shifted[j], i)
                    for half in range(2):
                        for m in range(IPT):
                            a = half * IPT * SPAN + m * R
                            mm = nc.tensor.matmul(by_head(bank[2 * j + half][0:R, :]), qm[j][:, a:a + R],
                                                  kb[j][:, m * KW:(m + 1) * KW].rearrange("p (h s) -> p h s", h=HH),
                                                  start=(m == 0), stop=(m == IPT - 1))
                    mm.then_inc(scored[j], 1)

                def turn_probs(pair_at, j):
                    if pair_at is None:
                        return
                    i, n1 = pair_at
                    pe.wait_ge(scaled[j], n1)
                    for half in range(2):
                        last = (o_copied, added)[half]
                        if j:
                            pe.wait_ge(last[0], n1)
                        else:
                            wait_free(pe, last[1], i)
                        for k in range(HH // 2):
                            a = (half * HH + 2 * k) * HP
                            mm = nc.tensor.transpose(bank[4 + half][0:PR, k * R:(k + 1) * R], prob[j][:, a:a + PR],
                                                     ident[0:R, 0:R])
                        mm.then_inc(p_turned[half][j], 1)

                def mix_values(pair_at, j):
                    if pair_at is None:
                        return
                    i, n1 = pair_at
                    pe.wait_ge(v_block[j], n1)
                    for half in range(2):
                        pe.wait_ge(p_copied[half][j], n1)
                        for m in range(IPT):
                            for k in range(HH // 2):
                                a = (half * HH // 2 + k) * R + m * TOK
                                mm = nc.tensor.matmul(
                                    bank[4][32 * k:32 * (k + 1), half * R + m * TOK:half * R + (m + 1) * TOK],
                                    vb[j][:, m * 32:(m + 1) * 32], pt[j][:, a:a + TOK], start=True, stop=True)
                    mm.then_inc(mixed_v[j], 1)

                def project(pair_at, j):
                    if pair_at is None:
                        return
                    i, n1 = pair_at
                    pe.wait_ge(o_copied[j], n1)
                    for k in range(2):
                        mm = nc.tensor.matmul(bank[5][0:R, 0:D], ot[j][:, k * R:(k + 1) * R],
                                              w_o[:, k, :], start=(k == 0), stop=(k == 1))
                    mm.then_inc(projected[j], 1)

                def turn_rows(pair_at, j):
                    if pair_at is None:
                        return
                    i, n1 = pair_at
                    pe.wait_ge(normed[j], n1)
                    if j:
                        pe.wait_ge(logits_out[0], n1)
                    else:
                        wait_free(pe, logits_out[1], i)
                    for k in range(2):
                        mm = nc.tensor.transpose(bank[7][:, k * R:(k + 1) * R], xn[j][:, k * 128:(k + 1) * 128],
                                                 ident[0:R, 0:R])
                    mm.then_inc(turned[j], 1)

                def gate_logits(pair_at, j):
                    if pair_at is None:
                        return
                    i, n1 = pair_at
                    pe.wait_ge(xt_ready[j], n1)
                    for k in range(2):
                        mm = nc.tensor.matmul(bank[7][0:R, 2 * R:2 * R + E0], xt[j][:, k * R:(k + 1) * R],
                                              proj[:, k, :], start=(k == 0), stop=(k == 1))
                    mm.then_inc(logits[j], 1)

                def turn(i):
                    last, this, following = at(pe, i, -1), at(pe, i), at(pe, i, 1)
                    scores(this, 0)
                    turn_probs(last, 1)
                    turn_queries(this, 1)
                    turn_rows(last, 0)
                    mix_values(last, 1)
                    gate_logits(last, 0)
                    project(last, 1)
                    scores(this, 1)
                    turn_probs(this, 0)
                    turn_queries(following, 0)
                    turn_rows(last, 1)
                    mix_values(this, 0)
                    gate_logits(last, 1)
                    project(this, 0)

                run_turns(pe, turn, ahead=1, behind=1)

            @block.vector
            def _(dve):
                def shift_scores(pair_at, j):
                    if pair_at is None:
                        return
                    i, n1 = pair_at
                    dve.wait_ge(scored[j], n1)
                    for half in range(2):
                        mx = nc.vector.tensor_reduce(small[j][:, half * HH:(half + 1) * HH],
                                                     by_head(bank[2 * j + half][0:R, :]), AX_X, ALU.max)
                    mx.then_inc(maxed[j], 1)
                    dve.wait_ge(maxed[j], n1)
                    for half in range(2):
                        sub = nc.vector.tensor_tensor(
                            by_head(prob[j][:, half * HH * HP:(half + 1) * HH * HP]), by_head(bank[2 * j + half][0:R, :]),
                            small[j][:, half * HH:(half + 1) * HH].unsqueeze(2).broadcast_to([R, HH, TOK]), ALU.subtract)
                    sub.then_inc(shifted[j], 1)

                def sum_probs(pair_at, j):
                    if pair_at is None:
                        return
                    i, n1 = pair_at
                    dve.wait_ge(exped[j], n1)
                    nc.vector.tensor_reduce(small[j][:, NH:2 * NH], by_head(prob[j], NH), AX_X,
                                            ALU.add).then_inc(row_sum[j], 1)
                    dve.wait_ge(row_sum[j], n1)
                    nc.vector.reciprocal(small[j][:, 2 * NH:3 * NH], small[j][:, NH:2 * NH]).then_inc(row_inv[j], 1)

                def add_and_norm(pair_at, j):
                    if pair_at is None:
                        return
                    i, n1 = pair_at
                    h = resid[0:R, bass.ds((2 * i + j) * D, D)]
                    dve.wait_ge(projected[j], n1)
                    dve.wait_ge(with_bo[j], n1)
                    nc.vector.tensor_tensor(h, bank[5][0:R, 0:D], hbo[j], ALU.add).then_inc(added[j], 1)
                    norm_stats(dve, h, j, stats, n1, added)
                    dve.wait_ge(powered[j], n1)
                    norm_apply(xn[j], h, j).then_inc(normed[j], 1)

                def keep_logits(pair_at, j):
                    if pair_at is None:
                        return
                    i, n1 = pair_at
                    dve.wait_ge(logits[j], n1)
                    nc.vector.tensor_copy(lg0[:, bass.ds((2 * i + j) * E0, E0)],
                                          bank[7][0:R, 2 * R:2 * R + E0]).then_inc(logits_out[j], 1)

                def turn(i):
                    last, this = at(dve, i, -1), at(dve, i)
                    shift_scores(this, 0)
                    sum_probs(this, 0)
                    keep_logits(last, 0)
                    add_and_norm(last, 1)
                    shift_scores(this, 1)
                    sum_probs(this, 1)
                    keep_logits(last, 1)
                    add_and_norm(this, 0)

                run_turns(dve, turn, behind=1)

            @block.scalar
            def _(act):
                def copy_probs(pair_at, j):
                    if pair_at is None:
                        return
                    i, n1 = pair_at
                    for half in range(2):
                        act.wait_ge(p_turned[half][j], n1)
                        wait_free(act, mixed_v[j], i)
                        nc.scalar.copy(pt[j][:, half * HH // 2 * R:(half + 1) * HH // 2 * R],
                                       bank[4 + half][0:PR, 0:HH // 2 * R]).then_inc(p_copied[half][j], 1)

                def mask_queries(pair_at, j):
                    if pair_at is None:
                        return
                    i, n1 = pair_at
                    act.wait_ge(q_turned[j], n1)
                    wait_free(act, scored[j], i)
                    nc.scalar.mul(qm[j].rearrange("p (c m w) -> p c m w", c=2, m=IPT)[:, :, :, 0:TOK],
                                  bank[6][:, 0:2 * R].rearrange("p (c m t) -> p c m t", c=2, m=IPT),
                                  HD ** -0.5).then_inc(q_masked[j], 1)

                def exponentials(pair_at, j):
                    if pair_at is None:
                        return
                    i, n1 = pair_at
                    act.wait_ge(shifted[j], n1)
                    nc.scalar.activation(by_head(prob[j], NH), by_head(prob[j], NH), ACT.Exp).then_inc(exped[j], 1)

                def copy_output(pair_at, j):
                    if pair_at is None:
                        return
                    i, n1 = pair_at
                    act.wait_ge(mixed_v[j], n1)
                    wait_free(act, projected[j], i)
                    nc.scalar.copy(ot[j], bank[4][:, 0:2 * R]).then_inc(o_copied[j], 1)

                def copy_rows(pair_at, j):
                    if pair_at is None:
                        return
                    i, n1 = pair_at
                    act.wait_ge(turned[j], n1)
                    wait_free(act, x_saved[j], i)
                    nc.scalar.copy(xt[j], bank[7][:, 0:2 * R]).then_inc(xt_ready[j], 1)

                def turn(i):
                    last, this, following = at(act, i, -1), at(act, i), at(act, i, 1)
                    copy_probs(last, 1)
                    mask_queries(this, 1)
                    exponentials(this, 0)
                    copy_rows(last, 0)
                    copy_output(last, 1)
                    copy_probs(this, 0)
                    mask_queries(following, 0)
                    exponentials(this, 1)
                    copy_rows(last, 1)
                    copy_output(this, 0)

                run_turns(act, turn, ahead=1, behind=1)

            @block.gpsimd
            def _(pool):
                pool.wait_ge(in_params2, 16 * PAIRS)

                def spread_keys(pair_at, j):
                    if pair_at is None:
                        return
                    i, n1 = pair_at
                    wait_free(pool, scored[j], i)
                    nc.gpsimd.tensor_tensor(
                        kb[j].rearrange("p (m h s) -> p m h s", m=IPT, h=HH),
                        k_rep[:, bass.ds((2 * i + j) * R, R)].rearrange("p (m s) -> p m s", m=IPT).unsqueeze(2)
                        .broadcast_to([128, IPT, HH, TOK]),
                        p2("mask_head").unsqueeze(1).unsqueeze(3).broadcast_to([128, IPT, HH, TOK]),
                        ALU.mult).then_inc(k_block[j], 1)

                def spread_values(pair_at, j):
                    if pair_at is None:
                        return
                    i, n1 = pair_at
                    wait_free(pool, mixed_v[j], i)
                    nc.gpsimd.tensor_tensor(
                        vb[j].rearrange("p (m h d) -> p m h d", m=IPT, h=2),
                        v_rep[:, bass.ds((2 * i + j) * IPT * HD, IPT * HD)].rearrange("p (m d) -> p m d", m=IPT)
                        .unsqueeze(2).broadcast_to([PR, IPT, 2, HD]),
                        p2("mask_pair", PR).unsqueeze(1).unsqueeze(3).broadcast_to([PR, IPT, 2, HD]),
                        ALU.mult).then_inc(v_block[j], 1)
                    wait_free(pool, added[j], i)
                    nc.gpsimd.tensor_tensor(hbo[j], resid[0:R, bass.ds((2 * i + j) * D, D)], p2("b_o", R),
                                            ALU.add).then_inc(with_bo[j], 1)

                def scale_probs(pair_at, j):
                    if pair_at is None:
                        return
                    i, n1 = pair_at
                    pool.wait_ge(row_inv[j], n1)
                    nc.gpsimd.tensor_tensor(
                        by_head(prob[j], NH), by_head(prob[j], NH),
                        small[j][:, 2 * NH:3 * NH].unsqueeze(2).broadcast_to([R, NH, TOK]), ALU.mult).then_inc(scaled[j], 1)

                def save_rows(pair_at, j):
                    if pair_at is None:
                        return
                    i, n1 = pair_at
                    stand_alone(pool)
                    pool.wait_ge(xt_ready[j], n1)
                    nc.gpsimd.tensor_copy(
                        x_t.rearrange("p (k n) -> p k n", k=2)[:, :, bass.ds((2 * i + j) * R, R)],
                        xt[j].rearrange("p (k n) -> p k n", k=2)).then_inc(x_saved[j], 1)

                def power(pair_at, j):
                    if pair_at is not None:
                        norm_power(pool, j, stats[2], powered, pair_at[1])

                def turn(i):
                    last, this, following = at(pool, i, -1), at(pool, i), at(pool, i, 1)
                    spread_keys(this, 1)
                    spread_values(this, 0)
                    scale_probs(this, 0)
                    save_rows(last, 0)
                    power(last, 1)
                    spread_keys(following, 0)
                    spread_values(this, 1)
                    scale_probs(this, 1)
                    save_rows(last, 1)
                    power(this, 0)

                run_turns(pool, turn, ahead=1, behind=1)

        with phase():
            chain = psem("chain")
            var_ready = psem("var_ready")
            std_ready = psem("std_ready")
            delta_ready = psem("delta_ready")
            root_ready = psem("root_ready")
            gates_ready = psem("gates_ready")
            gates_turned = psem("gates_turned")
            gates_stored = psem("gates_stored")
            NG = NT * E0
            ec = carver(arena_w1, n1w + n2w)
            z, zs, zr, s1, s2, t1 = (ec(NG, R) for _ in range(6))
            m1, m2 = ec(NT, R), ec(NT, R)
            block = enter(nc.Block())

            def grp(ap):
                return ap.rearrange("p (t e) -> p t e", t=NT)

            def wide(ap):
                return ap.unsqueeze(2).broadcast_to([R, NT, E0])

            @block.vector
            def _(dve):
                count = [0]

                def link(ins):
                    count[0] += 1
                    ins.then_inc(chain, 1)
                    dve.wait_ge(chain, count[0])

                tt, ts, red = nc.vector.tensor_tensor, nc.vector.tensor_scalar, nc.vector.tensor_reduce
                link(red(m1, grp(lg0), AX_X, ALU.add))
                link(ts(m2, m1, 1.0 / E0, None, ALU.mult))
                link(tt(grp(z), grp(lg0), wide(m2), ALU.subtract))
                link(tt(t1, z, z, ALU.mult))
                link(red(m1, grp(t1), AX_X, ALU.add))
                ts(m2, m1, 1.0 / E0, EPS, ALU.mult, ALU.add).then_inc(var_ready, 1)
                dve.wait_ge(std_ready, 1)
                link(nc.vector.reciprocal(m2, m1))
                link(tt(grp(z), grp(z), wide(m2), ALU.mult))
                link(red(m1, grp(z), AX_X, ALU.max))
                link(tt(grp(t1), grp(z), wide(m1), ALU.subtract))
                link(ts(z, t1, 0.5, None, ALU.mult))
                for t in range(NT):
                    last = nc.vector.max(zs[:, t * E0:t * E0 + 8], z[:, t * E0:(t + 1) * E0])
                link(last)
                for t in range(NT):
                    last = nc.vector.match_replace(zr[:, t * E0:(t + 1) * E0], zs[:, t * E0:t * E0 + 8],
                                                   z[:, t * E0:(t + 1) * E0], -1e30)
                link(last)
                for t in range(NT):
                    last = nc.vector.max(zs[:, t * E0 + 8:(t + 1) * E0], zr[:, t * E0:(t + 1) * E0])
                link(last)
                link(tt(t1, zs, zs, ALU.mult))
                link(nc.vector.tensor_tensor_scan(s1, p2("seg_e0", R), zs, 0.0, ALU.mult, ALU.add))
                link(nc.vector.tensor_tensor_scan(s2, p2("seg_e0", R), t1, 0.0, ALU.mult, ALU.add))
                link(tt(s1, s1, p2("inv_k", R), ALU.mult))
                link(tt(s2, s2, p2("inv_k", R), ALU.mult))
                link(tt(t1, s1, s1, ALU.mult))
                link(tt(s2, s2, t1, ALU.subtract))
                link(tt(t1, p2("inv_k", R), s2, ALU.subtract))
                ts(s2, t1, 0.0, None, ALU.max).then_inc(delta_ready, 1)
                dve.wait_ge(root_ready, 1)
                link(tt(s1, s1, t1, ALU.subtract))
                link(tt(t1, s1, zs, ALU.is_le))
                link(red(m1, grp(t1), AX_X, ALU.add))
                link(tt(grp(t1), grp(p2("rank_k", R)), wide(m1), ALU.is_equal))
                link(tt(t1, t1, s1, ALU.mult))
                link(red(m1, grp(t1), AX_X, ALU.add))
                link(tt(grp(t1), grp(z), wide(m1), ALU.subtract))
                nc.vector.scalar_tensor_tensor(z, t1, 0.0, t1, ALU.max, ALU.mult).then_inc(gates_ready, 1)
                for b in range(-(-NT // 4)):
                    n = min(4, NT - 4 * b)
                    dve.wait_ge(gates_turned, b + 1)
                    nc.vector.tensor_copy(gate_t[:, 4 * b * R:(4 * b + n) * R], bank[b][0:E0, 0:n * R]).then_inc(gates_stored, 1)

            @block.scalar
            def _(act):
                act.wait_ge(var_ready, 1)
                nc.scalar.activation(m1, m2, ACT.Sqrt).then_inc(std_ready, 1)
                act.wait_ge(delta_ready, 1)
                nc.scalar.activation(t1, s2, ACT.Sqrt).then_inc(root_ready, 1)

            @block.tensor
            def _(pe):
                pe.wait_ge(gates_ready, 1)
                for b in range(-(-NT // 4)):
                    n = min(4, NT - 4 * b)
                    for k in range(n):
                        t = 4 * b + k
                        mm = nc.tensor.transpose(bank[b][0:E0, k * R:(k + 1) * R], z[:, t * E0:(t + 1) * E0], ident[0:R, 0:R])
                    mm.then_inc(gates_turned, 1)

        with phase():
            z1_done, z1_gated, hid_done, hid_act, z2_done, z2_gated, y_done, y_added = (
                psem(n) for n in ("z1_done", "z1_gated", "hid_done", "hid_act", "z2_done", "z2_gated", "y_done", "y_added"))
            g1_out = psem("g1_out")
            g_out = psem("g_out")
            W = 2 * R
            bc = carver(arena_w1, n1w + n2w)
            z1 = bc(W)
            z2 = bc(W)
            g1 = bc(W)
            g2 = bc(W)
            hid = bc(OC * W)
            block = enter(nc.Block())

            @block.tensor
            def _(pe):
                w_in1 = p2("w_in1").rearrange("p (c n) -> p c n", c=2)
                w_out1 = p2("w_out1").rearrange("p (c n) -> p c n", c=OC)
                w_in2 = p2("w_in2").rearrange("p (c n) -> p c n", c=OC)

                def first_products(pair_at):
                    if pair_at is None:
                        return
                    i, n1 = pair_at
                    tok = i * W if isinstance(i, int) else pe.snap(i * W)
                    wait_free(pe, z1_gated, i)
                    wait_free(pe, g_out, i)
                    for g, name in enumerate(("c1", "c2")):
                        nc.tensor.matmul(bank[6][:, g * W:(g + 1) * W], p2(name, E0), gate_t[:, bass.ds(tok, W)],
                                         start=True, stop=True)
                    for k in range(2):
                        mm = nc.tensor.matmul(bank[0][:, 0:W], w_in1[:, k, :], x_t[:, bass.ds(tok + k * NT * R, W)],
                                              start=(k == 0), stop=(k == 1))
                    mm.then_inc(z1_done, 1)

                def hidden(pair_at):
                    if pair_at is None:
                        return
                    i, n1 = pair_at
                    pe.wait_ge(z1_gated, n1)
                    wait_free(pe, hid_act, i * (OC // 2))
                    for f in range(OC):
                        mm = nc.tensor.matmul(bank[2 + f // 2][:, (f % 2) * W:(f % 2 + 1) * W], w_out1[:, f, :], z1,
                                              start=True, stop=True)
                        if f % 2:
                            mm.then_inc(hid_done, 1)

                def second_products(pair_at):
                    if pair_at is None:
                        return
                    i, n1 = pair_at
                    wait_free(pe, z2_gated, i)
                    for f in range(OC):
                        if f % 2 == 0:
                            pe.wait_ge(hid_act, i * (OC // 2) + f // 2 + 1)
                        mm = nc.tensor.matmul(bank[1][:, 0:W], w_in2[:, f, :], hid[:, f * W:(f + 1) * W],
                                              start=(f == 0), stop=(f == OC - 1))
                    mm.then_inc(z2_done, 1)

                def outputs(pair_at):
                    if pair_at is None:
                        return
                    i, n1 = pair_at
                    pe.wait_ge(z2_gated, n1)
                    wait_free(pe, y_added, i)
                    for j in range(2):
                        mm = nc.tensor.matmul(bank[7][0:R, j * D:(j + 1) * D], z2[:, j * R:(j + 1) * R], p2("w_out2"),
                                              start=True, stop=True)
                    mm.then_inc(y_done, 1)

                def turn(i):
                    last, this = at(pe, i, -1), at(pe, i)
                    first_products(this)
                    second_products(last)
                    hidden(this)
                    outputs(last)

                run_turns(pe, turn, behind=1)

            @block.vector
            def _(dve):
                def gate_first(pair_at):
                    if pair_at is None:
                        return
                    i, n1 = pair_at
                    dve.wait_ge(z1_done, n1)
                    nc.vector.tensor_copy(g1, bank[6][:, 0:W]).then_inc(g1_out, 1)
                    dve.wait_ge(g1_out, n1)
                    wait_free(dve, hid_done, i * (OC // 2))
                    nc.vector.scalar_tensor_tensor(z1, bank[0][:, 0:W], p2("b_in1"), g1,
                                                   ALU.add, ALU.mult).then_inc(z1_gated, 1)

                def keep_second_gates(pair_at):
                    if pair_at is None:
                        return
                    i, n1 = pair_at
                    wait_free(dve, z2_gated, i)
                    nc.vector.tensor_copy(g2, bank[6][:, W:2 * W]).then_inc(g_out, 1)

                def gate_second(pair_at):
                    if pair_at is None:
                        return
                    i, n1 = pair_at
                    dve.wait_ge(z2_done, n1)
                    dve.wait_ge(g_out, n1)
                    wait_free(dve, y_done, i)
                    nc.vector.scalar_tensor_tensor(z2, bank[1][:, 0:W], p2("b_in2"), g2,
                                                   ALU.add, ALU.mult).then_inc(z2_gated, 1)

                def add_outputs(pair_at):
                    if pair_at is None:
                        return
                    i, n1 = pair_at
                    dve.wait_ge(y_done, n1)
                    h = resid[0:R, bass.ds(i * 2 * D, 2 * D)]
                    nc.vector.tensor_tensor(h, h, bank[7][0:R, 0:2 * D], ALU.add).then_inc(y_added, 1)

                def turn(i):
                    last, this = at(dve, i, -1), at(dve, i)
                    gate_first(this)
                    gate_second(last)
                    keep_second_gates(this)
                    add_outputs(last)

                run_turns(dve, turn, behind=1)

            @block.sync
            def _(sp):
                sp.dma_start(x_slots.rearrange("(s p) d -> p s d", p=128),
                             zeros.unsqueeze(1).broadcast_to([128, ST, D])).then_inc(zeros_out, 16)
                sp.dma_start(a_rows[B * TOK:, :], zeros[0:NT * R - B * TOK, 0:H1 * TOK]).then_inc(zeros_out, 16)
                sp.wait_ge(zeros_out, 32)

            @block.scalar
            def _(act):
                def turn(i):
                    wait_free(act, z2_done, i)
                    for f in range(OC // 2):
                        act.wait_ge(hid_done, i * (OC // 2) + f + 1)
                        nc.scalar.activation(hid[:, 2 * f * W:2 * (f + 1) * W], bank[2 + f][:, 0:2 * W],
                                             ACT.Gelu).then_inc(hid_act, 1)

                run_turns(act, turn)

        with phase():
            stats = [pair("st"), pair("ag"), pair("ve")]
            (powered, normed, sq_done, roots, rooted, floored, inverted, k_ready, turned, t_ready, v_done, g_done, beta_out,
             v_out, at_out, n_masked, n_reduced, n_scaled, n_stored) = (
                pair(n) for n in ("powered", "normed", "sq_done", "roots", "rooted", "floored", "inverted", "k_ready",
                                      "turned", "t_ready", "v_done", "g_done", "beta_out", "v_out", "at_out", "n_masked",
                                      "n_reduced", "n_scaled", "n_stored"))
            rows_free = pair("rows_free")
            tables = psem("tables")
            chain = psem("chain")
            cc = carver(arena_w1, n1w + n2w)
            lt, ln = cc(H1 * R, R), cc(H1 * R, R)
            dec = cc(8, R)
            kn = [cc(D, R) for _ in range(2)]
            xk = [cc(4 * R) for _ in range(2)]
            sq = [cc(D, R) for _ in range(2)]
            nf = [cc(H1 * R, R) for _ in range(2)]
            nk = [cc(H1 * TOK, R) for _ in range(2)]
            nb = [cc(H1 * TOK, R) for _ in range(2)]
            sc = [cc(12, R) for _ in range(2)]
            block = enter(nc.Block())

            @block.sync
            def _(sp):
                sp.dma_start(arena_w2[:, 0:W2S // 2], w2_h[:, 0:W2S // 2]).then_inc(w2a_in, 16)

                def turn(i):
                    for j in range(2):
                        sp.wait_ge(n_scaled[j], i + 1)
                        sp.dma_start(n_rows[bass.ds((2 * i + j) * R, R), :], nb[j]).then_inc(n_stored[j], 16)

                run_turns(sp, turn)
                for j in range(2):
                    sp.wait_ge(n_stored[j], 16 * PAIRS)

            @block.tensor
            def _(pe):
                w_vb = p2("w_vb").rearrange("p (c n) -> p c n", c=2)

                def products(pair_at, j):
                    if pair_at is None:
                        return
                    i, n1 = pair_at
                    pe.wait_ge(t_ready[j], n1)
                    wait_free(pe, v_out[j], i)
                    wait_free(pe, n_masked[j], i)
                    for k in range(2):
                        mm = nc.tensor.matmul(bank[2 + j][0:R, 0:D + H1], xk[j][:, k * R:(k + 1) * R], w_vb[:, k, :],
                                              start=(k == 0), stop=(k == 1))
                    mm.then_inc(v_done[j], 1)
                    for h in range(H1):
                        kt = xk[j][:, (2 + h) * R:(3 + h) * R]
                        mm = nc.tensor.matmul(bank[4 + j][0:R, h * R:(h + 1) * R], kt, kt, start=True, stop=True)
                    mm.then_inc(g_done[j], 1)

                def turn_rows_and_keys(pair_at, j):
                    if pair_at is None:
                        return
                    i, n1 = pair_at
                    pe.wait_ge(normed[j], n1)
                    pe.wait_ge(k_ready[j], n1)
                    wait_free(pe, t_ready[j], i)
                    for k in range(4):
                        src = (xn, kn)[k // 2][j][:, (k % 2) * 128:(k % 2 + 1) * 128]
                        mm = nc.tensor.transpose(bank[j][:, k * R:(k + 1) * R], src, ident[0:R, 0:R])
                    mm.then_inc(turned[j], 1)

                def turn(i):
                    last, this = at(pe, i, -1), at(pe, i)
                    products(last, 0)
                    turn_rows_and_keys(last, 1)
                    products(last, 1)
                    turn_rows_and_keys(this, 0)

                run_turns(pe, turn, behind=1)

            @block.scalar
            def _(act):
                act.wait_ge(tables, 1)
                nc.scalar.activation(dec[:, 0:H1], p2("decay", R), ACT.Sigmoid).then_inc(chain, 1)
                act.wait_ge(chain, 1)
                nc.scalar.activation(dec[:, H1:2 * H1], dec[:, 0:H1], ACT.Ln).then_inc(chain, 1)
                act.wait_ge(chain, 2)
                for h in range(H1):
                    g = dec[:, H1 + h:H1 + h + 1]
                    nc.scalar.activation(lt[:, h * R:(h + 1) * R], p2("lag_t", R), ACT.Exp, scale=g)
                    nc.scalar.activation(ln[:, h * R:(h + 1) * R], p2("lag", R), ACT.Exp, scale=g).then_inc(chain, 1)

                def scale_keys(pair_at, j):
                    if pair_at is None:
                        return
                    i, n1 = pair_at
                    act.wait_ge(inverted[j], n1)
                    wait_free(act, turned[j], i)
                    for g in range(H1):
                        kk = nc.scalar.activation(kn[j][:, g * 128:(g + 1) * 128], xn[j][:, g * 128:(g + 1) * 128],
                                                  ACT.Copy, scale=sc[j][:, 4 + g:5 + g])
                    kk.then_inc(k_ready[j], 1)

                def gate_values(pair_at, j):
                    if pair_at is None:
                        return
                    i, n1 = pair_at
                    act.wait_ge(v_done[j], n1)
                    wait_free(act, n_scaled[j], i)
                    nc.scalar.activation(sc[j][:, 6:8], bank[2 + j][0:R, D:D + H1], ACT.Sigmoid).then_inc(beta_out[j], 1)
                    act.wait_ge(beta_out[j], n1)
                    for h in range(H1):
                        cp = nc.scalar.activation(keepx[0:R, bass.ds((2 * i + j) * D + h * 128, 128)],
                                                  bank[2 + j][0:R, h * 128:(h + 1) * 128], ACT.Copy,
                                                  scale=sc[j][:, 6 + h:7 + h])
                    cp.then_inc(v_out[j], 1)

                def copy_rows_and_keys(pair_at, j):
                    if pair_at is None:
                        return
                    i, n1 = pair_at
                    act.wait_ge(turned[j], n1)
                    wait_free(act, g_done[j], i)
                    nc.scalar.copy(xk[j], bank[j][:, 0:4 * R]).then_inc(t_ready[j], 1)

                def turn(i):
                    last, this = at(act, i, -1), at(act, i)
                    scale_keys(last, 1)
                    gate_values(last, 0)
                    copy_rows_and_keys(last, 1)
                    scale_keys(this, 0)
                    gate_values(last, 1)
                    copy_rows_and_keys(this, 0)

                run_turns(act, turn, behind=1)

            @block.vector
            def _(dve):
                for j in range(2):
                    nc.vector.memset(sc[j][:, 8:10], 0.5).then_inc(rows_free[j], 1)
                nc.vector.memset(sc[0][:, 10:11], 0.5).then_inc(tables, 1)
                dve.wait_ge(chain, 2 + H1)
                for h in range(H1):
                    nc.vector.tensor_tensor(lt[:, h * R:(h + 1) * R], lt[:, h * R:(h + 1) * R], p2("keep_t", R), ALU.mult)
                    last = nc.vector.tensor_tensor(ln[:, h * R:(h + 1) * R], ln[:, h * R:(h + 1) * R], p2("keep", R), ALU.mult)
                last.then_inc(tables, 1)
                dve.wait_ge(tables, 2)

                def row(pair_at, j):
                    return resid[0:R, bass.ds((2 * pair_at[0] + j) * D, D)]

                def row_stats(pair_at, j):
                    if pair_at is not None:
                        norm_stats(dve, row(pair_at, j), j, stats, pair_at[1], rows_free)

                def normalise(pair_at, j):
                    if pair_at is None:
                        return
                    i, n1 = pair_at
                    dve.wait_ge(powered[j], n1)
                    wait_free(dve, turned[j], i)
                    norm_apply(xn[j], row(pair_at, j), j).then_inc(normed[j], 1)

                def key_squares(pair_at, j):
                    if pair_at is None:
                        return
                    i, n1 = pair_at
                    dve.wait_ge(sq_done[j], n1)
                    nc.vector.tensor_reduce(sc[j][:, 0:2], sq[j].rearrange("p (h d) -> p h d", h=H1), AX_X,
                                            ALU.add).then_inc(roots[j], 1)

                def key_inverses(pair_at, j):
                    if pair_at is None:
                        return
                    i, n1 = pair_at
                    dve.wait_ge(rooted[j], n1)
                    nc.vector.tensor_scalar(sc[j][:, 2:4], sc[j][:, 10:12], 1e-12, None, ALU.max).then_inc(floored[j], 1)
                    dve.wait_ge(floored[j], n1)
                    wait_free(dve, k_ready[j], i)
                    nc.vector.reciprocal(sc[j][:, 4:6], sc[j][:, 2:4]).then_inc(inverted[j], 1)

                def decay_products(pair_at, j):
                    if pair_at is None:
                        return
                    i, n1 = pair_at
                    dve.wait_ge(g_done[j], n1)
                    nc.vector.tensor_tensor(attn_t[:, bass.ds((2 * i + j) * H1 * R, H1 * R)], bank[4 + j][0:R, 0:H1 * R],
                                            lt, ALU.mult)
                    nc.vector.tensor_tensor(nf[j], bank[4 + j][0:R, 0:H1 * R], ln, ALU.mult).then_inc(n_masked[j], 1)
                    dve.wait_ge(n_masked[j], n1)
                    nc.vector.tensor_reduce(nk[j].rearrange("p (h t) -> p h t", h=H1),
                                            nf[j].rearrange("p (h m t) -> p h t m", h=H1, m=IPT), AX_X,
                                            ALU.add).then_inc(n_reduced[j], 1)
                    dve.wait_ge(n_reduced[j], n1)
                    dve.wait_ge(beta_out[j], n1)
                    wait_free(dve, n_stored[j], 16 * i)
                    nc.vector.tensor_tensor(nb[j].rearrange("p (h t) -> p h t", h=H1), nk[j].rearrange("p (h t) -> p h t", h=H1),
                                            sc[j][:, 6:8].unsqueeze(2).broadcast_to([R, H1, TOK]),
                                            ALU.mult).then_inc(n_scaled[j], 1)

                def turn(i):
                    before_last, last, this = at(dve, i, -2), at(dve, i, -1), at(dve, i)
                    row_stats(this, 0)
                    key_squares(last, 1)
                    normalise(this, 0)
                    decay_products(before_last, 1)
                    key_inverses(last, 1)
                    row_stats(this, 1)
                    key_squares(this, 0)
                    normalise(this, 1)
                    decay_products(last, 0)
                    key_inverses(this, 0)

                run_turns(dve, turn, behind=2)

            @block.gpsimd
            def _(pool):
                pool.wait_ge(tables, 1)

                def power(pair_at, j):
                    if pair_at is not None:
                        norm_power(pool, j, stats[2], powered, pair_at[1])

                def key_norms(pair_at, j):
                    if pair_at is None:
                        return
                    i, n1 = pair_at
                    pool.wait_ge(roots[j], n1)
                    nc.gpsimd.tensor_tensor(sc[j][:, 10:12], sc[j][:, 0:2], sc[j][:, 8:10], ALU.pow).then_inc(rooted[j], 1)

                def square_and_add(pair_at, j):
                    if pair_at is None:
                        return
                    i, n1 = pair_at
                    h = resid[0:R, bass.ds((2 * i + j) * D, D)]
                    pool.wait_ge(normed[j], n1)
                    nc.gpsimd.tensor_tensor(sq[j], xn[j], xn[j], ALU.mult).then_inc(sq_done[j], 1)
                    nc.gpsimd.tensor_tensor(h, h, xn[j], ALU.add).then_inc(rows_free[j], 1)

                def turn(i):
                    last, this = at(pool, i, -1), at(pool, i)
                    power(this, 0)
                    key_norms(last, 1)
                    square_and_add(this, 0)
                    power(this, 1)
                    key_norms(this, 0)
                    square_and_add(this, 1)

                run_turns(pool, turn, behind=1)

        with phase():
            n_in = psem("n_in")
            chain = psem("chain")
            zeroed = psem("zeroed")
            solved = psem("solved")
            a_stored = psem("a_stored")
            prod = work[:, 0:(TOK - 1) ** 2]
            block = enter(nc.Block())

            def systems(rows, h):
                return rows[0:B * TOK, h * TOK:(h + 1) * TOK].rearrange("(b i) j -> b i j", b=B)

            @block.sync
            def _(sp):
                for h in range(H1):
                    sp.dma_start(sys_n[h * B:(h + 1) * B, :].rearrange("p (i j) -> p i j", i=TOK),
                                 systems(n_rows, h)).then_inc(n_in, 16)
                sp.dma_start(arena_w1[:, :], w1_h).then_inc(w1_in, 16)
                sp.wait_ge(solved, 1)
                for h in range(H1):
                    sp.dma_start(systems(a_rows, h),
                                 sys_x[h * B:(h + 1) * B, :].rearrange("p (j i) -> p j i", j=TOK)).then_inc(a_stored, 16)
                sp.wait_ge(a_stored, 16 * H1)

            @block.vector
            def _(dve):
                x = sys_x.rearrange("p (c i) -> p c i", c=TOK)
                n = sys_n.rearrange("p (i j) -> p i j", i=TOK)
                nc.vector.memset(sys_x, 0.0).then_inc(zeroed, 1)
                dve.wait_ge(zeroed, 1)
                nc.vector.memset(sys_x[:, 0:TOK * TOK:TOK + 1], 1.0).then_inc(zeroed, 1)
                dve.wait_ge(zeroed, 2)
                dve.wait_ge(n_in, 16 * H1)
                for i in range(1, TOK):
                    w = prod[:, 0:i * i].rearrange("p (c j) -> p c j", c=i)
                    nc.vector.tensor_tensor(w, x[:, 0:i, 0:i], n[:, i, 0:i].unsqueeze(1).broadcast_to([128, i, i]),
                                            ALU.mult).then_inc(chain, 1)
                    dve.wait_ge(chain, 2 * i - 1)
                    nc.vector.tensor_reduce(x[:, 0:i, i], w, AX_X, ALU.add).then_inc(chain, 1)
                    dve.wait_ge(chain, 2 * i)
                nc.vector.engine_nop().then_inc(solved, 1)

        with phase():
            stats = [pair("st"), pair("ag"), pair("ve")]
            (a_in, a_block, vn_done, vn_out, o_done, o_out, r_done, added, powered, normed, turned, xt_ready, logits,
             logits_out, x_kept) = (
                pair(n) for n in ("a_in", "a_block", "vn_done", "vn_out", "o_done", "o_out", "r_done", "added",
                                      "powered", "normed", "turned", "xt_ready", "logits", "logits_out", "x_kept"))
            setup = psem("setup")
            wc = carver(work)
            lgr = wc(NT * NE, R)
            xn = [wc(D, R) for _ in range(2)]
            xt = [wc(2 * R) for _ in range(2)]
            st = [wc(8, R) for _ in range(2)]
            ve = [wc(4, R) for _ in range(2)]
            ac = [wc(H1 * TOK, R) for _ in range(2)]
            ab = [wc(H1 * R, R) for _ in range(2)]
            vn = [wc(D, R) for _ in range(2)]
            ot = [wc(H1 * R) for _ in range(2)]
            block = enter(nc.Block())

            @block.sync
            def _(sp):
                def turn(i):
                    for j in range(2):
                        wait_free(sp, a_block[j], i)
                        sp.dma_start(ac[j], a_rows[bass.ds((2 * i + j) * R, R), :]).then_inc(a_in[j], 16)

                run_turns(sp, turn)

            @block.gpsimd
            def _(pool):
                pool.wait_ge(in_cst, 16 * PAIRS)
                pool.wait_ge(setup, 2)

                def spread_inverses(pair_at, j):
                    if pair_at is None:
                        return
                    i, n1 = pair_at
                    pool.wait_ge(a_in[j], 16 * n1)
                    wait_free(pool, vn_done[j], i)
                    for h in range(H1):
                        tt = nc.gpsimd.tensor_tensor(
                            ab[j][:, h * R:(h + 1) * R].rearrange("p (m t) -> p m t", m=IPT),
                            ac[j][:, h * TOK:(h + 1) * TOK].unsqueeze(1).broadcast_to([R, IPT, TOK]),
                            c("mask_img", R).unsqueeze(2).broadcast_to([R, IPT, TOK]), ALU.mult)
                    tt.then_inc(a_block[j], 1)

                def power(pair_at, j):
                    if pair_at is not None:
                        norm_power(pool, j, stats[2], powered, pair_at[1])

                def turn(i):
                    last, this, following = at(pool, i, -1), at(pool, i), at(pool, i, 1)
                    power(last, 1)
                    spread_inverses(following, 0)
                    power(this, 0)
                    spread_inverses(following, 1)

                run_turns(pool, turn, ahead=1, behind=1)

            @block.tensor
            def _(pe):
                w_read = c("w_read").rearrange("p (c n) -> p c n", c=2)
                w_r = c("w_r").rearrange("p (c n) -> p c n", c=2)

                def solve_values(pair_at, j):
                    if pair_at is None:
                        return
                    i, n1 = pair_at
                    pe.wait_ge(a_block[j], n1)
                    wait_free(pe, vn_out[j], i)
                    for h in range(H1):
                        mm = nc.tensor.matmul(bank[j][0:R, h * 128:(h + 1) * 128], ab[j][:, h * R:(h + 1) * R],
                                              keepx[0:R, bass.ds((2 * i + j) * D + h * 128, 128)], start=True, stop=True)
                    mm.then_inc(vn_done[j], 1)

                def attend(pair_at, j):
                    if pair_at is None:
                        return
                    i, n1 = pair_at
                    pe.wait_ge(vn_out[j], n1)
                    wait_free(pe, o_out[j], i)
                    for h in range(H1):
                        mm = nc.tensor.matmul(bank[2 + j][:, h * R:(h + 1) * R], vn[j][:, h * 128:(h + 1) * 128],
                                              attn_t[:, bass.ds(((2 * i + j) * H1 + h) * R, R)], start=True, stop=True)
                    mm.then_inc(o_done[j], 1)

                def read_out(pair_at, j):
                    if pair_at is None:
                        return
                    i, n1 = pair_at
                    pe.wait_ge(o_out[j], n1)
                    wait_free(pe, added[j], i)
                    for k in range(2):
                        mm = nc.tensor.matmul(bank[4 + j][0:R, 0:D], ot[j][:, k * R:(k + 1) * R], w_read[:, k, :],
                                              start=(k == 0), stop=(k == 1))
                    mm.then_inc(r_done[j], 1)

                def turn_rows(pair_at, j):
                    if pair_at is None:
                        return
                    i, n1 = pair_at
                    pe.wait_ge(normed[j], n1)
                    wait_free(pe, logits_out[j], i)
                    for k in range(2):
                        mm = nc.tensor.transpose(bank[6 + j][:, k * R:(k + 1) * R], xn[j][:, k * 128:(k + 1) * 128],
                                                 ident[0:R, 0:R])
                    mm.then_inc(turned[j], 1)

                def router_logits(pair_at, j):
                    if pair_at is None:
                        return
                    i, n1 = pair_at
                    pe.wait_ge(xt_ready[j], n1)
                    for k in range(2):
                        mm = nc.tensor.matmul(bank[6 + j][0:R, 2 * R:2 * R + NE], xt[j][:, k * R:(k + 1) * R],
                                              w_r[:, k, :], start=(k == 0), stop=(k == 1))
                    mm.then_inc(logits[j], 1)

                def turn(i):
                    last, this = at(pe, i, -1), at(pe, i)
                    solve_values(this, 0)
                    read_out(last, 1)
                    turn_rows(last, 0)
                    attend(this, 0)
                    router_logits(last, 0)
                    solve_values(this, 1)
                    read_out(this, 0)
                    turn_rows(last, 1)
                    attend(this, 1)
                    router_logits(last, 1)

                run_turns(pe, turn, behind=1)

            @block.scalar
            def _(act):
                def copy_values(pair_at, j):
                    if pair_at is None:
                        return
                    i, n1 = pair_at
                    act.wait_ge(vn_done[j], n1)
                    wait_free(act, o_done[j], i)
                    nc.scalar.copy(vn[j], bank[j][0:R, 0:D]).then_inc(vn_out[j], 1)

                def copy_output(pair_at, j):
                    if pair_at is None:
                        return
                    i, n1 = pair_at
                    act.wait_ge(o_done[j], n1)
                    wait_free(act, r_done[j], i)
                    nc.scalar.copy(ot[j], bank[2 + j][:, 0:H1 * R]).then_inc(o_out[j], 1)

                def copy_rows(pair_at, j):
                    if pair_at is None:
                        return
                    i, n1 = pair_at
                    act.wait_ge(turned[j], n1)
                    wait_free(act, logits[j], i)
                    nc.scalar.copy(xt[j], bank[6 + j][:, 0:2 * R]).then_inc(xt_ready[j], 1)

                def keep_rows(pair_at, j):
                    if pair_at is None:
                        return
                    i, n1 = pair_at
                    act.wait_ge(normed[j], n1)
                    nc.scalar.copy(keepx[0:R, bass.ds((2 * i + j) * D, D)], xn[j]).then_inc(x_kept[j], 1)

                def turn(i):
                    last, this = at(act, i, -1), at(act, i)
                    copy_values(this, 0)
                    copy_rows(last, 0)
                    copy_output(this, 0)
                    keep_rows(last, 0)
                    copy_values(this, 1)
                    copy_rows(last, 1)
                    copy_output(this, 1)
                    keep_rows(last, 1)

                run_turns(act, turn, behind=1)

            @block.vector
            def _(dve):
                for j in range(2):
                    nc.vector.memset(ve[j][:, 2:3], -0.5).then_inc(setup, 1)

                def add_and_norm(pair_at, j):
                    if pair_at is None:
                        return
                    i, n1 = pair_at
                    h = resid[0:R, bass.ds((2 * i + j) * D, D)]
                    dve.wait_ge(r_done[j], n1)
                    nc.vector.tensor_tensor(h, h, bank[4 + j][0:R, 0:D], ALU.add).then_inc(added[j], 1)
                    norm_stats(dve, h, j, stats, n1, added)
                    dve.wait_ge(powered[j], n1)
                    wait_free(dve, turned[j], i)
                    wait_free(dve, x_kept[j], i)
                    norm_apply(xn[j], h, j).then_inc(normed[j], 1)

                def keep_logits(pair_at, j):
                    if pair_at is None:
                        return
                    i, n1 = pair_at
                    dve.wait_ge(logits[j], n1)
                    nc.vector.tensor_tensor(lgr[:, bass.ds((2 * i + j) * NE, NE)], bank[6 + j][0:R, 2 * R:2 * R + NE],
                                            c("b_r", R), ALU.add).then_inc(logits_out[j], 1)

                def turn(i):
                    last, this = at(dve, i, -1), at(dve, i)
                    add_and_norm(last, 1)
                    keep_logits(last, 0)
                    add_and_norm(this, 0)
                    keep_logits(last, 1)

                run_turns(dve, turn, behind=1)

        x_sent = psem("x_sent")
        with phase():
            chain = psem("chain")
            shifted_s = psem("shifted")
            exp_done = psem("exp_done")
            hot_ready = psem("hot_ready")
            counted = psem("counted")
            slots_ready = psem("slots_ready")
            NG = NT * NE
            rc = carver(work, NG)
            dl, ex, eq, cu, one_hot, cte, inc, tmp = (rc(NG, R) for _ in range(8))
            m1, m2 = rc(NT, R), rc(NT, R)
            cmp_t = rc(NE * MT, R)
            tiles_e, upto_e, off_e = rc(NE, R), rc(NE, R), rc(NE, R)
            past = rc(ST * NE, R)
            eno = rc(ST, R)
            block = enter(nc.Block())

            def by_tile(ap):
                return ap.rearrange("p (t e) -> p t e", t=NT)

            @block.sync
            def _(sp):
                sp.dma_start(arena_w2[:, W2S // 2:W2S], w2_h[:, W2S // 2:W2S]).then_inc(w2b_in, 16)

            @block.scalar
            def _(act):
                act.wait_ge(shifted_s, 1)
                nc.scalar.activation(ex, dl, ACT.Exp).then_inc(exp_done, 1)

            @block.tensor
            def _(pe):
                pe.wait_ge(hot_ready, 1)
                nc.tensor.matmul(bank[0][0:R, 0:NG], c("before", R), one_hot, start=True, stop=True)
                nc.tensor.matmul(bank[1][0:R, 0:NG], c("ones", R), one_hot, start=True, stop=True).then_inc(counted, 1)

            @block.vector
            def _(dve):
                count = [0]

                def link(ins):
                    count[0] += 1
                    ins.then_inc(chain, 1)
                    dve.wait_ge(chain, count[0])

                tt, ts, red = nc.vector.tensor_tensor, nc.vector.tensor_scalar, nc.vector.tensor_reduce
                link(red(m1, by_tile(lgr), AX_X, ALU.max))
                tt(by_tile(dl), by_tile(lgr), m1.unsqueeze(2).broadcast_to([R, NT, NE]), ALU.subtract).then_inc(shifted_s, 1)
                dve.wait_ge(shifted_s, 1)
                link(ts(eq, dl, 0.0, None, ALU.is_equal))
                link(nc.vector.tensor_tensor_scan(cu, c("seg_e", R), eq, 0.0, ALU.mult, ALU.add))
                link(nc.vector.scalar_tensor_tensor(tmp, cu, 1.0, eq, ALU.is_equal, ALU.mult))
                tt(by_tile(one_hot), by_tile(tmp), c("valid", R).unsqueeze(2).broadcast_to([R, NT, NE]), ALU.mult).then_inc(hot_ready, 1)
                dve.wait_ge(exp_done, 1)
                link(red(m2, by_tile(ex), AX_X, ALU.add))
                link(nc.vector.reciprocal(gate[0:R, :], m2))
                dve.wait_ge(counted, 1)
                link(nc.vector.tensor_copy(cte.rearrange("p (e t) -> p e t", e=NE),
                                           bank[1][0:R, 0:NG].rearrange("p (t e) -> p e t", e=NE)))
                link(nc.vector.tensor_tensor_scan(inc, c("seg_t", R), cte, 0.0, ALU.mult, ALU.add))
                link(tt(cte, inc, cte, ALU.subtract))
                total = inc.rearrange("p (e t) -> p e t", e=NE)[:, :, NT - 1:NT]
                link(tt(cmp_t.rearrange("p (e k) -> p e k", e=NE), total.broadcast_to([R, NE, MT]),
                        c("starts", R).unsqueeze(1).broadcast_to([R, NE, MT]), ALU.is_gt))
                link(red(tiles_e, cmp_t.rearrange("p (e k) -> p e k", e=NE), AX_X, ALU.add))
                link(nc.vector.tensor_tensor_scan(upto_e, c("ones", R)[:, 0:NE], tiles_e, 0.0, ALU.mult, ALU.add))
                link(tt(off_e, upto_e, tiles_e, ALU.subtract))
                link(ts(off_e, off_e, 128.0, None, ALU.mult))
                link(tt(cte.rearrange("p (e t) -> p e t", e=NE), cte.rearrange("p (e t) -> p e t", e=NE),
                        off_e.unsqueeze(2).broadcast_to([R, NE, NT]), ALU.add))
                link(tt(by_tile(tmp), by_tile(bank[0][0:R, 0:NG]), cte.rearrange("p (e t) -> p t e", e=NE), ALU.add))
                link(tt(tmp, tmp, one_hot, ALU.mult))
                link(red(m1, by_tile(tmp), AX_X, ALU.add))
                nc.vector.tensor_copy(slot_i[0:R, :], m1).then_inc(slots_ready, 1)
                link(tt(past.rearrange("p (s e) -> p s e", s=ST), upto_e.unsqueeze(1).broadcast_to([R, ST, NE]),
                        c("tile_no", R).unsqueeze(2).broadcast_to([R, ST, NE]), ALU.is_le))
                link(red(eno, past.rearrange("p (s e) -> p s e", s=ST), AX_X, ALU.add))
                link(ts(eno, eno, float(NE - 1), None, ALU.min))
                link(nc.vector.tensor_copy(expert_i[0:1, :], eno[0:1, :]))

            @block.gpsimd
            def _(pool):
                pool.wait_ge(slots_ready, 1)
                for t in range(NT):
                    rows = min(R, (B - t * IPT) * TOK)
                    pool.indirect_dma_start(x_slots, bass.IndirectOffsetOnAxis(ap=slot_i[0:rows, t:t + 1], axis=0),
                                            keepx[0:rows, t * D:(t + 1) * D], None).then_inc(x_sent, 16)
                pool.wait_ge(x_sent, 16 * NT)

        with phase():
            (x_in, x_turned, xt_ready, h_done, h_out, h_act, y_done, y_out, y_stored) = (
                pair(n) for n in ("x_in", "x_turned", "xt_ready", "h_done", "h_out", "h_act", "y_done", "y_out", "y_stored"))
            h_turned = [pair(f"h_turned{f}_") for f in range(2)]
            SP = ST // 2
            wc = carver(work)
            xg = [wc(D) for _ in range(2)]
            xgt = [wc(D) for _ in range(2)]
            hp = [wc(FF) for _ in range(2)]
            ht = [wc(FF) for _ in range(2)]
            yo = [wc(D) for _ in range(2)]
            block = enter(nc.Block())

            def expert_of(eng, pair_at, j):
                if pair_at is None:
                    return None
                return eng.value_load(expert_i[0:1, bass.ds(2 * pair_at[0] + j, 1)], min_val=0, max_val=NE - 1)

            def other_slot_free(eng, semaphores, pair_at, j, count=1):
                i, n1 = pair_at
                if j:
                    eng.wait_ge(semaphores[0], n1 * count)
                else:
                    wait_free(eng, semaphores[1], i * count)

            @block.sync
            def _(sp):
                def turn(i):
                    for j in range(2):
                        wait_free(sp, x_turned[j], i)
                        sp.dma_start(xg[j], x_slots[bass.ds((2 * i + j) * 128, 128), :]).then_inc(x_in[j], 16)

                run_turns(sp, turn, total=SP)

            @block.tensor
            def _(pe):
                pe.wait_ge(w1_in, 16)
                pe.wait_ge(w2a_in, 16)
                pe.wait_ge(w2b_in, 16)

                def turn_tokens(pair_at, j):
                    if pair_at is None:
                        return
                    i, n1 = pair_at
                    pe.wait_ge(x_in[j], 16 * n1)
                    other_slot_free(pe, xt_ready, pair_at, j)
                    for k in range(2):
                        mm = nc.tensor.transpose(bank[6][:, k * 128:(k + 1) * 128], xg[j][:, k * 128:(k + 1) * 128], ident)
                    mm.then_inc(x_turned[j], 1)

                def hidden(pair_at, j, expert):
                    if pair_at is None:
                        return
                    i, n1 = pair_at
                    pe.wait_ge(xt_ready[j], n1)
                    wait_free(pe, h_out[j], i * 2)
                    for f in range(2):
                        for k in range(2):
                            mm = nc.tensor.matmul(bank[2 * j + f][:, :], xgt[j][:, k * 128:(k + 1) * 128],
                                                  arena_w1[:, bass.ds(expert * (2 * FF) + (k * FF + f * 512), 512)],
                                                  start=(k == 0), stop=(k == 1))
                        mm.then_inc(h_done[j], 1)

                def turn_hidden(pair_at, j):
                    if pair_at is None:
                        return
                    i, n1 = pair_at
                    other_slot_free(pe, h_act, pair_at, j, FC)
                    for f in range(2):
                        pe.wait_ge(h_out[j], i * 2 + f + 1)
                        for k in range(4):
                            mm = nc.tensor.transpose(bank[4 + f][:, k * 128:(k + 1) * 128],
                                                     hp[j][:, (4 * f + k) * 128:(4 * f + k + 1) * 128], ident)
                        mm.then_inc(h_turned[f][j], 1)

                def outputs(pair_at, j, expert):
                    if pair_at is None:
                        return
                    i, n1 = pair_at
                    other_slot_free(pe, y_out, pair_at, j)
                    for g in range(FC):
                        pe.wait_ge(h_act[j], i * FC + g + 1)
                        mm = nc.tensor.matmul(bank[7][:, 0:D], ht[j][:, g * 128:(g + 1) * 128],
                                              arena_w2[:, bass.ds(expert * (FC * D) + g * D, D)],
                                              start=(g == 0), stop=(g == FC - 1))
                    mm.then_inc(y_done[j], 1)

                def turn(i):
                    last, this, following = at(pe, i, -1, SP), at(pe, i, 0, SP), at(pe, i, 1, SP)
                    last_expert = expert_of(pe, last, 1)
                    experts = [expert_of(pe, this, j) for j in range(2)]
                    hidden(this, 0, experts[0])
                    turn_tokens(this, 1)
                    outputs(last, 1, last_expert)
                    turn_hidden(this, 0)
                    hidden(this, 1, experts[1])
                    turn_tokens(following, 0)
                    outputs(this, 0, experts[0])
                    turn_hidden(this, 1)

                run_turns(pe, turn, ahead=1, behind=1, total=SP)

            @block.vector
            def _(dve):
                def copy_tokens(pair_at, j):
                    if pair_at is None:
                        return
                    i, n1 = pair_at
                    dve.wait_ge(x_turned[j], n1)
                    wait_free(dve, h_done[j], i * 2)
                    nc.vector.tensor_copy(xgt[j], bank[6][:, 0:D]).then_inc(xt_ready[j], 1)

                def copy_hidden(pair_at, j):
                    if pair_at is None:
                        return
                    i, n1 = pair_at
                    for f in range(2):
                        dve.wait_ge(h_done[j], i * 2 + f + 1)
                        wait_free(dve, h_turned[f][j], i)
                        nc.vector.tensor_copy(hp[j][:, f * 512:(f + 1) * 512], bank[2 * j + f][:, :]).then_inc(h_out[j], 1)

                def add_bias(pair_at, j, expert):
                    if pair_at is None:
                        return
                    i, n1 = pair_at
                    dve.wait_ge(y_done[j], n1)
                    wait_free(dve, y_stored[j], 16 * i)
                    nc.vector.tensor_tensor(yo[j], bank[7][:, 0:D],
                                            cst[:, bass.ds(expert * D + atc["b2"][0], D)], ALU.add).then_inc(y_out[j], 1)

                def turn(i):
                    last, this, following = at(dve, i, -1, SP), at(dve, i, 0, SP), at(dve, i, 1, SP)
                    last_expert, expert = expert_of(dve, last, 1), expert_of(dve, this, 0)
                    copy_hidden(this, 0)
                    copy_tokens(this, 1)
                    add_bias(last, 1, last_expert)
                    copy_hidden(this, 1)
                    copy_tokens(following, 0)
                    add_bias(this, 0, expert)

                run_turns(dve, turn, ahead=1, behind=1, total=SP)

            @block.scalar
            def _(act):
                def activate(pair_at, j, expert):
                    i, n1 = pair_at
                    wait_free(act, y_done[j], i)
                    for f in range(2):
                        act.wait_ge(h_turned[f][j], n1)
                        for k in range(4):
                            g = 4 * f + k
                            nc.scalar.activation(ht[j][:, g * 128:(g + 1) * 128], bank[4 + f][:, k * 128:(k + 1) * 128],
                                                 ACT.Gelu, bias=cst[:, bass.ds(expert * FC + (atc["b1"][0] + g), 1)]
                                                 ).then_inc(h_act[j], 1)

                def turn(i):
                    this = at(act, i, 0, SP)
                    for j in range(2):
                        activate(this, j, expert_of(act, this, j))

                run_turns(act, turn, total=SP)

            @block.gpsimd
            def _(pool):
                def turn(i):
                    for j in range(2):
                        pool.wait_ge(y_out[j], i + 1)
                        pool.dma_start(y_slots[bass.ds((2 * i + j) * 128, 128), :], yo[j]).then_inc(y_stored[j], 16)

                run_turns(pool, turn, total=SP)
                for j in range(2):
                    pool.wait_ge(y_stored[j], 16 * SP)

        with phase():
            NB = 4
            y_in = [psem(f"y_in{k}") for k in range(NB)]
            gated = psem("gated")
            out_sent = psem("out_sent")
            yg = [work[:, k * D:(k + 1) * D] for k in range(NB)]
            block = enter(nc.Block())

            def rows_of(t):
                return min(R, (B - t * IPT) * TOK)

            @block.gpsimd
            def _(pool):
                for t in range(NT):
                    if t >= NB:
                        pool.wait_ge(gated, t - NB + 1)
                    n = rows_of(t)
                    pool.indirect_dma_start(yg[t % NB][0:n, :], None, y_slots,
                                            bass.IndirectOffsetOnAxis(ap=slot_i[0:n, t:t + 1], axis=0)).then_inc(y_in[t % NB], 16)

            @block.vector
            def _(dve):
                for t in range(NT):
                    n = rows_of(t)
                    h = resid[0:n, t * D:(t + 1) * D]
                    dve.wait_ge(y_in[t % NB], 16 * (t // NB + 1))
                    nc.vector.scalar_tensor_tensor(h, yg[t % NB][0:n, :], gate[0:n, t:t + 1], h, ALU.mult,
                                                   ALU.add).then_inc(gated, 1)

            @block.sync
            def _(sp):
                for t in range(NT):
                    n = rows_of(t)
                    sp.wait_ge(gated, t + 1)
                    sp.dma_start(out_h[t * R:t * R + n, :], resid[0:n, t * D:(t + 1) * D]).then_inc(out_sent, 16)
                sp.wait_ge(out_sent, 16 * NT)


def lay_out(inp):
    import numpy as np

    f = {k: np.asarray(v) for k, v in inp.items()}

    def chunks(w, c):
        return w.reshape(c, 128, -1).transpose(1, 0, 2).reshape(128, -1)

    def rows(v, n=R):
        return np.broadcast_to(np.asarray(v).reshape(1, -1), (n, v.size))

    patches = f["x"].reshape(B, 3, 6, 16, 6, 16).transpose(0, 2, 4, 1, 3, 5).reshape(B, TOK - 1, FP)
    padded = np.zeros((NT * IPT, TOK, FP), np.float32)
    padded[:B, 1:] = patches
    x_h = np.ascontiguousarray(padded.reshape(NT, IPT, TOK, PC, 128).transpose(0, 4, 3, 1, 2).reshape(NT, 128, -1))

    p = {}
    p["w_lin"] = chunks(f["L0_tok_W_lin"].T, PC)
    p["pos"] = np.tile(f["L0_tok_position_embeddings"][0], (IPT, 1))
    add = np.concatenate([f["L0_tok_class_token"][0], rows(f["L0_tok_b_lin"], TOK - 1)], 0)
    p["pos_add"] = np.tile(add, (IPT, 1))
    p["w_q"] = chunks(f["L0_attn_Wq"].T, 2)
    p["b_q"] = rows(f["L0_attn_bq"])
    kv, bkv = f["L0_attn_Wkv"], f["L0_attn_bkv"]
    p["w_k"] = chunks(np.tile(kv[:HD].T, (1, HH)), 2)
    p["b_k"] = np.tile(bkv[:HD], HH)[:, None]
    p["w_v"] = chunks(kv[HD:].T, 2)
    p["b_v"] = rows(bkv[HD:])
    p["w_o"] = chunks(f["L0_attn_Wo"].T, 2)
    p["b_o"] = rows(f["L0_attn_bo"])
    p["proj"] = chunks(f["L0_ffn_proj"], 2)
    p["w_in1"] = chunks(f["L0_ffn_Win1"][:D], 2)
    p["b_in1"] = f["L0_ffn_Win1"][D][:, None]
    p["c1"], p["c2"] = f["L0_ffn_C1"], f["L0_ffn_C2"]
    p["w_out1"] = f["L0_ffn_Wout1"].T
    p["w_in2"] = chunks(f["L0_ffn_Win2"][:O0], OC)
    p["b_in2"] = f["L0_ffn_Win2"][O0][:, None]
    p["w_out2"] = f["L0_ffn_Wout2"].T
    p["w_vb"] = chunks(np.concatenate([f["L1_attn_W_write"].T, f["L1_attn_W_beta"].T], 1), 2)
    p["decay"] = rows(f["L1_attn_decay"])
    p["w_read"] = chunks(f["L1_attn_W_read"].T, 2)
    p["w_r"] = chunks(f["L1_ffn_Wr"], 2)
    p["b_r"] = rows(f["L1_ffn_br"])
    p["b1"] = f["L1_ffn_b1"].reshape(NE, FC, 128).transpose(2, 0, 1).reshape(128, -1)
    p["b2"] = rows(f["L1_ffn_b2"], 128)

    r = np.arange(R)
    img, pos = r // TOK, r % TOK
    same = img[:, None] == img[None, :]
    lag = (pos[:, None] - pos[None, :]).astype(np.float32)
    p["mask_head"] = np.arange(128)[:, None] // HD == np.arange(HH)
    p["mask_pair"] = np.arange(128)[:, None] // HP == np.arange(2)
    p["lag"] = np.where(same & (lag > 0), lag, 0)
    p["keep"] = -1.0 * (same & (lag > 0))
    p["lag_t"] = np.where(same.T & (lag.T >= 0), lag.T, 0)
    p["keep_t"] = same.T & (lag.T >= 0)
    k = np.tile(np.arange(1, E0 + 1, dtype=np.float32), NT)
    p["inv_k"], p["rank_k"], p["seg_e0"] = rows(1 / k), rows(k), rows(np.float32(k > 1))
    p["ident"] = np.eye(128)
    p["mask_img"] = img[:, None] == np.arange(IPT)
    p["before"] = r[:, None] < r[None, :]
    p["ones"] = np.ones((R, R))
    p["valid"] = np.arange(NT)[None, :] * R + r[:, None] < B * TOK
    p["seg_e"] = rows(np.float32(np.arange(NT * NE) % NE > 0))
    p["seg_t"] = rows(np.float32(np.arange(NT * NE) % NT > 0))
    p["starts"] = rows(128.0 * np.arange(MT))
    p["tile_no"] = rows(1.0 * np.arange(ST))

    def packed(pack, start=0):
        at, n = offsets(pack, start)
        out = np.zeros((128, n), np.float32)
        for name, (a, w) in at.items():
            out[:p[name].shape[0], a:a + w] = p[name]
        return out

    w1 = f["L1_ffn_W1"].reshape(NE, 2, 128, FF).transpose(2, 0, 1, 3).reshape(128, -1)
    w2 = f["L1_ffn_W2"].reshape(NE, FC, 128, D).transpose(2, 0, 1, 3).reshape(128, -1)
    return {"in_x": x_h, "in_pack1": packed(PACK1), "in_pack2": packed(PACK2), "in_packc": packed(PACKC, 128),
            "in_w1": np.ascontiguousarray(w1), "in_w2": np.ascontiguousarray(w2)}


def kernel(**inputs):
    import concourse.bacc as _bacc
    from concourse import mybir as _mybir
    from concourse.bass_utils import run_bass_kernel_spmd as _run

    nc = _bacc.Bacc("TRN2", target_bir_lowering=False, num_devices=1)
    arrays = lay_out(inputs)
    args = [nc.dram_tensor(n, a.shape, _mybir.dt.from_np(a.dtype), kind="ExternalInput").ap() for n, a in arrays.items()]
    args.append(nc.dram_tensor("out_0", (B * TOK, D), F32, kind="ExternalOutput").ap())
    build(nc, *args)
    r = _run(nc, [arrays], core_ids=[0])
    return r.results[0]["out_0"].reshape(B, TOK, D)
```

```python
from contextlib import ExitStack, contextmanager

import concourse.bass as bass
from concourse import mybir

ALU = mybir.AluOpType
ACT = mybir.ActivationFunctionType
F32 = mybir.dt.float32
I32 = mybir.dt.int32
AX_X = mybir.AxisListType.X

B, TOK, D = 64, 37, 256
IPT = 3
R = IPT * TOK
NT = -(-B // IPT)
PAIRS = NT // 2
FP = 768
PC = FP // 128
NH, HD = 16, 16
HH = NH // 2
E0, RK, O0 = 16, 128, 1024
OC = O0 // 128
H1 = 2
NE, FF = 8, 1024
FC = FF // 128
ST = (B * TOK + NE * 127) // 128
EPS = 1e-5
RW = 2 * D + 2
HC = NH // 2
KR = IPT * 2 * HD
HP = 64
PR = HP + TOK
CUTS = [i if i < 8 else 6 if i < 18 else 16 for i in range(TOK)]
MT = 19

PACK1 = [("w_lin", PC * D), ("pos", D), ("pos_add", D), ("w_q", 2 * D), ("b_q", D), ("w_k", 2 * 2 * HD),
         ("b_k", 1), ("w_v", 2 * HD), ("b_v", HD)]
PACK2 = [("w_o", 2 * D), ("b_o", D), ("proj", 2 * E0), ("w_in1", 2 * RK), ("b_in1", 1), ("c1", RK), ("c2", RK),
         ("w_out1", O0), ("w_in2", OC * RK), ("b_in2", 1), ("w_out2", D), ("w_vb", 2 * (D + H1)),
         ("mask_head", 2), ("mask_pair", 2), ("lag_t", R), ("keep_t", R), ("lag", R), ("keep", R), ("decay", H1),
         ("inv_k", NT * E0), ("rank_k", NT * E0), ("seg_e0", NT * E0)]
PACKC = [("ident", 128), ("mask_img", IPT), ("w_read", 2 * D), ("w_r", 2 * NE), ("b_r", NE), ("before", R),
         ("ones", R), ("out_row", NT), ("b1", NE * FC), ("b2", NE * D), ("seg_e", NT * NE), ("seg_t", NE * NT),
         ("starts", MT), ("tile_no", ST)]


def offsets(pack, start=0):
    at, out = 0, {}
    for name, width in pack:
        out[name] = (at, width)
        at += width
    return out, start + -(-(at - start) // PAIRS) * PAIRS


def build(nc, x_h, pack1_h, pack2_h, packc_h, w1_h, w2_h, out_h):
    at1, n1w = offsets(PACK1)
    at2, n2w = offsets(PACK2)
    atc, ncw = offsets(PACKC, 128)

    q_rows = nc.dram_tensor("q_rows", (NT * R, D), F32).ap()
    n_rows = nc.dram_tensor("n_rows", (H1, NT * R, TOK), F32).ap()
    a_rows = nc.dram_tensor("a_rows", (H1, NT * R, TOK), F32).ap()
    x_slots = nc.dram_tensor("x_slots", (ST * 128, RW), F32).ap()

    with ExitStack() as top:
        def sb(name, width, dt=F32, rows=128):
            return top.enter_context(nc.sbuf_tensor(name, [rows, width], dt))

        def sem(name):
            return top.enter_context(nc.semaphore(name))

        W1S = NE * 2 * FF
        W2S = NE * FC * D
        arena_w1 = sb("arena_w1", W1S)
        arena_w2 = sb("arena_w2", W2S)
        tokens = sb("tokens", NT * RW)
        cst = sb("cst", ncw)
        work = sb("work", 5632)
        slot_i = sb("slot_i", NT, I32)
        expert_i = sb("expert_i", ST, I32, rows=1)
        out_row = sb("out_row", 2, I32)
        bank = [top.enter_context(nc.psum_tensor(f"bank{k}", [128, 512], F32)) for k in range(8)]

        def carver(arena, start=0):
            pos = [start]

            def carve(width, rows=128):
                a = pos[0]
                pos[0] += width
                assert pos[0] <= arena.shape[1], (pos[0], arena.shape)
                return arena[0:rows, a:a + width]
            return carve

        def c(name, rows=128):
            a, w = atc[name]
            return cst[0:rows, a:a + w]

        ident = c("ident")
        carve_a = carver(arena_w1)
        pack1 = carve_a(n1w)
        pack2 = carve_a(n2w)

        def p1(name, rows=128):
            a, w = at1[name]
            return pack1[0:rows, a:a + w]

        def p2(name, rows=128):
            a, w = at2[name]
            return pack2[0:rows, a:a + w]

        carve_0 = carver(arena_w2)
        x_t = carve_0(2 * NT * R)
        k_rep = carve_0(NT * TOK, KR)
        carve_1 = carver(arena_w2, W2S // 2)
        attn_t = carve_1(NT * H1 * R, R)
        sys_n = carve_1(TOK * TOK)
        sys_x = carve_1(TOK * TOK)
        beta_img = carve_1(NT * H1 * IPT, R)
        carve_1b = carver(arena_w2, W2S // 2)
        v_rep = carve_1b(NT * IPT * HD, PR)
        gate_t = carver(arena_w2, W2S // 2 + NT * H1 * R)(NT * R, E0)
        lg0 = carve_1b(NT * E0, R)

        zeros = arena_w2[:, W2S - RW // 2:W2S]

        q_stored = [sem(f"q_stored{j}") for j in range(2)]
        q_in = [sem(f"q_in{j}") for j in range(2)]
        in_params = sem("in_params")
        in_qkv = sem("in_qkv")
        in_ident = sem("in_ident")
        in_params2 = sem("in_params2")
        in_cst = sem("in_cst")
        zeros_out = sem("zeros_out")
        w2a_in = sem("w2a_in")
        w2b_in = sem("w2b_in")
        w1_in = sem("w1_in")

        phase_sems = []

        def psem(name):
            phase_sems.append(nc.alloc_semaphore(name=f"p{len(blocks)}_{name}"))
            return phase_sems[-1]

        def pair(name):
            return [psem(f"{name}{j}") for j in range(2)]

        @contextmanager
        def phase():
            with ExitStack() as inner:
                blocks.append(inner)
                yield
            nc.clear_and_free_semaphores(phase_sems)
            nc.all_engine_barrier()
            phase_sems.clear()

        blocks = []

        def enter(block):
            return blocks[-1].enter_context(block)

        def stand_alone(eng):
            eng.wait_ge(in_ident, 16)

        def at(eng, i, shift=0, total=PAIRS):
            if isinstance(i, int):
                return (i + shift, i + shift + 1) if 0 <= i + shift < total else None
            return (eng.snap(i + shift), eng.snap(i + shift + 1))

        def run_turns(eng, turn, ahead=0, behind=0, total=PAIRS):
            for i in range(-ahead, behind + 1):
                turn(i)
            with eng.Fori(behind + 1, total - ahead) as i:
                turn(i)
            for i in range(total - ahead, total + behind):
                turn(i)

        def wait_free(eng, semaphore, n):
            if not (isinstance(n, int) and n == 0):
                eng.wait_ge(semaphore, n)

        def other_slot_free(eng, semaphores, pair_at, j, count=1):
            i, n1 = pair_at
            if j:
                eng.wait_ge(semaphores[0], n1 * count)
            else:
                wait_free(eng, semaphores[1], i * count)

        ph2_carve = carver(arena_w1, n1w + n2w)
        posb = ph2_carve(D, R)
        qm = [ph2_carve(HC * R, KR) for _ in range(2)]
        kb = [ph2_carve(2 * TOK, KR) for _ in range(2)]
        qx = [ph2_carve(NH * IPT * HD, R) for _ in range(2)]
        vb = [ph2_carve(IPT * 2 * HD, PR) for _ in range(2)]
        xp = [ph2_carve(IPT * PC * TOK) for _ in range(2)]
        wc = carver(work)
        xn = [wc(D, R) for _ in range(2)]
        xt = [wc(2 * R) for _ in range(2)]
        st = [wc(8, R) for _ in range(2)]
        ve = [wc(4, R) for _ in range(2)]
        qn = [wc(D, R) for _ in range(2)]
        small = [wc(3 * NH, R) for _ in range(2)]
        prob = [wc(NH * HP, R) for _ in range(2)]

        def norm_stats(dve, x, j, sems, n1, after):
            s_st, s_ag, s_ve = sems
            stand_alone(dve)
            dve.wait_ge(after[j], n1)
            nc.vector.bn_stats(st[j][:, 0:6], x).then_inc(s_st[j], 1)
            stand_alone(dve)
            dve.wait_ge(s_st[j], n1)
            nc.vector.bn_aggr(st[j][:, 6:8], st[j][:, 0:6]).then_inc(s_ag[j], 1)
            dve.wait_ge(s_ag[j], n1)
            nc.vector.tensor_scalar(ve[j][:, 0:1], st[j][:, 7:8], EPS, None, ALU.add).then_inc(s_ve[j], 1)

        def norm_power(pool, j, s_ve, s_rs, n1):
            pool.wait_ge(s_ve[j], n1)
            nc.gpsimd.tensor_tensor(ve[j][:, 1:2], ve[j][:, 0:1], ve[j][:, 2:3], ALU.pow).then_inc(s_rs[j], 1)

        def norm_apply(out, x, j):
            return nc.vector.tensor_scalar(out, x, st[j][:, 6:7], ve[j][:, 1:2], ALU.subtract, ALU.mult)

        def load_queries(sp, i, j):
            for m in range(IPT):
                src = q_rows[bass.ds((2 * i + j) * R + m * TOK, TOK), :].rearrange("t (g d) -> (t g) d", d=HD)
                for e in range(2):
                    sp.dma_start(
                        qx[j][m * TOK:(m + 1) * TOK, :].rearrange("t (c m e d) -> t c m e d", m=IPT, e=2, d=HD)[:, :, m, e, :],
                        src.rearrange("(c e t) d -> t c e d", e=2, t=TOK)[:, :, e, :]).then_inc(q_in[j], 16)

        with phase():
            x_in = pair("x_in")
            embedded = pair("embedded")
            summed = pair("summed")
            stats = [pair("st"), pair("ag"), pair("ve")]
            powered = pair("powered")
            normed = pair("normed")
            turned = pair("turned")
            xt_ready = pair("xt_ready")
            q_done = pair("q_done")
            kv_done = pair("kv_done")
            q_out = pair("q_out")
            k_out = pair("k_out")
            v_out = pair("v_out")
            setup = psem("setup")
            pos_ready = psem("pos_ready")
            zero_ready = psem("zero_ready")
            block = enter(nc.Block())

            @block.sync
            def _(sp):
                embed_w = at1["w_q"][0]
                sp.dma_start(pack1[:, 0:embed_w], pack1_h[:, 0:embed_w]).then_inc(in_params, 16)

                def turn(i):
                    for j in range(2):
                        wait_free(sp, embedded[j], i)
                        sp.dma_start(xp[j], x_h[bass.ds(2 * i + j, 1)].rearrange("o p n -> (o p) n")).then_inc(x_in[j], 16)

                run_turns(sp, turn)
                sp.wait_ge(zero_ready, 6)
                for j in range(2):
                    sp.wait_ge(q_stored[j], 16)
                    load_queries(sp, 0, j)

            @block.tensor
            def _(pe):
                pe.wait_ge(in_params, 16)
                pe.wait_ge(in_ident, 16)
                pe.wait_ge(in_qkv, 16)
                w_lin = p1("w_lin").rearrange("p (c n) -> p c n", c=PC)
                w_q = p1("w_q").rearrange("p (c n) -> p c n", c=2)
                w_k = p1("w_k").rearrange("p (c n) -> p c n", c=2)
                w_v = p1("w_v").rearrange("p (c n) -> p c n", c=2)

                def embed(pair_at, j):
                    if pair_at is None:
                        return
                    i, n1 = pair_at
                    pe.wait_ge(x_in[j], 16 * n1)
                    wait_free(pe, summed[j], i)
                    for k in range(PC):
                        mm = nc.tensor.matmul(bank[j][0:R, 0:D], xp[j][:, k * R:(k + 1) * R], w_lin[:, k, :],
                                              start=(k == 0), stop=(k == PC - 1))
                    mm.then_inc(embedded[j], 1)

                def turn_rows(pair_at, j):
                    if pair_at is None:
                        return
                    i, n1 = pair_at
                    pe.wait_ge(normed[j], n1)
                    wait_free(pe, xt_ready[j], i)
                    for k in range(2):
                        mm = nc.tensor.transpose(bank[2 + j][:, k * R:(k + 1) * R], xn[j][:, k * 128:(k + 1) * 128],
                                                 ident[0:R, 0:R])
                    mm.then_inc(turned[j], 1)

                def queries_keys_values(pair_at, j):
                    if pair_at is None:
                        return
                    i, n1 = pair_at
                    pe.wait_ge(xt_ready[j], n1)
                    wait_free(pe, q_out[j], i)
                    for k in range(2):
                        mm = nc.tensor.matmul(bank[4 + j][0:R, 0:D], xt[j][:, k * R:(k + 1) * R], w_q[:, k, :],
                                              start=(k == 0), stop=(k == 1))
                    mm.then_inc(q_done[j], 1)
                    wait_free(pe, k_out[j], i)
                    wait_free(pe, v_out[j], 2 * i)
                    for m in range(IPT):
                        for k in range(2):
                            a = k * R + m * TOK
                            nc.tensor.matmul(bank[6 + j][m * 2 * HD:(m + 1) * 2 * HD, 0:TOK], w_k[:, k, :],
                                             xt[j][:, a:a + TOK], start=(k == 0), stop=(k == 1))
                    for lo in (0, HP):
                        for m in range(IPT):
                            for k in range(2):
                                a = k * R + m * TOK
                                mm = nc.tensor.matmul(bank[6 + j][lo:lo + TOK, R + m * HD:R + (m + 1) * HD],
                                                      xt[j][:, a:a + TOK], w_v[:, k, :], start=(k == 0), stop=(k == 1))
                    mm.then_inc(kv_done[j], 1)

                def turn(i):
                    last, this = at(pe, i, -1), at(pe, i)
                    embed(this, 0)
                    turn_rows(last, 1)
                    queries_keys_values(last, 0)
                    embed(this, 1)
                    turn_rows(this, 0)
                    queries_keys_values(last, 1)

                run_turns(pe, turn, behind=1)

            @block.vector
            def _(dve):
                dve.wait_ge(in_params, 16)
                dve.wait_ge(in_qkv, 16)
                nc.vector.tensor_tensor(posb, p1("pos", R), p1("pos_add", R), ALU.add).then_inc(pos_ready, 1)
                for j in range(2):
                    nc.vector.memset(ve[j][:, 2:3], -0.5).then_inc(setup, 1)
                dve.wait_ge(pos_ready, 1)

                def add_and_norm(pair_at, j):
                    if pair_at is None:
                        return
                    i, n1 = pair_at
                    h = tokens[0:R, bass.ds((2 * i + j) * RW, D)]
                    dve.wait_ge(embedded[j], n1)
                    nc.vector.tensor_tensor(h, bank[j][0:R, 0:D], posb, ALU.add).then_inc(summed[j], 1)
                    norm_stats(dve, h, j, stats, n1, summed)
                    dve.wait_ge(powered[j], n1)
                    wait_free(dve, turned[j], i)
                    norm_apply(xn[j], h, j).then_inc(normed[j], 1)

                def queries_keys_values(pair_at, j):
                    if pair_at is None:
                        return
                    i, n1 = pair_at
                    dve.wait_ge(q_done[j], n1)
                    wait_free(dve, q_stored[j], 16 * i)
                    nc.vector.tensor_tensor(qn[j], bank[4 + j][0:R, 0:D], p1("b_q", R), ALU.add).then_inc(q_out[j], 1)
                    dve.wait_ge(kv_done[j], n1)
                    nc.vector.tensor_scalar(k_rep[:, bass.ds((2 * i + j) * TOK, TOK)], bank[6 + j][0:KR, 0:TOK],
                                            p1("b_k", KR), None, ALU.add).then_inc(k_out[j], 1)
                    for lo in (0, HP):
                        rows = slice(lo, lo + TOK)
                        nc.vector.tensor_tensor(
                            v_rep[rows, bass.ds((2 * i + j) * IPT * HD, IPT * HD)].rearrange("p (m d) -> p m d", m=IPT),
                            bank[6 + j][rows, R:R + IPT * HD].rearrange("p (m d) -> p m d", m=IPT),
                            p1("b_v")[rows, :].unsqueeze(1).broadcast_to([TOK, IPT, HD]), ALU.add).then_inc(v_out[j], 1)

                def turn(i):
                    last, this = at(dve, i, -1), at(dve, i)
                    add_and_norm(this, 0)
                    queries_keys_values(last, 0)
                    add_and_norm(this, 1)
                    queries_keys_values(last, 1)

                dve.wait_ge(zero_ready, 6)
                run_turns(dve, turn, behind=1)

            @block.scalar
            def _(act):
                embed_w = at1["w_q"][0]
                act.dma_start(ident, packc_h[:, 0:128]).then_inc(in_ident, 16)
                act.dma_start(pack1[:, embed_w:], pack1_h[:, embed_w:]).then_inc(in_qkv, 16)

                def copy_rows(pair_at, j):
                    if pair_at is None:
                        return
                    i, n1 = pair_at
                    act.wait_ge(turned[j], n1)
                    wait_free(act, kv_done[j], i)
                    nc.scalar.copy(xt[j], bank[2 + j][:, 0:2 * R]).then_inc(xt_ready[j], 1)

                def store_queries(pair_at, j):
                    if pair_at is None:
                        return
                    i, n1 = pair_at
                    act.wait_ge(q_out[j], n1)
                    act.dma_start(q_rows[bass.ds((2 * i + j) * R, R), :], qn[j]).then_inc(q_stored[j], 16)

                def turn(i):
                    for part, source, arrived in ((pack2, pack2_h, in_params2), (cst[:, 128:], packc_h[:, 128:], in_cst)):
                        w = part.shape[1] // PAIRS
                        if not isinstance(i, int) or i < PAIRS:
                            act.dma_start(part[:, bass.ds(i * w, w)], source[:, bass.ds(i * w, w)]).then_inc(arrived, 16)
                    last, this = at(act, i, -1), at(act, i)
                    copy_rows(this, 0)
                    store_queries(last, 0)
                    copy_rows(this, 1)
                    store_queries(last, 1)

                run_turns(act, turn, behind=1)

            @block.gpsimd
            def _(pool):
                nc.gpsimd.memset(v_rep[:, :], 0.0).then_inc(zero_ready, 1)
                nc.gpsimd.memset(zeros, 0.0).then_inc(zero_ready, 1)
                for j in range(2):
                    nc.gpsimd.memset(qx[j], 0.0).then_inc(zero_ready, 1)
                for j in range(2):
                    nc.gpsimd.memset(prob[j], 0.0).then_inc(zero_ready, 1)
                pool.wait_ge(setup, 2)

                def turn(i):
                    for j in range(2):
                        norm_power(pool, j, stats[2], powered, at(pool, i)[1])

                run_turns(pool, turn)
                pool.wait_ge(zero_ready, 6)

        with phase():
            pt = [wc(HH * R, PR) for _ in range(2)]
            q_turned = pair("q_turned")
            q_copied = pair("q_copied")
            k_block = pair("k_block")
            v_block = pair("v_block")
            with_bo = pair("with_bo")
            scored = pair("scored")
            maxed = pair("maxed")
            shifted = pair("shifted")
            exped = pair("exped")
            row_sum = pair("row_sum")
            row_inv = pair("row_inv")
            scaled = pair("scaled")
            p_turned = [pair(f"p_turned{half}_") for half in range(2)]
            p_copied = [pair(f"p_copied{half}_") for half in range(2)]
            mixed_v = pair("mixed_v")
            o_copied = pair("o_copied")
            projected = pair("projected")
            added = pair("added")
            stats = [pair("st"), pair("ag"), pair("ve")]
            powered = pair("powered")
            normed = pair("normed")
            turned = pair("turned")
            xt_ready = pair("xt_ready")
            x_saved = pair("x_saved")
            logits = pair("logits")
            logits_out = pair("logits_out")
            ot = [q[:, 0:2 * R] for q in (ph2_carve(2 * R), ph2_carve(2 * R))]
            hbo = [ph2_carve(D, R) for _ in range(2)]
            block = enter(nc.Block())

            def by_head(ap, heads=HH):
                return ap.rearrange("p (h s) -> p h s", h=heads)[:, :, 0:TOK]

            @block.sync
            def _(sp):
                def turn(i):
                    for j in range(2):
                        wait_free(sp, q_turned[j], i)
                        sp.wait_ge(q_stored[j], 16 * i + 16)
                        load_queries(sp, i, j)

                turn(1)
                with sp.Fori(2, PAIRS) as i:
                    turn(i)

            @block.tensor
            def _(pe):
                pe.wait_ge(in_params2, 16 * PAIRS)
                w_o = p2("w_o").rearrange("p (c n) -> p c n", c=2)
                proj = p2("proj").rearrange("p (c n) -> p c n", c=2)

                def turn_queries(pair_at, j):
                    if pair_at is None:
                        return
                    i, n1 = pair_at
                    pe.wait_ge(q_in[j], 16 * 2 * IPT * n1)
                    other_slot_free(pe, q_copied, pair_at, j, 2)
                    for half in range(2):
                        for k in range(HC // 2):
                            a = (half * HC // 2 + k) * KR
                            mm = nc.tensor.transpose(bank[2 + half][0:KR, k * R:(k + 1) * R], qx[j][:, a:a + KR],
                                                     ident[0:R, 0:R])
                    mm.then_inc(q_turned[j], 1)

                def scores(pair_at, j):
                    if pair_at is None:
                        return
                    i, n1 = pair_at
                    pe.wait_ge(q_copied[j], 2 * n1)
                    pe.wait_ge(k_block[j], n1)
                    other_slot_free(pe, shifted, pair_at, j)
                    for k in range(HC):
                        a = k % (HC // 2) * 2 * HP
                        mm = nc.tensor.matmul(by_head(bank[k // (HC // 2)][0:R, a:a + 2 * HP], 2), qm[j][:, k * R:(k + 1) * R],
                                              kb[j].rearrange("p (h s) -> p h s", h=2), start=True, stop=True)
                    mm.then_inc(scored[j], 1)

                def turn_probs(pair_at, j):
                    if pair_at is None:
                        return
                    i, n1 = pair_at
                    pe.wait_ge(scaled[j], n1)
                    for half in range(2):
                        last = (o_copied, added)[half]
                        if j:
                            pe.wait_ge(last[0], n1)
                        else:
                            wait_free(pe, last[1], i)
                        for k in range(HH // 2):
                            a = (half * HH + 2 * k) * HP
                            mm = nc.tensor.transpose(bank[4 + half][0:PR, k * R:(k + 1) * R], prob[j][:, a:a + PR],
                                                     ident[0:R, 0:R])
                        mm.then_inc(p_turned[half][j], 1)

                def mix_values(pair_at, j):
                    if pair_at is None:
                        return
                    i, n1 = pair_at
                    pe.wait_ge(v_block[j], n1)
                    for half in range(2):
                        pe.wait_ge(p_copied[half][j], n1)
                        for m in range(IPT):
                            for k in range(HH // 2):
                                a = (half * HH // 2 + k) * R + m * TOK
                                mm = nc.tensor.matmul(
                                    bank[4][32 * k:32 * (k + 1), half * R + m * TOK:half * R + (m + 1) * TOK],
                                    vb[j][:, m * 32:(m + 1) * 32], pt[j][:, a:a + TOK], start=True, stop=True)
                    mm.then_inc(mixed_v[j], 1)

                def project(pair_at, j):
                    if pair_at is None:
                        return
                    i, n1 = pair_at
                    pe.wait_ge(o_copied[j], n1)
                    for k in range(2):
                        mm = nc.tensor.matmul(bank[5][0:R, 0:D], ot[j][:, k * R:(k + 1) * R],
                                              w_o[:, k, :], start=(k == 0), stop=(k == 1))
                    mm.then_inc(projected[j], 1)

                def turn_rows(pair_at, j):
                    if pair_at is None:
                        return
                    i, n1 = pair_at
                    pe.wait_ge(normed[j], n1)
                    if j:
                        pe.wait_ge(logits_out[0], n1)
                    else:
                        wait_free(pe, logits_out[1], i)
                    for k in range(2):
                        mm = nc.tensor.transpose(bank[7][:, k * R:(k + 1) * R], xn[j][:, k * 128:(k + 1) * 128],
                                                 ident[0:R, 0:R])
                    mm.then_inc(turned[j], 1)

                def gate_logits(pair_at, j):
                    if pair_at is None:
                        return
                    i, n1 = pair_at
                    pe.wait_ge(xt_ready[j], n1)
                    for k in range(2):
                        mm = nc.tensor.matmul(bank[7][0:R, 2 * R:2 * R + E0], xt[j][:, k * R:(k + 1) * R],
                                              proj[:, k, :], start=(k == 0), stop=(k == 1))
                    mm.then_inc(logits[j], 1)

                def turn(i):
                    last, this, following = at(pe, i, -1), at(pe, i), at(pe, i, 1)
                    scores(this, 0)
                    turn_probs(last, 1)
                    turn_queries(this, 1)
                    mix_values(last, 1)
                    turn_rows(last, 0)
                    project(last, 1)
                    gate_logits(last, 0)
                    scores(this, 1)
                    turn_probs(this, 0)
                    turn_queries(following, 0)
                    mix_values(this, 0)
                    turn_rows(last, 1)
                    project(this, 0)
                    gate_logits(last, 1)

                run_turns(pe, turn, ahead=1, behind=1)

            @block.vector
            def _(dve):
                def shift_scores(pair_at, j):
                    if pair_at is None:
                        return
                    i, n1 = pair_at
                    dve.wait_ge(scored[j], n1)
                    for half in range(2):
                        mx = nc.vector.tensor_reduce(small[j][:, half * HH:(half + 1) * HH],
                                                     by_head(bank[half][0:R, :]), AX_X, ALU.max)
                    mx.then_inc(maxed[j], 1)
                    dve.wait_ge(maxed[j], n1)
                    for half in range(2):
                        sub = nc.vector.tensor_tensor(
                            by_head(prob[j][:, half * HH * HP:(half + 1) * HH * HP]), by_head(bank[half][0:R, :]),
                            small[j][:, half * HH:(half + 1) * HH].unsqueeze(2).broadcast_to([R, HH, TOK]), ALU.subtract)
                    sub.then_inc(shifted[j], 1)

                def sum_probs(pair_at, j):
                    if pair_at is None:
                        return
                    i, n1 = pair_at
                    dve.wait_ge(exped[j], n1)
                    nc.vector.tensor_reduce(small[j][:, NH:2 * NH], by_head(prob[j], NH), AX_X,
                                            ALU.add).then_inc(row_sum[j], 1)
                    dve.wait_ge(row_sum[j], n1)
                    nc.vector.reciprocal(small[j][:, 2 * NH:3 * NH], small[j][:, NH:2 * NH]).then_inc(row_inv[j], 1)

                def add_projection(pair_at, j):
                    if pair_at is None:
                        return
                    i, n1 = pair_at
                    h = tokens[0:R, bass.ds((2 * i + j) * RW, D)]
                    dve.wait_ge(projected[j], n1)
                    dve.wait_ge(with_bo[j], n1)
                    nc.vector.tensor_tensor(h, bank[5][0:R, 0:D], hbo[j], ALU.add).then_inc(added[j], 1)
                    norm_stats(dve, h, j, stats, n1, added)

                def normalise(pair_at, j):
                    if pair_at is None:
                        return
                    i, n1 = pair_at
                    dve.wait_ge(powered[j], n1)
                    wait_free(dve, turned[j], i)
                    norm_apply(xn[j], tokens[0:R, bass.ds((2 * i + j) * RW, D)], j).then_inc(normed[j], 1)

                def keep_logits(pair_at, j):
                    if pair_at is None:
                        return
                    i, n1 = pair_at
                    dve.wait_ge(logits[j], n1)
                    nc.vector.tensor_copy(lg0[:, bass.ds((2 * i + j) * E0, E0)],
                                          bank[7][0:R, 2 * R:2 * R + E0]).then_inc(logits_out[j], 1)

                def turn(i):
                    last, this = at(dve, i, -1), at(dve, i)
                    shift_scores(this, 0)
                    normalise(last, 0)
                    sum_probs(this, 0)
                    add_projection(last, 1)
                    keep_logits(last, 0)
                    shift_scores(this, 1)
                    normalise(last, 1)
                    sum_probs(this, 1)
                    add_projection(this, 0)
                    keep_logits(last, 1)

                run_turns(dve, turn, behind=1)

            @block.scalar
            def _(act):
                def copy_probs(pair_at, j):
                    if pair_at is None:
                        return
                    i, n1 = pair_at
                    for half in range(2):
                        act.wait_ge(p_turned[half][j], n1)
                        wait_free(act, mixed_v[j], i)
                        nc.scalar.copy(pt[j][:, half * HH // 2 * R:(half + 1) * HH // 2 * R],
                                       bank[4 + half][0:PR, 0:HH // 2 * R]).then_inc(p_copied[half][j], 1)

                def copy_queries(pair_at, j):
                    if pair_at is None:
                        return
                    i, n1 = pair_at
                    act.wait_ge(q_turned[j], n1)
                    wait_free(act, scored[j], i)
                    for half in range(2):
                        w = HC // 2 * R
                        nc.scalar.mul(qm[j][:, half * w:(half + 1) * w], bank[2 + half][0:KR, 0:w],
                                      HD ** -0.5).then_inc(q_copied[j], 1)

                def exponentials(pair_at, j):
                    if pair_at is None:
                        return
                    i, n1 = pair_at
                    act.wait_ge(shifted[j], n1)
                    nc.scalar.activation(by_head(prob[j], NH), by_head(prob[j], NH), ACT.Exp).then_inc(exped[j], 1)

                def copy_output(pair_at, j):
                    if pair_at is None:
                        return
                    i, n1 = pair_at
                    act.wait_ge(mixed_v[j], n1)
                    wait_free(act, projected[j], i)
                    nc.scalar.copy(ot[j], bank[4][:, 0:2 * R]).then_inc(o_copied[j], 1)

                def copy_rows(pair_at, j):
                    if pair_at is None:
                        return
                    i, n1 = pair_at
                    act.wait_ge(turned[j], n1)
                    wait_free(act, x_saved[j], i)
                    wait_free(act, logits[j], i)
                    nc.scalar.copy(xt[j], bank[7][:, 0:2 * R]).then_inc(xt_ready[j], 1)

                def save_rows(pair_at, j):
                    if pair_at is None:
                        return
                    i, n1 = pair_at
                    act.wait_ge(xt_ready[j], n1)
                    nc.scalar.copy(x_t.rearrange("p (k n) -> p k n", k=2)[:, :, bass.ds((2 * i + j) * R, R)],
                                   xt[j].rearrange("p (k n) -> p k n", k=2)).then_inc(x_saved[j], 1)

                def turn(i):
                    last, this, following = at(act, i, -1), at(act, i), at(act, i, 1)
                    copy_probs(last, 1)
                    copy_queries(this, 1)
                    copy_output(last, 1)
                    exponentials(this, 0)
                    copy_rows(last, 0)
                    save_rows(last, 0)
                    copy_probs(this, 0)
                    copy_queries(following, 0)
                    copy_output(this, 0)
                    exponentials(this, 1)
                    copy_rows(last, 1)
                    save_rows(last, 1)

                run_turns(act, turn, ahead=1, behind=1)

            @block.gpsimd
            def _(pool):
                pool.wait_ge(in_params2, 16 * PAIRS)

                def spread_keys(pair_at, j):
                    if pair_at is None:
                        return
                    i, n1 = pair_at
                    wait_free(pool, scored[j], i)
                    nc.gpsimd.tensor_tensor(
                        kb[j].rearrange("p (h s) -> p h s", h=2),
                        k_rep[:, bass.ds((2 * i + j) * TOK, TOK)].unsqueeze(1).broadcast_to([KR, 2, TOK]),
                        p2("mask_head", KR).unsqueeze(2).broadcast_to([KR, 2, TOK]), ALU.mult).then_inc(k_block[j], 1)

                def spread_values(pair_at, j):
                    if pair_at is None:
                        return
                    i, n1 = pair_at
                    wait_free(pool, mixed_v[j], i)
                    nc.gpsimd.tensor_tensor(
                        vb[j].rearrange("p (m h d) -> p m h d", m=IPT, h=2),
                        v_rep[:, bass.ds((2 * i + j) * IPT * HD, IPT * HD)].rearrange("p (m d) -> p m d", m=IPT)
                        .unsqueeze(2).broadcast_to([PR, IPT, 2, HD]),
                        p2("mask_pair", PR).unsqueeze(1).unsqueeze(3).broadcast_to([PR, IPT, 2, HD]),
                        ALU.mult).then_inc(v_block[j], 1)
                    wait_free(pool, added[j], i)
                    nc.gpsimd.tensor_tensor(hbo[j], tokens[0:R, bass.ds((2 * i + j) * RW, D)], p2("b_o", R),
                                            ALU.add).then_inc(with_bo[j], 1)

                def scale_probs(pair_at, j):
                    if pair_at is None:
                        return
                    i, n1 = pair_at
                    pool.wait_ge(row_inv[j], n1)
                    nc.gpsimd.tensor_tensor(
                        by_head(prob[j], NH), by_head(prob[j], NH),
                        small[j][:, 2 * NH:3 * NH].unsqueeze(2).broadcast_to([R, NH, TOK]), ALU.mult).then_inc(scaled[j], 1)

                def power(pair_at, j):
                    if pair_at is not None:
                        norm_power(pool, j, stats[2], powered, pair_at[1])

                def turn(i):
                    last, this, following = at(pool, i, -1), at(pool, i), at(pool, i, 1)
                    spread_keys(this, 1)
                    spread_values(this, 0)
                    scale_probs(this, 0)
                    power(last, 1)
                    spread_keys(following, 0)
                    spread_values(this, 1)
                    scale_probs(this, 1)
                    power(this, 0)

                run_turns(pool, turn, ahead=1, behind=1)

        with phase():
            chain = psem("chain")
            var_ready = psem("var_ready")
            std_ready = psem("std_ready")
            delta_ready = psem("delta_ready")
            root_ready = psem("root_ready")
            gates_ready = psem("gates_ready")
            gates_turned = psem("gates_turned")
            decay_ready = psem("decay_ready")
            lags_ready = psem("lags_ready")
            NG = NT * E0
            ec = carver(arena_w1, n1w + n2w)
            lt, ln = ec(H1 * R, R), ec(H1 * R, R)
            dec = ec(2 * H1, R)
            beta = ec(NT * H1, R)
            nk = ec(NT * H1 * TOK, R)
            z, zs, zr, s1, s2, t1 = (ec(NG, R) for _ in range(6))
            m1, m2 = ec(NT, R), ec(NT, R)
            block = enter(nc.Block())

            def grp(ap):
                return ap.rearrange("p (t e) -> p t e", t=NT)

            def wide(ap):
                return ap.unsqueeze(2).broadcast_to([R, NT, E0])

            @block.vector
            def _(dve):
                count = [0]

                def link(ins):
                    count[0] += 1
                    ins.then_inc(chain, 1)
                    dve.wait_ge(chain, count[0])

                tt, ts, red = nc.vector.tensor_tensor, nc.vector.tensor_scalar, nc.vector.tensor_reduce
                link(red(m1, grp(lg0), AX_X, ALU.add))
                link(ts(m2, m1, 1.0 / E0, None, ALU.mult))
                link(tt(grp(z), grp(lg0), wide(m2), ALU.subtract))
                link(tt(t1, z, z, ALU.mult))
                link(red(m1, grp(t1), AX_X, ALU.add))
                ts(m2, m1, 1.0 / E0, EPS, ALU.mult, ALU.add).then_inc(var_ready, 1)
                dve.wait_ge(std_ready, 1)
                link(nc.vector.reciprocal(m2, m1))
                link(tt(grp(z), grp(z), wide(m2), ALU.mult))
                link(red(m1, grp(z), AX_X, ALU.max))
                link(tt(grp(t1), grp(z), wide(m1), ALU.subtract))
                link(ts(z, t1, 0.5, None, ALU.mult))
                for t in range(NT):
                    last = nc.vector.max(zs[:, t * E0:t * E0 + 8], z[:, t * E0:(t + 1) * E0])
                link(last)
                for t in range(NT):
                    last = nc.vector.match_replace(zr[:, t * E0:(t + 1) * E0], zs[:, t * E0:t * E0 + 8],
                                                   z[:, t * E0:(t + 1) * E0], -1e30)
                link(last)
                for t in range(NT):
                    last = nc.vector.max(zs[:, t * E0 + 8:(t + 1) * E0], zr[:, t * E0:(t + 1) * E0])
                link(last)
                link(tt(t1, zs, zs, ALU.mult))
                link(nc.vector.tensor_tensor_scan(s1, p2("seg_e0", R), zs, 0.0, ALU.mult, ALU.add))
                link(nc.vector.tensor_tensor_scan(s2, p2("seg_e0", R), t1, 0.0, ALU.mult, ALU.add))
                link(tt(s1, s1, p2("inv_k", R), ALU.mult))
                link(tt(s2, s2, p2("inv_k", R), ALU.mult))
                link(tt(t1, s1, s1, ALU.mult))
                link(tt(s2, s2, t1, ALU.subtract))
                link(tt(t1, p2("inv_k", R), s2, ALU.subtract))
                ts(s2, t1, 0.0, None, ALU.max).then_inc(delta_ready, 1)
                dve.wait_ge(root_ready, 1)
                link(tt(s1, s1, t1, ALU.subtract))
                link(tt(t1, s1, zs, ALU.is_le))
                link(red(m1, grp(t1), AX_X, ALU.add))
                link(tt(grp(t1), grp(p2("rank_k", R)), wide(m1), ALU.is_equal))
                link(tt(t1, t1, s1, ALU.mult))
                link(red(m1, grp(t1), AX_X, ALU.add))
                link(tt(grp(t1), grp(z), wide(m1), ALU.subtract))
                nc.vector.scalar_tensor_tensor(z, t1, 0.0, t1, ALU.max, ALU.mult).then_inc(gates_ready, 1)
                for b in range(0, -(-NT // 4), 2):
                    n = min(4, NT - 4 * b)
                    dve.wait_ge(gates_turned, b + 1)
                    nc.vector.tensor_copy(gate_t[:, 4 * b * R:(4 * b + n) * R], bank[b][0:E0, 0:n * R])

            @block.gpsimd
            def _(pool):
                pool.wait_ge(lags_ready, H1)
                for h in range(H1):
                    nc.gpsimd.tensor_tensor(lt[:, h * R:(h + 1) * R], lt[:, h * R:(h + 1) * R], p2("keep_t", R), ALU.mult)
                    nc.gpsimd.tensor_tensor(ln[:, h * R:(h + 1) * R], ln[:, h * R:(h + 1) * R], p2("keep", R), ALU.mult)

            @block.scalar
            def _(act):
                act.wait_ge(var_ready, 1)
                nc.scalar.activation(m1, m2, ACT.Sqrt).then_inc(std_ready, 1)
                act.wait_ge(delta_ready, 1)
                nc.scalar.activation(t1, s2, ACT.Sqrt).then_inc(root_ready, 1)
                nc.scalar.activation(dec[:, 0:H1], p2("decay", R), ACT.Sigmoid).then_inc(decay_ready, 1)
                act.wait_ge(decay_ready, 1)
                nc.scalar.activation(dec[:, H1:2 * H1], dec[:, 0:H1], ACT.Ln).then_inc(decay_ready, 1)
                act.wait_ge(decay_ready, 2)
                for h in range(H1):
                    g = dec[:, H1 + h:H1 + h + 1]
                    nc.scalar.activation(lt[:, h * R:(h + 1) * R], p2("lag_t", R), ACT.Exp, scale=g)
                    nc.scalar.activation(ln[:, h * R:(h + 1) * R], p2("lag", R), ACT.Exp, scale=g).then_inc(lags_ready, 1)
                for b in range(1, -(-NT // 4), 2):
                    n = min(4, NT - 4 * b)
                    act.wait_ge(gates_turned, b + 1)
                    nc.scalar.copy(gate_t[:, 4 * b * R:(4 * b + n) * R], bank[b][0:E0, 0:n * R])

            @block.tensor
            def _(pe):
                pe.wait_ge(gates_ready, 1)
                for b in range(-(-NT // 4)):
                    n = min(4, NT - 4 * b)
                    for k in range(n):
                        t = 4 * b + k
                        mm = nc.tensor.transpose(bank[b][0:E0, k * R:(k + 1) * R], z[:, t * E0:(t + 1) * E0], ident[0:R, 0:R])
                    mm.then_inc(gates_turned, 1)

        with phase():
            (z1_done, g1_out, z1_gated, hid_done, hid_act, z2_done, g2_out, z2_gated, y_done, y_added) = (
                psem(n) for n in ("z1_done", "g1_out", "z1_gated", "hid_done", "hid_act", "z2_done", "g2_out", "z2_gated",
                                  "y_done", "y_added"))
            stats = [pair("st"), pair("ag"), pair("ve")]
            (powered, normed, sq_done, roots, rooted, floored, inverted, k_ready, turned, t_ready, v_done, g_done,
             v_out, n_masked, n_reduced) = (
                pair(n) for n in ("powered", "normed", "sq_done", "roots", "rooted", "floored", "inverted", "k_ready",
                                  "turned", "t_ready", "v_done", "g_done", "v_out", "n_masked", "n_reduced"))
            rows_free = pair("rows_free")
            W = 2 * R
            bc = carver(arena_w1, n1w + n2w + 2 * H1 * R + 2 * H1 + NT * H1 * (TOK + 1))
            z1, z2, g1, g2 = (bc(W) for _ in range(4))
            hid = bc(OC * W)
            cc = carver(arena_w1)
            kn = [cc(D, R) for _ in range(2)]
            xk = [cc(4 * R) for _ in range(2)]
            sq = [cc(D, R) for _ in range(2)]
            nf = [cc(H1 * R, R) for _ in range(2)]
            sc = [cc(12, R) for _ in range(2)]
            block = enter(nc.Block())
            HB = OC // 2

            @block.sync
            def _(sp):
                sp.dma_start(x_slots.rearrange("(p s) (e d) -> p (s e) d", p=128, e=2),
                             zeros.unsqueeze(1).broadcast_to([128, 2 * ST, RW // 2])).then_inc(zeros_out, 16)
                sp.dma_start(a_rows[:, B * TOK:, :].rearrange("h r i -> r h i"),
                             zeros[0:NT * R - B * TOK, 0:H1 * TOK].rearrange("r (h i) -> r h i", h=H1)).then_inc(zeros_out, 16)
                sp.wait_ge(zeros_out, 32)

            @block.tensor
            def _(pe):
                w_in1 = p2("w_in1").rearrange("p (c n) -> p c n", c=2)
                w_out1 = p2("w_out1").rearrange("p (c n) -> p c n", c=OC)
                w_in2 = p2("w_in2").rearrange("p (c n) -> p c n", c=OC)
                w_vb = p2("w_vb").rearrange("p (c n) -> p c n", c=2)

                def gates_of(name, i, place):
                    nc.tensor.matmul(bank[place][:, 0:W], p2(name, E0), gate_t[:, bass.ds(i * W, W)], start=True, stop=True)

                def first_products(pair_at):
                    if pair_at is None:
                        return
                    i, n1 = pair_at
                    wait_free(pe, z1_gated, i)
                    gates_of("c1", i, 0)
                    for k in range(2):
                        mm = nc.tensor.matmul(bank[0][:, W:2 * W], w_in1[:, k, :], x_t[:, bass.ds(i * W + k * NT * R, W)],
                                              start=(k == 0), stop=(k == 1))
                    mm.then_inc(z1_done, 1)

                def hidden(pair_at, chunks):
                    if pair_at is None:
                        return
                    i, n1 = pair_at
                    pe.wait_ge(z1_gated, n1)
                    for f in chunks:
                        if f % 4 == f and isinstance(i, int) and i == 0:
                            pass
                        elif f % 2 == 0:
                            pe.wait_ge(hid_act, i * HB + f // 2 - 1)
                        mm = nc.tensor.matmul(bank[2 + f // 2 % 2][:, (f % 2) * W:(f % 2 + 1) * W], w_out1[:, f, :], z1,
                                              start=True, stop=True)
                        if f % 2:
                            mm.then_inc(hid_done, 1)

                def second_products(pair_at):
                    if pair_at is None:
                        return
                    i, n1 = pair_at
                    wait_free(pe, z2_gated, i)
                    gates_of("c2", i, 1)
                    for f in range(OC):
                        if f % 2 == 0:
                            pe.wait_ge(hid_act, i * HB + f // 2 + 1)
                        mm = nc.tensor.matmul(bank[1][:, W:2 * W], w_in2[:, f, :], hid[:, f * W:(f + 1) * W],
                                              start=(f == 0), stop=(f == OC - 1))
                    mm.then_inc(z2_done, 1)

                def outputs(pair_at):
                    if pair_at is None:
                        return
                    i, n1 = pair_at
                    pe.wait_ge(z2_gated, n1)
                    wait_free(pe, y_added, i)
                    for j in range(2):
                        mm = nc.tensor.matmul(bank[4][0:R, j * D:(j + 1) * D], z2[:, j * R:(j + 1) * R], p2("w_out2"),
                                              start=True, stop=True)
                    mm.then_inc(y_done, 1)

                def turn_rows_and_keys(pair_at, j):
                    if pair_at is None:
                        return
                    i, n1 = pair_at
                    pe.wait_ge(normed[j], n1)
                    pe.wait_ge(k_ready[j], n1)
                    other_slot_free(pe, t_ready, pair_at, j)
                    for k in range(4):
                        src = (xn, kn)[k // 2][j][:, (k % 2) * 128:(k % 2 + 1) * 128]
                        mm = nc.tensor.transpose(bank[5][:, k * R:(k + 1) * R], src, ident[0:R, 0:R])
                    mm.then_inc(turned[j], 1)

                def row_products(pair_at, j):
                    if pair_at is None:
                        return
                    i, n1 = pair_at
                    pe.wait_ge(t_ready[j], n1)
                    other_slot_free(pe, v_out, pair_at, j)
                    for k in range(2):
                        mm = nc.tensor.matmul(bank[6][0:R, 0:D + H1], xk[j][:, k * R:(k + 1) * R], w_vb[:, k, :],
                                              start=(k == 0), stop=(k == 1))
                    mm.then_inc(v_done[j], 1)
                    other_slot_free(pe, n_masked, pair_at, j)
                    for h in range(H1):
                        kt = xk[j][:, (2 + h) * R:(3 + h) * R]
                        mm = nc.tensor.matmul(bank[7][0:R, h * R:(h + 1) * R], kt, kt, start=True, stop=True)
                    mm.then_inc(g_done[j], 1)

                def turn(i):
                    before_last, last, this = at(pe, i, -2), at(pe, i, -1), at(pe, i)
                    second_products(last)
                    turn_rows_and_keys(before_last, 0)
                    first_products(this)
                    row_products(before_last, 0)
                    outputs(last)
                    hidden(this, range(OC // 2))
                    turn_rows_and_keys(before_last, 1)
                    hidden(this, range(OC // 2, OC))
                    row_products(before_last, 1)

                run_turns(pe, turn, behind=2)

            @block.scalar
            def _(act):
                def activate(pair_at, chunk_pairs):
                    if pair_at is None:
                        return
                    i, n1 = pair_at
                    wait_free(act, z2_done, i)
                    for f in chunk_pairs:
                        act.wait_ge(hid_done, i * HB + f + 1)
                        nc.scalar.activation(hid[:, 2 * f * W:2 * (f + 1) * W], bank[2 + f % 2][:, 0:2 * W],
                                             ACT.Gelu).then_inc(hid_act, 1)

                def scale_keys(pair_at, j):
                    if pair_at is None:
                        return
                    i, n1 = pair_at
                    act.wait_ge(inverted[j], n1)
                    wait_free(act, turned[j], i)
                    for g in range(H1):
                        kk = nc.scalar.activation(kn[j][:, g * 128:(g + 1) * 128], xn[j][:, g * 128:(g + 1) * 128],
                                                  ACT.Copy, scale=sc[j][:, 4 + g:5 + g])
                    kk.then_inc(k_ready[j], 1)

                def keep_values(pair_at, j):
                    if pair_at is None:
                        return
                    i, n1 = pair_at
                    act.wait_ge(v_done[j], n1)
                    nc.scalar.copy(tokens[0:R, bass.ds((2 * i + j) * RW + D, D)], bank[6][0:R, 0:D])
                    nc.scalar.copy(beta[:, bass.ds((2 * i + j) * H1, H1)], bank[6][0:R, D:D + H1]).then_inc(v_out[j], 1)

                def copy_rows_and_keys(pair_at, j):
                    if pair_at is None:
                        return
                    i, n1 = pair_at
                    act.wait_ge(turned[j], n1)
                    wait_free(act, g_done[j], i)
                    nc.scalar.copy(xk[j], bank[5][:, 0:4 * R]).then_inc(t_ready[j], 1)

                def turn(i):
                    before_last, last, this = at(act, i, -2), at(act, i, -1), at(act, i)
                    copy_rows_and_keys(before_last, 0)
                    scale_keys(before_last, 1)
                    keep_values(before_last, 0)
                    activate(this, range(HB // 2))
                    copy_rows_and_keys(before_last, 1)
                    activate(this, range(HB // 2, HB))
                    scale_keys(last, 0)
                    keep_values(before_last, 1)

                run_turns(act, turn, behind=2)
                for j in range(2):
                    act.wait_ge(v_out[j], PAIRS)
                nc.scalar.activation(beta, beta, ACT.Sigmoid)

            @block.vector
            def _(dve):
                for j in range(2):
                    nc.vector.memset(sc[j][:, 6:8], 0.5).then_inc(rows_free[j], 1)

                def gate_first(pair_at):
                    if pair_at is None:
                        return
                    i, n1 = pair_at
                    dve.wait_ge(z1_done, n1)
                    nc.vector.tensor_copy(g1, bank[0][:, 0:W]).then_inc(g1_out, 1)
                    dve.wait_ge(g1_out, n1)
                    wait_free(dve, hid_done, i * HB)
                    nc.vector.scalar_tensor_tensor(z1, bank[0][:, W:2 * W], p2("b_in1"), g1,
                                                   ALU.add, ALU.mult).then_inc(z1_gated, 1)

                def gate_second(pair_at):
                    if pair_at is None:
                        return
                    i, n1 = pair_at
                    dve.wait_ge(z2_done, n1)
                    nc.vector.tensor_copy(g2, bank[1][:, 0:W]).then_inc(g2_out, 1)
                    dve.wait_ge(g2_out, n1)
                    wait_free(dve, y_done, i)
                    nc.vector.scalar_tensor_tensor(z2, bank[1][:, W:2 * W], p2("b_in2"), g2,
                                                   ALU.add, ALU.mult).then_inc(z2_gated, 1)

                def add_outputs(pair_at):
                    if pair_at is None:
                        return
                    i, n1 = pair_at
                    dve.wait_ge(y_done, n1)
                    h = tokens[0:R, bass.ds(i * 2 * RW, 2 * RW)].rearrange("p (j n) -> p j n", j=2)[:, :, 0:D]
                    nc.vector.tensor_tensor(h, h, bank[4][0:R, 0:2 * D].rearrange("p (j n) -> p j n", j=2),
                                            ALU.add).then_inc(y_added, 1)
                    stand_alone(dve)
                    dve.wait_ge(y_added, n1)

                def row(pair_at, j):
                    return tokens[0:R, bass.ds((2 * pair_at[0] + j) * RW, D)]

                def normalise(pair_at, j):
                    if pair_at is None:
                        return
                    i, n1 = pair_at
                    norm_stats(dve, row(pair_at, j), j, stats, n1, rows_free)
                    dve.wait_ge(powered[j], n1)
                    wait_free(dve, turned[j], i)
                    norm_apply(xn[j], row(pair_at, j), j).then_inc(normed[j], 1)

                def key_squares(pair_at, j):
                    if pair_at is None:
                        return
                    i, n1 = pair_at
                    dve.wait_ge(sq_done[j], n1)
                    nc.vector.tensor_reduce(sc[j][:, 0:2], sq[j].rearrange("p (h d) -> p h d", h=H1), AX_X,
                                            ALU.add).then_inc(roots[j], 1)

                def key_inverses(pair_at, j):
                    if pair_at is None:
                        return
                    i, n1 = pair_at
                    dve.wait_ge(rooted[j], n1)
                    nc.vector.tensor_scalar(sc[j][:, 2:4], sc[j][:, 8:10], 1e-12, None, ALU.max).then_inc(floored[j], 1)
                    dve.wait_ge(floored[j], n1)
                    wait_free(dve, k_ready[j], i)
                    nc.vector.reciprocal(sc[j][:, 4:6], sc[j][:, 2:4]).then_inc(inverted[j], 1)

                def decay_products(pair_at, j):
                    if pair_at is None:
                        return
                    i, n1 = pair_at
                    dve.wait_ge(g_done[j], n1)
                    nc.vector.tensor_tensor(attn_t[:, bass.ds((2 * i + j) * H1 * R, H1 * R)], bank[7][0:R, 0:H1 * R],
                                            lt, ALU.mult)
                    nc.vector.tensor_tensor(nf[j], bank[7][0:R, 0:H1 * R], ln, ALU.mult).then_inc(n_masked[j], 1)
                    dve.wait_ge(n_masked[j], n1)
                    nc.vector.tensor_reduce(
                        nk[:, bass.ds((2 * i + j) * H1 * TOK, H1 * TOK)].rearrange("p (h t) -> p h t", h=H1),
                        nf[j].rearrange("p (h m t) -> p h t m", h=H1, m=IPT), AX_X, ALU.add).then_inc(n_reduced[j], 1)

                def turn(i):
                    before_last, last, this = at(dve, i, -2), at(dve, i, -1), at(dve, i)
                    normalise(before_last, 1)
                    gate_second(last)
                    key_squares(before_last, 1)
                    gate_first(this)
                    key_inverses(before_last, 1)
                    decay_products(before_last, 0)
                    add_outputs(last)
                    normalise(last, 0)
                    key_squares(last, 0)
                    key_inverses(last, 0)
                    decay_products(before_last, 1)

                run_turns(dve, turn, behind=2)

            @block.gpsimd
            def _(pool):
                def prepare_keys(pair_at, j):
                    if pair_at is None:
                        return
                    i, n1 = pair_at
                    norm_power(pool, j, stats[2], powered, n1)
                    pool.wait_ge(normed[j], n1)
                    nc.gpsimd.tensor_tensor(sq[j], xn[j], xn[j], ALU.mult).then_inc(sq_done[j], 1)
                    pool.wait_ge(roots[j], n1)
                    nc.gpsimd.tensor_tensor(sc[j][:, 8:10], sc[j][:, 0:2], sc[j][:, 6:8], ALU.pow).then_inc(rooted[j], 1)
                    h = tokens[0:R, bass.ds((2 * i + j) * RW, D)]
                    nc.gpsimd.tensor_tensor(h, h, xn[j], ALU.add).then_inc(rows_free[j], 1)

                def turn(i):
                    before_last, last = at(pool, i, -2), at(pool, i, -1)
                    prepare_keys(before_last, 1)
                    prepare_keys(last, 0)

                run_turns(pool, turn, behind=2)

        with phase():
            n_scaled = psem("n_scaled")
            n_stored = psem("n_stored")
            beta_masked = psem("beta_masked")
            n_in = psem("n_in")
            chain = pair("chain")
            zeroed = psem("zeroed")
            solved = psem("solved")
            a_stored = psem("a_stored")
            prod = [work[:, 0:TOK * TOK], work[:, TOK * TOK:2 * TOK * TOK]]
            block = enter(nc.Block())

            def systems(rows, h):
                return rows[h, 0:B * TOK, :].rearrange("(b i) j -> b (i j)", b=B)

            @block.gpsimd
            def _(pool):
                nc.gpsimd.tensor_tensor(beta_img.rearrange("p (a m) -> p a m", m=IPT),
                                        beta.unsqueeze(2).broadcast_to([R, NT * H1, IPT]),
                                        c("mask_img", R).unsqueeze(1).broadcast_to([R, NT * H1, IPT]),
                                        ALU.mult).then_inc(beta_masked, 1)
                pool.wait_ge(beta_masked, 1)

            @block.sync
            def _(sp):
                for h in range(H1):
                    sp.wait_ge(n_scaled, h + 1)
                    sp.dma_start(n_rows[h].rearrange("(t p) n -> p t n", p=R),
                                 nk.rearrange("p (t h n) -> p t h n", t=NT, h=H1)[:, :, h, :]).then_inc(n_stored, 16)
                sp.wait_ge(n_stored, 16 * H1)
                for h in range(H1):
                    sp.dma_start(sys_n[h * B:(h + 1) * B, :],
                                 systems(n_rows, h)).then_inc(n_in, 16)
                sp.dma_start(arena_w2[:, 0:W2S // 2], w2_h[:, 0:W2S // 2]).then_inc(w2a_in, 16)
                sp.wait_ge(beta_masked, 1)
                sp.dma_start(arena_w1[:, :], w1_h).then_inc(w1_in, 16)
                sp.wait_ge(solved, 1)
                for h in range(H1):
                    sp.dma_start(systems(a_rows, h),
                                 sys_x[h * B:(h + 1) * B, :]).then_inc(a_stored, 16)
                sp.wait_ge(a_stored, 16 * H1)

            @block.vector
            def _(dve):
                for h in range(H1):
                    rows = nk.rearrange("p (t h j) -> p t h j", t=NT, h=H1)[:, :, h, :]
                    nc.vector.tensor_tensor(rows, rows, beta.rearrange("p (t h) -> p t h", t=NT)[:, :, h:h + 1]
                                            .broadcast_to([R, NT, TOK]), ALU.mult).then_inc(n_scaled, 1)
                x = sys_x.rearrange("p (c i) -> p c i", c=TOK)
                n = sys_n.rearrange("p (i j) -> p i j", i=TOK)
                nc.vector.memset(sys_x, 0.0).then_inc(zeroed, 1)
                dve.wait_ge(zeroed, 1)
                nc.vector.memset(sys_x[:, 0:TOK * TOK:TOK + 1], 1.0).then_inc(zeroed, 1)
                dve.wait_ge(zeroed, 2)
                dve.wait_ge(n_in, 16 * H1)
                last_cut = 0
                steps = [0, 0]
                for i in range(1, TOK):
                    cut = CUTS[i]
                    if cut != last_cut and steps[0]:
                        dve.wait_ge(chain[0], steps[0])
                        if steps[1]:
                            dve.wait_ge(chain[1], steps[1])
                        last_cut = cut
                    parts = [(0, 0, cut), (1, cut, i)] if cut < i else [(0, 0, i)]
                    products = []
                    for which, c0, c1 in parts:
                        w = prod[which][:, 0:(c1 - c0) * (i - c0)].rearrange("p (c j) -> p c j", c=c1 - c0)
                        products.append(w)
                        if steps[which]:
                            dve.wait_ge(chain[which], steps[which])
                        nc.vector.tensor_tensor(w, x[:, c0:c1, c0:i],
                                                n[:, i, c0:i].unsqueeze(1).broadcast_to([128, c1 - c0, i - c0]),
                                                ALU.mult).then_inc(chain[which], 1)
                        steps[which] += 1
                    for (which, c0, c1), w in zip(parts, products):
                        dve.wait_ge(chain[which], steps[which])
                        nc.vector.tensor_reduce(x[:, c0:c1, i], w, AX_X, ALU.add).then_inc(chain[which], 1)
                        steps[which] += 1
                for which in range(2):
                    dve.wait_ge(chain[which], steps[which])
                nc.vector.engine_nop().then_inc(solved, 1)

        with phase():
            stats = [pair("st"), pair("ag"), pair("ve")]
            (a_in, a_block, vn_done, vn_out, o_done, o_out, r_done, added, powered, normed, turned, xt_ready, logits,
             logits_out, x_kept) = (
                pair(n) for n in ("a_in", "a_block", "vn_done", "vn_out", "o_done", "o_out", "r_done", "added",
                                      "powered", "normed", "turned", "xt_ready", "logits", "logits_out", "x_kept"))
            setup = psem("setup")
            wc = carver(work)
            lgr = wc(NT * NE, R)
            xn = [wc(D, R) for _ in range(2)]
            xt = [wc(2 * R) for _ in range(2)]
            st = [wc(8, R) for _ in range(2)]
            ve = [wc(4, R) for _ in range(2)]
            ac = [wc(H1 * TOK, R) for _ in range(2)]
            ab = [wc(H1 * R, R) for _ in range(2)]
            vn = [wc(D, R) for _ in range(2)]
            ot = [wc(H1 * R) for _ in range(2)]
            block = enter(nc.Block())

            @block.sync
            def _(sp):
                def turn(i):
                    for j in range(2):
                        wait_free(sp, a_block[j], i)
                        sp.dma_start(ac[j].rearrange("p (h t) -> p h t", h=H1),
                                     a_rows[:, bass.ds((2 * i + j) * R, R), :].rearrange("h r t -> r h t")).then_inc(a_in[j], 16)

                run_turns(sp, turn)

            @block.gpsimd
            def _(pool):
                pool.wait_ge(in_cst, 16 * PAIRS)
                pool.wait_ge(setup, 2)

                def spread_inverses(pair_at, j):
                    if pair_at is None:
                        return
                    i, n1 = pair_at
                    pool.wait_ge(a_in[j], 16 * n1)
                    wait_free(pool, vn_done[j], i)
                    nc.gpsimd.tensor_tensor(
                        ab[j].rearrange("p (h m t) -> p h m t", h=H1, m=IPT),
                        ac[j].rearrange("p (h t) -> p h t", h=H1).unsqueeze(2).broadcast_to([R, H1, IPT, TOK]),
                        beta_img[:, bass.ds((2 * i + j) * H1 * IPT, H1 * IPT)].rearrange("p (h m) -> p h m", h=H1)
                        .unsqueeze(3).broadcast_to([R, H1, IPT, TOK]), ALU.mult).then_inc(a_block[j], 1)

                def power(pair_at, j):
                    if pair_at is not None:
                        norm_power(pool, j, stats[2], powered, pair_at[1])

                def turn(i):
                    last, this, following = at(pool, i, -1), at(pool, i), at(pool, i, 1)
                    power(last, 1)
                    spread_inverses(following, 0)
                    power(this, 0)
                    spread_inverses(following, 1)

                run_turns(pool, turn, ahead=1, behind=1)

            @block.tensor
            def _(pe):
                w_read = c("w_read").rearrange("p (c n) -> p c n", c=2)
                w_r = c("w_r").rearrange("p (c n) -> p c n", c=2)

                def solve_values(pair_at, j):
                    if pair_at is None:
                        return
                    i, n1 = pair_at
                    pe.wait_ge(a_block[j], n1)
                    wait_free(pe, vn_out[j], i)
                    for h in range(H1):
                        mm = nc.tensor.matmul(bank[j][0:R, h * 128:(h + 1) * 128], ab[j][:, h * R:(h + 1) * R],
                                              tokens[0:R, bass.ds((2 * i + j) * RW + D + h * 128, 128)], start=True, stop=True)
                    mm.then_inc(vn_done[j], 1)

                def attend(pair_at, j):
                    if pair_at is None:
                        return
                    i, n1 = pair_at
                    pe.wait_ge(vn_out[j], n1)
                    wait_free(pe, o_out[j], i)
                    for h in range(H1):
                        mm = nc.tensor.matmul(bank[2 + j][:, h * R:(h + 1) * R], vn[j][:, h * 128:(h + 1) * 128],
                                              attn_t[:, bass.ds(((2 * i + j) * H1 + h) * R, R)], start=True, stop=True)
                    mm.then_inc(o_done[j], 1)

                def read_out(pair_at, j):
                    if pair_at is None:
                        return
                    i, n1 = pair_at
                    pe.wait_ge(o_out[j], n1)
                    wait_free(pe, added[j], i)
                    for k in range(2):
                        mm = nc.tensor.matmul(bank[4 + j][0:R, 0:D], ot[j][:, k * R:(k + 1) * R], w_read[:, k, :],
                                              start=(k == 0), stop=(k == 1))
                    mm.then_inc(r_done[j], 1)

                def turn_rows(pair_at, j):
                    if pair_at is None:
                        return
                    i, n1 = pair_at
                    pe.wait_ge(normed[j], n1)
                    wait_free(pe, logits_out[j], i)
                    for k in range(2):
                        mm = nc.tensor.transpose(bank[6 + j][:, k * R:(k + 1) * R], xn[j][:, k * 128:(k + 1) * 128],
                                                 ident[0:R, 0:R])
                    mm.then_inc(turned[j], 1)

                def router_logits(pair_at, j):
                    if pair_at is None:
                        return
                    i, n1 = pair_at
                    pe.wait_ge(xt_ready[j], n1)
                    for k in range(2):
                        mm = nc.tensor.matmul(bank[6 + j][0:R, 2 * R:2 * R + NE], xt[j][:, k * R:(k + 1) * R],
                                              w_r[:, k, :], start=(k == 0), stop=(k == 1))
                    mm.then_inc(logits[j], 1)

                def turn(i):
                    before_last, last, this = at(pe, i, -2), at(pe, i, -1), at(pe, i)
                    solve_values(this, 0)
                    read_out(last, 1)
                    turn_rows(before_last, 1)
                    attend(this, 0)
                    router_logits(before_last, 1)
                    solve_values(this, 1)
                    read_out(this, 0)
                    turn_rows(last, 0)
                    attend(this, 1)
                    router_logits(last, 0)

                run_turns(pe, turn, behind=2)

            @block.scalar
            def _(act):
                def copy_values(pair_at, j):
                    if pair_at is None:
                        return
                    i, n1 = pair_at
                    act.wait_ge(vn_done[j], n1)
                    wait_free(act, o_done[j], i)
                    nc.scalar.copy(vn[j], bank[j][0:R, 0:D]).then_inc(vn_out[j], 1)

                def copy_output(pair_at, j):
                    if pair_at is None:
                        return
                    i, n1 = pair_at
                    act.wait_ge(o_done[j], n1)
                    wait_free(act, r_done[j], i)
                    nc.scalar.copy(ot[j], bank[2 + j][:, 0:H1 * R]).then_inc(o_out[j], 1)

                def copy_rows(pair_at, j):
                    if pair_at is None:
                        return
                    i, n1 = pair_at
                    act.wait_ge(turned[j], n1)
                    wait_free(act, logits[j], i)
                    nc.scalar.copy(xt[j], bank[6 + j][:, 0:2 * R]).then_inc(xt_ready[j], 1)

                def keep_rows(pair_at, j):
                    if pair_at is None:
                        return
                    i, n1 = pair_at
                    act.wait_ge(normed[j], n1)
                    nc.scalar.copy(tokens[0:R, bass.ds((2 * i + j) * RW + D, D)], xn[j]).then_inc(x_kept[j], 1)

                def turn(i):
                    before_last, last, this = at(act, i, -2), at(act, i, -1), at(act, i)
                    copy_values(this, 0)
                    copy_rows(before_last, 1)
                    copy_output(this, 0)
                    keep_rows(last, 0)
                    copy_values(this, 1)
                    copy_rows(last, 0)
                    copy_output(this, 1)
                    keep_rows(last, 1)

                run_turns(act, turn, behind=2)

            @block.vector
            def _(dve):
                for j in range(2):
                    nc.vector.memset(ve[j][:, 2:3], -0.5).then_inc(setup, 1)

                def add_and_norm(pair_at, j):
                    if pair_at is None:
                        return
                    i, n1 = pair_at
                    h = tokens[0:R, bass.ds((2 * i + j) * RW, D)]
                    dve.wait_ge(r_done[j], n1)
                    nc.vector.tensor_tensor(h, h, bank[4 + j][0:R, 0:D], ALU.add).then_inc(added[j], 1)
                    norm_stats(dve, h, j, stats, n1, added)
                    dve.wait_ge(powered[j], n1)
                    wait_free(dve, turned[j], i)
                    wait_free(dve, x_kept[j], i)
                    norm_apply(xn[j], h, j).then_inc(normed[j], 1)

                def keep_logits(pair_at, j):
                    if pair_at is None:
                        return
                    i, n1 = pair_at
                    dve.wait_ge(logits[j], n1)
                    nc.vector.tensor_tensor(lgr[:, bass.ds((2 * i + j) * NE, NE)], bank[6 + j][0:R, 2 * R:2 * R + NE],
                                            c("b_r", R), ALU.add).then_inc(logits_out[j], 1)

                def turn(i):
                    before_last, last, this = at(dve, i, -2), at(dve, i, -1), at(dve, i)
                    add_and_norm(last, 1)
                    keep_logits(before_last, 1)
                    add_and_norm(this, 0)
                    keep_logits(last, 0)

                run_turns(dve, turn, behind=2)

        x_sent = psem("x_sent")
        with phase():
            chain = psem("chain")
            shifted_s = psem("shifted")
            exp_done = psem("exp_done")
            hot_ready = psem("hot_ready")
            counted = psem("counted")
            slots_ready = psem("slots_ready")
            NG = NT * NE
            rc = carver(work, NG)
            dl, ex, eq, cu, one_hot, cte, inc, tmp = (rc(NG, R) for _ in range(8))
            m1, m2, valid = rc(NT, R), rc(NT, R), rc(NT, R)
            cmp_t = rc(NE * MT, R)
            tiles_e, upto_e, off_e = rc(NE, R), rc(NE, R), rc(NE, R)
            past = rc(ST * NE, R)
            eno = rc(ST, R)
            block = enter(nc.Block())

            def by_tile(ap):
                return ap.rearrange("p (t e) -> p t e", t=NT)

            @block.sync
            def _(sp):
                sp.dma_start(arena_w2[:, W2S // 2:W2S], w2_h[:, W2S // 2:W2S]).then_inc(w2b_in, 16)

            @block.scalar
            def _(act):
                act.wait_ge(shifted_s, 1)
                nc.scalar.activation(ex, dl, ACT.Exp).then_inc(exp_done, 1)

            @block.tensor
            def _(pe):
                pe.wait_ge(hot_ready, 1)
                nc.tensor.matmul(bank[0][0:R, 0:NG], c("before", R), one_hot, start=True, stop=True)
                nc.tensor.matmul(bank[1][0:R, 0:NG], c("ones", R), one_hot, start=True, stop=True).then_inc(counted, 1)

            @block.vector
            def _(dve):
                count = [0]

                def link(ins):
                    count[0] += 1
                    ins.then_inc(chain, 1)
                    dve.wait_ge(chain, count[0])

                tt, ts, red = nc.vector.tensor_tensor, nc.vector.tensor_scalar, nc.vector.tensor_reduce
                link(red(m1, by_tile(lgr), AX_X, ALU.max))
                tt(by_tile(dl), by_tile(lgr), m1.unsqueeze(2).broadcast_to([R, NT, NE]), ALU.subtract).then_inc(shifted_s, 1)
                dve.wait_ge(shifted_s, 1)
                link(ts(eq, dl, 0.0, None, ALU.is_equal))
                link(nc.vector.tensor_tensor_scan(cu, c("seg_e", R), eq, 0.0, ALU.mult, ALU.add))
                link(nc.vector.scalar_tensor_tensor(tmp, cu, 1.0, eq, ALU.is_equal, ALU.mult))
                link(ts(valid, c("out_row", R), float(B * TOK), None, ALU.is_le))
                tt(by_tile(one_hot), by_tile(tmp), valid.unsqueeze(2).broadcast_to([R, NT, NE]), ALU.mult).then_inc(hot_ready, 1)
                dve.wait_ge(exp_done, 1)
                link(red(m2, by_tile(ex), AX_X, ALU.add))
                by_row = tokens[0:R, :].rearrange("p (t n) -> p t n", t=NT)
                link(nc.vector.reciprocal(m1, m2))
                nc.vector.tensor_copy(by_row[:, :, 2 * D:2 * D + 1], m1.unsqueeze(2))
                link(nc.vector.tensor_copy(by_row[:, :, 2 * D + 1:RW], c("out_row", R).unsqueeze(2)))
                dve.wait_ge(counted, 1)
                link(nc.vector.tensor_copy(cte.rearrange("p (e t) -> p e t", e=NE),
                                           bank[1][0:R, 0:NG].rearrange("p (t e) -> p e t", e=NE)))
                link(nc.vector.tensor_tensor_scan(inc, c("seg_t", R), cte, 0.0, ALU.mult, ALU.add))
                link(tt(cte, inc, cte, ALU.subtract))
                total = inc.rearrange("p (e t) -> p e t", e=NE)[:, :, NT - 1:NT]
                link(tt(cmp_t.rearrange("p (e k) -> p e k", e=NE), total.broadcast_to([R, NE, MT]),
                        c("starts", R).unsqueeze(1).broadcast_to([R, NE, MT]), ALU.is_gt))
                link(red(tiles_e, cmp_t.rearrange("p (e k) -> p e k", e=NE), AX_X, ALU.add))
                link(nc.vector.tensor_tensor_scan(upto_e, c("ones", R)[:, 0:NE], tiles_e, 0.0, ALU.mult, ALU.add))
                link(tt(off_e, upto_e, tiles_e, ALU.subtract))
                link(ts(off_e, off_e, 128.0, None, ALU.mult))
                link(tt(cte.rearrange("p (e t) -> p e t", e=NE), cte.rearrange("p (e t) -> p e t", e=NE),
                        off_e.unsqueeze(2).broadcast_to([R, NE, NT]), ALU.add))
                link(tt(by_tile(tmp), by_tile(bank[0][0:R, 0:NG]), cte.rearrange("p (e t) -> p t e", e=NE), ALU.add))
                link(tt(tmp, tmp, one_hot, ALU.mult))
                link(red(m1, by_tile(tmp), AX_X, ALU.add))
                nc.vector.tensor_copy(slot_i[0:R, :], m1).then_inc(slots_ready, 1)
                link(tt(past.rearrange("p (s e) -> p s e", s=ST), upto_e.unsqueeze(1).broadcast_to([R, ST, NE]),
                        c("tile_no", R).unsqueeze(2).broadcast_to([R, ST, NE]), ALU.is_le))
                link(red(eno, past.rearrange("p (s e) -> p s e", s=ST), AX_X, ALU.add))
                link(ts(eno, eno, float(NE - 1), None, ALU.min))
                link(nc.vector.tensor_copy(expert_i[0:1, :], eno[0:1, :]))

            @block.gpsimd
            def _(pool):
                pool.wait_ge(slots_ready, 1)
                for t in range(NT):
                    rows = min(R, (B - t * IPT) * TOK)
                    pool.indirect_dma_start(x_slots, bass.IndirectOffsetOnAxis(ap=slot_i[0:rows, t:t + 1], axis=0),
                                            tokens[0:rows, t * RW:(t + 1) * RW], None).then_inc(x_sent, 16)
                pool.wait_ge(x_sent, 16 * NT)

        with phase():
            (x_in, rest_in, biased, row_ready, x_turned, xt_ready, h_done, h_out, h_act, y_done, y_out, y_stored) = (
                pair(n) for n in ("x_in", "rest_in", "biased", "row_ready", "x_turned", "xt_ready", "h_done", "h_out",
                                  "h_act", "y_done", "y_out", "y_stored"))
            h_turned = [pair(f"h_turned{f}_") for f in range(2)]
            SP = ST // 2
            wc = carver(work)
            xg = [tokens[:, j * D:(j + 1) * D] for j in range(2)]
            rest = [tokens[:, (2 + j) * RW:(2 + j) * RW + D + 2] for j in range(2)]
            yb = [tokens[:, (4 + j) * RW:(4 + j) * RW + D] for j in range(2)]
            xgt = [wc(D) for _ in range(2)]
            hp = [wc(FF) for _ in range(2)]
            ht = [wc(FF) for _ in range(2)]
            yo = [wc(D) for _ in range(2)]
            block = enter(nc.Block())

            def expert_of(eng, pair_at, j):
                if pair_at is None:
                    return None
                return eng.value_load(expert_i[0:1, bass.ds(2 * pair_at[0] + j, 1)], min_val=0, max_val=NE - 1)

            @block.sync
            def _(sp):
                def turn(i):
                    for j in range(2):
                        wait_free(sp, x_turned[j], i)
                        sp.dma_start(xg[j], x_slots[bass.ds((2 * i + j) * 128, 128), D:2 * D]).then_inc(x_in[j], 16)

                run_turns(sp, turn, total=SP)

            @block.gpsimd
            def _(pool):

                def load_rest(pair_at, j):
                    if pair_at is None:
                        return
                    i, n1 = pair_at
                    slots = bass.ds((2 * i + j) * 128, 128)
                    wait_free(pool, y_out[j], i)
                    pool.dma_start(rest[j][:, 0:D], x_slots[slots, 0:D]).then_inc(rest_in[j], 16)
                    sent = i - 1 + j
                    if not isinstance(sent, int) or sent > 0:
                        pool.wait_ge(y_stored[1 - j], 16 * sent)
                    pool.dma_start(rest[j][:, D:D + 2], x_slots[slots, 2 * D:RW]).then_inc(rest_in[j], 16)

                def send_outputs(i, n1, j):
                    if isinstance(i, int):
                        other_slot_free(pool, y_stored, (i, n1), j, 16)
                    stand_alone(pool)
                    pool.wait_ge(y_out[j], n1)
                    pool.wait_ge(row_ready[j], n1)
                    pool.indirect_dma_start(out_h, bass.IndirectOffsetOnAxis(ap=out_row[:, j:j + 1], axis=0),
                                            yo[j], None).then_inc(y_stored[j], 16)

                def turn(i):
                    following = at(pool, i, 1, SP)
                    n1 = following[0] if following else i + 1
                    for j in range(2):
                        load_rest(following, j)
                        if not isinstance(i, int) or i >= 0:
                            send_outputs(i, n1, j)

                run_turns(pool, turn, ahead=1, total=SP)
                for j in range(2):
                    pool.wait_ge(y_stored[j], 16 * SP)

            @block.tensor
            def _(pe):
                pe.wait_ge(w1_in, 16)
                pe.wait_ge(w2a_in, 16)
                pe.wait_ge(w2b_in, 16)

                def turn_tokens(pair_at, j):
                    if pair_at is None:
                        return
                    i, n1 = pair_at
                    pe.wait_ge(x_in[j], 16 * n1)
                    other_slot_free(pe, xt_ready, pair_at, j)
                    for k in range(2):
                        mm = nc.tensor.transpose(bank[6][:, k * 128:(k + 1) * 128], xg[j][:, k * 128:(k + 1) * 128], ident)
                    mm.then_inc(x_turned[j], 1)

                def hidden(pair_at, j, expert):
                    if pair_at is None:
                        return
                    i, n1 = pair_at
                    pe.wait_ge(xt_ready[j], n1)
                    wait_free(pe, h_out[j], i * 2)
                    for f in range(2):
                        for k in range(2):
                            mm = nc.tensor.matmul(bank[2 * j + f][:, :], xgt[j][:, k * 128:(k + 1) * 128],
                                                  arena_w1[:, bass.ds(expert * (2 * FF) + (k * FF + f * 512), 512)],
                                                  start=(k == 0), stop=(k == 1))
                        mm.then_inc(h_done[j], 1)

                def turn_hidden(pair_at, j):
                    if pair_at is None:
                        return
                    i, n1 = pair_at
                    other_slot_free(pe, h_act, pair_at, j, FC)
                    for f in range(2):
                        pe.wait_ge(h_out[j], i * 2 + f + 1)
                        for k in range(4):
                            mm = nc.tensor.transpose(bank[4 + f][:, k * 128:(k + 1) * 128],
                                                     hp[j][:, (4 * f + k) * 128:(4 * f + k + 1) * 128], ident)
                        mm.then_inc(h_turned[f][j], 1)

                def outputs(pair_at, j, expert):
                    if pair_at is None:
                        return
                    i, n1 = pair_at
                    other_slot_free(pe, biased, pair_at, j)
                    for g in range(FC):
                        pe.wait_ge(h_act[j], i * FC + g + 1)
                        mm = nc.tensor.matmul(bank[7][:, 0:D], ht[j][:, g * 128:(g + 1) * 128],
                                              arena_w2[:, bass.ds(expert * (FC * D) + g * D, D)],
                                              start=(g == 0), stop=(g == FC - 1))
                    mm.then_inc(y_done[j], 1)

                def turn(i):
                    last, this, following = at(pe, i, -1, SP), at(pe, i, 0, SP), at(pe, i, 1, SP)
                    last_expert = expert_of(pe, last, 1)
                    experts = [expert_of(pe, this, j) for j in range(2)]
                    hidden(this, 0, experts[0])
                    turn_tokens(this, 1)
                    outputs(last, 1, last_expert)
                    turn_hidden(this, 0)
                    hidden(this, 1, experts[1])
                    turn_tokens(following, 0)
                    outputs(this, 0, experts[0])
                    turn_hidden(this, 1)

                run_turns(pe, turn, ahead=1, behind=1, total=SP)

            @block.vector
            def _(dve):
                def copy_tokens(pair_at, j):
                    if pair_at is None:
                        return
                    i, n1 = pair_at
                    dve.wait_ge(x_turned[j], n1)
                    wait_free(dve, h_done[j], i * 2)
                    nc.vector.tensor_copy(xgt[j], bank[6][:, 0:D]).then_inc(xt_ready[j], 1)

                def copy_hidden(pair_at, j):
                    if pair_at is None:
                        return
                    i, n1 = pair_at
                    for f in range(2):
                        dve.wait_ge(h_done[j], i * 2 + f + 1)
                        wait_free(dve, h_turned[f][j], i)
                        nc.vector.tensor_copy(hp[j][:, f * 512:(f + 1) * 512], bank[2 * j + f][:, :]).then_inc(h_out[j], 1)

                def add_bias(pair_at, j, expert):
                    if pair_at is None:
                        return
                    i, n1 = pair_at
                    dve.wait_ge(y_done[j], n1)
                    nc.vector.tensor_tensor(yb[j], bank[7][:, 0:D],
                                            cst[:, bass.ds(expert * D + atc["b2"][0], D)], ALU.add).then_inc(biased[j], 1)
                    dve.wait_ge(biased[j], n1)
                    dve.wait_ge(rest_in[j], 32 * n1)
                    wait_free(dve, y_stored[j], 16 * i)
                    nc.vector.tensor_copy(out_row[:, j:j + 1], rest[j][:, D + 1:D + 2]).then_inc(row_ready[j], 1)
                    nc.vector.scalar_tensor_tensor(yo[j], yb[j], rest[j][:, D:D + 1], rest[j][:, 0:D],
                                                   ALU.mult, ALU.add).then_inc(y_out[j], 1)

                def turn(i):
                    last, this, following = at(dve, i, -1, SP), at(dve, i, 0, SP), at(dve, i, 1, SP)
                    last_expert, expert = expert_of(dve, last, 1), expert_of(dve, this, 0)
                    copy_hidden(this, 0)
                    copy_tokens(this, 1)
                    add_bias(last, 1, last_expert)
                    copy_hidden(this, 1)
                    copy_tokens(following, 0)
                    add_bias(this, 0, expert)

                run_turns(dve, turn, ahead=1, behind=1, total=SP)

            @block.scalar
            def _(act):
                def activate(pair_at, j, expert):
                    i, n1 = pair_at
                    wait_free(act, y_done[j], i)
                    for f in range(2):
                        act.wait_ge(h_turned[f][j], n1)
                        for k in range(4):
                            g = 4 * f + k
                            nc.scalar.activation(ht[j][:, g * 128:(g + 1) * 128], bank[4 + f][:, k * 128:(k + 1) * 128],
                                                 ACT.Gelu, bias=cst[:, bass.ds(expert * FC + (atc["b1"][0] + g), 1)]
                                                 ).then_inc(h_act[j], 1)

                def turn(i):
                    this = at(act, i, 0, SP)
                    for j in range(2):
                        activate(this, j, expert_of(act, this, j))

                run_turns(act, turn, total=SP)


def lay_out(inp):
    import numpy as np

    f = {k: np.asarray(v) for k, v in inp.items()}

    def chunks(w, c):
        return w.reshape(c, 128, -1).transpose(1, 0, 2).reshape(128, -1)

    def rows(v, n=R):
        return np.broadcast_to(np.asarray(v).reshape(1, -1), (n, v.size))

    patches = f["x"].reshape(B, 3, 6, 16, 6, 16).transpose(0, 2, 4, 1, 3, 5).reshape(B, TOK - 1, FP)
    padded = np.zeros((NT * IPT, TOK, FP), np.float32)
    padded[:B, 1:] = patches
    x_h = np.ascontiguousarray(padded.reshape(NT, IPT, TOK, PC, 128).transpose(0, 4, 3, 1, 2).reshape(NT, 128, -1))

    p = {}
    p["w_lin"] = chunks(f["L0_tok_W_lin"].T, PC)
    p["pos"] = np.tile(f["L0_tok_position_embeddings"][0], (IPT, 1))
    add = np.concatenate([f["L0_tok_class_token"][0], rows(f["L0_tok_b_lin"], TOK - 1)], 0)
    p["pos_add"] = np.tile(add, (IPT, 1))
    p["w_q"] = chunks(f["L0_attn_Wq"].T, 2)
    p["b_q"] = rows(f["L0_attn_bq"])
    kv, bkv = f["L0_attn_Wkv"], f["L0_attn_bkv"]
    p["w_k"] = chunks(np.tile(kv[:HD].T, (1, 2)), 2)
    p["b_k"] = np.tile(bkv[:HD], 2 * IPT)[:, None]
    p["w_v"] = chunks(kv[HD:].T, 2)
    p["b_v"] = rows(bkv[HD:])
    p["w_o"] = chunks(f["L0_attn_Wo"].T, 2)
    p["b_o"] = rows(f["L0_attn_bo"])
    p["proj"] = chunks(f["L0_ffn_proj"], 2)
    p["w_in1"] = chunks(f["L0_ffn_Win1"][:D], 2)
    p["b_in1"] = f["L0_ffn_Win1"][D][:, None]
    p["c1"], p["c2"] = f["L0_ffn_C1"], f["L0_ffn_C2"]
    p["w_out1"] = f["L0_ffn_Wout1"].T
    p["w_in2"] = chunks(f["L0_ffn_Win2"][:O0], OC)
    p["b_in2"] = f["L0_ffn_Win2"][O0][:, None]
    p["w_out2"] = f["L0_ffn_Wout2"].T
    p["w_vb"] = chunks(np.concatenate([f["L1_attn_W_write"].T, f["L1_attn_W_beta"].T], 1), 2)
    p["decay"] = rows(f["L1_attn_decay"])
    p["w_read"] = chunks(f["L1_attn_W_read"].T, 2)
    p["w_r"] = chunks(f["L1_ffn_Wr"], 2)
    p["b_r"] = rows(f["L1_ffn_br"])
    p["b1"] = f["L1_ffn_b1"].reshape(NE, FC, 128).transpose(2, 0, 1).reshape(128, -1)
    p["b2"] = rows(f["L1_ffn_b2"], 128)

    r = np.arange(R)
    img, pos = r // TOK, r % TOK
    same = img[:, None] == img[None, :]
    lag = (pos[:, None] - pos[None, :]).astype(np.float32)
    p["mask_head"] = np.arange(128)[:, None] // HD % 2 == np.arange(2)
    p["mask_pair"] = np.arange(128)[:, None] // HP == np.arange(2)
    p["lag"] = np.where(same & (lag > 0), lag, 0)
    p["keep"] = -1.0 * (same & (lag > 0))
    p["lag_t"] = np.where(same.T & (lag.T >= 0), lag.T, 0)
    p["keep_t"] = same.T & (lag.T >= 0)
    k = np.tile(np.arange(1, E0 + 1, dtype=np.float32), NT)
    p["inv_k"], p["rank_k"], p["seg_e0"] = rows(1 / k), rows(k), rows(np.float32(k > 1))
    p["ident"] = np.eye(128)
    p["mask_img"] = img[:, None] == np.arange(IPT)
    p["before"] = r[:, None] < r[None, :]
    p["ones"] = np.ones((R, R))
    p["out_row"] = np.arange(NT)[None, :] * R + r[:, None] + 1
    p["seg_e"] = rows(np.float32(np.arange(NT * NE) % NE > 0))
    p["seg_t"] = rows(np.float32(np.arange(NT * NE) % NT > 0))
    p["starts"] = rows(128.0 * np.arange(MT))
    p["tile_no"] = rows(1.0 * np.arange(ST))

    def packed(pack, start=0):
        at, n = offsets(pack, start)
        out = np.zeros((128, n), np.float32)
        for name, (a, w) in at.items():
            out[:p[name].shape[0], a:a + w] = p[name]
        return out

    w1 = f["L1_ffn_W1"].reshape(NE, 2, 128, FF).transpose(2, 0, 1, 3).reshape(128, -1)
    w2 = f["L1_ffn_W2"].reshape(NE, FC, 128, D).transpose(2, 0, 1, 3).reshape(128, -1)
    return {"in_x": x_h, "in_pack1": packed(PACK1), "in_pack2": packed(PACK2), "in_packc": packed(PACKC, 128),
            "in_w1": np.ascontiguousarray(w1), "in_w2": np.ascontiguousarray(w2)}


def kernel(**inputs):
    import concourse.bacc as _bacc
    from concourse import mybir as _mybir
    from concourse.bass_utils import run_bass_kernel_spmd as _run

    nc = _bacc.Bacc("TRN2", target_bir_lowering=False, num_devices=1)
    arrays = lay_out(inputs)
    args = [nc.dram_tensor(n, a.shape, _mybir.dt.from_np(a.dtype), kind="ExternalInput").ap() for n, a in arrays.items()]
    args.append(nc.dram_tensor("out_0", (1 + B * TOK, D), F32, kind="ExternalOutput").ap())
    build(nc, *args)
    r = _run(nc, [arrays], core_ids=[0])
    return r.results[0]["out_0"][1:].reshape(B, TOK, D)
```
